# Optimizing a Trainium2 kernel written in Bass

```python
import numpy as np
import jax
import jax.numpy as jnp

def _softmax(x, axis=-1):
    return jax.nn.softmax(x, axis=axis)

def _gelu(x):
    return jax.nn.gelu(x, approximate=True)

def _silu(x):
    return jax.nn.silu(x)

def _sigmoid(x):
    return jax.nn.sigmoid(x)

def _layernorm(x, axis=-1, eps=1e-05):
    m = jnp.mean(x, axis=axis, keepdims=True)
    v = jnp.var(x, axis=axis, keepdims=True)
    return (x - m) / jnp.sqrt(v + eps)

def _scatter_add(tgt, idx, src, axis=0):
    return tgt.at[idx].add(src)

def _segment_sum(src, seg, n):
    return jax.ops.segment_sum(src, seg, n)
kernel_name = 'mk_lm_tower_d2_tok_ids256_r4_f3cadc'

def setup_inputs(seed: int=0):
    np.random.seed(seed)
    _w = jnp.asarray

    def _rec_inputs():
        import jax
        import jax.numpy as jnp
        _rk = jax.random.key(seed)
        x = jax.random.randint(jax.random.fold_in(_rk, 1), (32, 512), 0, 100001, jnp.int32)
        return x
    x = _rec_inputs()

    def _L0_tok_setup():
        import jax, jax.numpy as jnp
        import numpy as np
        NUM_ITEMS = 25000
        D = 64
        FOURIER_DIM = 64
        VISIT_DIM = 24
        RESIDUAL_SCALE = 0.1
        LN_EPS = 1e-05

        def _layer_norm(x, gamma, beta):
            mu = jnp.mean(x, axis=-1, keepdims=True)
            var = jnp.mean(jnp.square(x - mu), axis=-1, keepdims=True)
            return (x - mu) * jax.lax.rsqrt(var + LN_EPS) * gamma + beta
        key = jax.random.key(seed)
        ks = jax.random.split(key, 12)
        item_ids = jax.random.randint(ks[0], (128, 512), 0, NUM_ITEMS + 1)
        emb_table = 0.02 * jax.random.normal(ks[1], (NUM_ITEMS + 1, D), dtype=jnp.float32)
        emb_table = emb_table.at[0].set(0.0)
        geo_table = jax.random.normal(ks[2], (NUM_ITEMS + 1, FOURIER_DIM), dtype=jnp.float32)
        visit_table = jax.random.uniform(ks[3], (NUM_ITEMS + 1, VISIT_DIM), dtype=jnp.float32)

        def xavier(k, fan_in, fan_out):
            lim = np.sqrt(6.0 / (fan_in + fan_out))
            return jax.random.uniform(k, (fan_in, fan_out), jnp.float32, -lim, lim)
        w_item = xavier(ks[4], D, D)
        b_item = jnp.zeros((D,), jnp.float32)
        w_geo = xavier(ks[5], FOURIER_DIM, D)
        b_geo = jnp.zeros((D,), jnp.float32)
        w_visit = xavier(ks[6], VISIT_DIM, D)
        b_visit = jnp.zeros((D,), jnp.float32)
        w_fuse = xavier(ks[7], 3 * D, D)
        b_fuse = jnp.zeros((D,), jnp.float32)
        ln_gamma = jnp.ones((D,), jnp.float32)
        ln_beta = jnp.zeros((D,), jnp.float32)
        return dict(item_ids=item_ids, emb_table=emb_table, geo_table=geo_table, visit_table=visit_table, w_item=w_item, b_item=b_item, w_geo=w_geo, b_geo=b_geo, w_visit=w_visit, b_visit=b_visit, w_fuse=w_fuse, b_fuse=b_fuse, ln_gamma=ln_gamma, ln_beta=ln_beta)
    _L0_tok_all = _L0_tok_setup()
    _L0_tok_in = {k: v for k, v in _L0_tok_all.items() if k in ('emb_table', 'geo_table', 'visit_table', 'w_item', 'b_item', 'w_geo', 'b_geo', 'w_visit', 'b_visit', 'w_fuse', 'b_fuse', 'ln_gamma', 'ln_beta')}
    del _L0_tok_all

    def _L0_attn_setup():
        import jax, jax.numpy as jnp
        import numpy as np
        B0, L0, C0 = (4, 144, 64)
        DST, DCONV, EXP = (48, 4, 2)
        DIN = EXP * C0
        DTR = C0 // 16
        FD = 2 * C0

        def _ln(x, g, b, eps=0.001):
            m = jnp.mean(x, -1, keepdims=True)
            v = jnp.mean((x - m) ** 2, -1, keepdims=True)
            return (x - m) / jnp.sqrt(v + eps) * g + b

        def _selective_scan(u, delta, A, Bm, Cm, D):
            dA = jnp.einsum('bld,dn->bldn', delta, A)
            dB_u = jnp.einsum('bld,bld,bln->bldn', delta, u, Bm)
            shifted = jnp.pad(dA[:, 1:], ((0, 0), (1, 1), (0, 0), (0, 0)))[:, 1:]
            dA_cumsum = jnp.exp(jnp.cumsum(shifted[:, ::-1], axis=1))[:, ::-1]
            xs = jnp.cumsum(dB_u * dA_cumsum, axis=1) / (dA_cumsum + 1e-12)
            y = jnp.einsum('bldn,bln->bld', xs, Cm)
            return y + u * D

        def _forward(x, ln1_g, ln1_b, mln_g, mln_b, w_in, conv_w, conv_b, w_xproj, w_dt, b_dt, A_log, D, w_out, ln2_g, ln2_b, fc1_w, bn1_s, bn1_b, Wr, Wi, rb, ib, fc2_w, bn2_s, bn2_b):
            h = _ln(_ln(x, ln1_g, ln1_b), mln_g, mln_b)
            xr = h @ w_in
            xm, res = (xr[..., :DIN], xr[..., DIN:])
            xp = jnp.pad(xm, ((0, 0), (DCONV - 1, 0), (0, 0)))
            xc = jax.lax.conv_general_dilated(xp, conv_w[:, None, :], (1,), 'VALID', dimension_numbers=('NLC', 'LIO', 'NLC'), feature_group_count=DIN) + conv_b
            xc = jax.nn.silu(xc)
            A = -jnp.exp(A_log)
            x_dbl = xc @ w_xproj
            dt, Bm, Cm = (x_dbl[..., :DTR], x_dbl[..., DTR:DTR + DST], x_dbl[..., DTR + DST:])
            delta = jax.nn.softplus(dt @ w_dt + b_dt)
            y = _selective_scan(xc, delta, A, Bm, Cm, D)
            y = y * jax.nn.silu(res)
            x = x + y @ w_out
            h2 = _ln(x, ln2_g, ln2_b)
            f = jax.nn.relu(h2 @ fc1_w * bn1_s + bn1_b)
            L = f.shape[1]
            scale = L ** 0.5
            fr = jnp.fft.rfft(f, axis=1)
            real, imag = (fr.real / scale, fr.imag / scale)
            xre = jax.nn.relu(jnp.einsum('bnc,cd->bnd', real, Wr) - jnp.einsum('bnc,cd->bnd', imag, Wi) + rb)
            xim = jax.nn.relu(jnp.einsum('bnc,cd->bnd', imag, Wr) + jnp.einsum('bnc,cd->bnd', real, Wi) + ib)
            ff = jnp.fft.irfft((xre + 1j * xim) * scale, n=L, axis=1)
            out2 = ff @ fc2_w * bn2_s + bn2_b
            return x + out2
        key = jax.random.key(seed)
        ks = iter(jax.random.split(key, 32))

        def n(shape, s=0.02):
            return jax.random.normal(next(ks), shape, dtype=jnp.float32) * s
        return {'x': jax.random.normal(next(ks), (B0, L0, C0), dtype=jnp.float32), 'ln1_g': jnp.ones((C0,), jnp.float32), 'ln1_b': jnp.zeros((C0,), jnp.float32), 'mln_g': jnp.ones((C0,), jnp.float32), 'mln_b': jnp.zeros((C0,), jnp.float32), 'w_in': n((C0, DIN * EXP)), 'conv_w': n((DCONV, DIN)), 'conv_b': jnp.zeros((DIN,), jnp.float32), 'w_xproj': n((DIN, DTR + 2 * DST)), 'w_dt': n((DTR, DIN)), 'b_dt': jnp.zeros((DIN,), jnp.float32), 'A_log': jnp.log(jnp.tile(jnp.arange(1, DST + 1, dtype=jnp.float32), (DIN, 1))), 'D': jnp.ones((DIN,), jnp.float32), 'w_out': n((DIN, C0)), 'ln2_g': jnp.ones((C0,), jnp.float32), 'ln2_b': jnp.zeros((C0,), jnp.float32), 'fc1_w': n((C0, FD)), 'bn1_s': jnp.ones((FD,), jnp.float32), 'bn1_b': jnp.zeros((FD,), jnp.float32), 'Wr': n((FD, FD)), 'Wi': n((FD, FD)), 'rb': n((FD,)), 'ib': n((FD,)), 'fc2_w': n((FD, C0)), 'bn2_s': jnp.ones((C0,), jnp.float32), 'bn2_b': jnp.zeros((C0,), jnp.float32)}
    _L0_attn_all = _L0_attn_setup()
    _L0_attn_in = {k: v for k, v in _L0_attn_all.items() if k in ('ln1_g', 'ln1_b', 'mln_g', 'mln_b', 'w_in', 'conv_w', 'conv_b', 'w_xproj', 'w_dt', 'b_dt', 'A_log', 'D', 'w_out', 'ln2_g', 'ln2_b', 'fc1_w', 'bn1_s', 'bn1_b', 'Wr', 'Wi', 'rb', 'ib', 'fc2_w', 'bn2_s', 'bn2_b')}
    del _L0_attn_all

    def _L0_ffn_setup():
        import jax, jax.numpy as jnp
        import numpy as np
        B, A = (1024, 8)
        IN, OUT = (64, 64)
        SH1, SH2 = (64, 128)
        EH1, EH2 = (128, 64)
        E, TOPK = (4, 2)

        def _shared_mlp(x, W1, b1, W2, b2, W3, b3):
            h = jax.nn.relu(x @ W1 + b1)
            h = jax.nn.relu(h @ W2 + b2)
            return h @ W3 + b3

        def _experts_mlp(x, eW1, eb1, eW2, eb2, eW3, eb3):
            h = jax.nn.relu(jnp.einsum('baf,efh->ebah', x, eW1) + eb1[:, None, None, :])
            h = jax.nn.relu(jnp.einsum('ebah,ehg->ebag', h, eW2) + eb2[:, None, None, :])
            o = jnp.einsum('ebag,ego->ebao', h, eW3) + eb3[:, None, None, :]
            return jnp.moveaxis(o, 0, -1)
        key = jax.random.key(seed)
        ks = jax.random.split(key, 16)
        s = 0.05
        return {'x': jax.random.normal(ks[0], (B, A, IN), jnp.float32), 'sW1': jax.random.normal(ks[1], (IN, SH1), jnp.float32) * s, 'sb1': jnp.zeros((SH1,), jnp.float32), 'sW2': jax.random.normal(ks[2], (SH1, SH2), jnp.float32) * s, 'sb2': jnp.zeros((SH2,), jnp.float32), 'sW3': jax.random.normal(ks[3], (SH2, OUT), jnp.float32) * s, 'sb3': jnp.zeros((OUT,), jnp.float32), 'eW1': jax.random.normal(ks[4], (E, IN, EH1), jnp.float32) * s, 'eb1': jnp.zeros((E, EH1), jnp.float32), 'eW2': jax.random.normal(ks[5], (E, EH1, EH2), jnp.float32) * s, 'eb2': jnp.zeros((E, EH2), jnp.float32), 'eW3': jax.random.normal(ks[6], (E, EH2, OUT), jnp.float32) * s, 'eb3': jnp.zeros((E, OUT), jnp.float32), 'gW': jax.random.normal(ks[7], (IN, E), jnp.float32) * s, 'gb': jnp.zeros((E,), jnp.float32)}
    _L0_ffn_all = _L0_ffn_setup()
    _L0_ffn_in = {k: v for k, v in _L0_ffn_all.items() if k in ('sW1', 'sb1', 'sW2', 'sb2', 'sW3', 'sb3', 'eW1', 'eb1', 'eW2', 'eb2', 'eW3', 'eb3', 'gW', 'gb')}
    del _L0_ffn_all

    def _L1_attn_setup():
        import jax, jax.numpy as jnp
        import numpy as np
        H = 8
        key = jax.random.key(seed)
        ks = jax.random.split(key, 10)
        B, N, D, E = (1, 1024, 64, 16384)
        s = 0.02
        return {'x': jax.random.normal(ks[0], (B, N, D), jnp.float32), 'edge_index': jax.random.randint(ks[1], (2, E), 0, N, jnp.int32), 'edge_attr': jax.random.normal(ks[2], (E, 3), jnp.float32), 'Wq': jax.random.normal(ks[3], (D, D), jnp.float32) * s, 'bq': jnp.zeros((D,), jnp.float32), 'Wk': jax.random.normal(ks[4], (D, D), jnp.float32) * s, 'bk': jnp.zeros((D,), jnp.float32), 'Wv': jax.random.normal(ks[5], (D, D), jnp.float32) * s, 'bv': jnp.zeros((D,), jnp.float32), 'Wo': jax.random.normal(ks[6], (D, D), jnp.float32) * s, 'bo': jnp.zeros((D,), jnp.float32), 'We': jax.random.normal(ks[7], (3, H), jnp.float32) * s, 'be': jnp.zeros((H,), jnp.float32)}
    _L1_attn_all = _L1_attn_setup()
    _L1_attn_in = {k: v for k, v in _L1_attn_all.items() if k in ('edge_index', 'edge_attr', 'Wq', 'bq', 'Wk', 'bk', 'Wv', 'bv', 'Wo', 'bo', 'We', 'be')}
    del _L1_attn_all

    def _L1_ffn_setup():
        import jax, jax.numpy as jnp
        import numpy as np
        NUM_EXPERTS = 8
        TOP_K = 2
        B, S, D = (8, 2048, 64)

        def _moe(tokens, router_w, w1, b1, w2, b2):
            N = tokens.shape[0]
            E = router_w.shape[0]
            logits = tokens.astype(jnp.float32) @ router_w.astype(jnp.float32).T
            probs = jax.nn.softmax(logits, axis=-1)
            rw, re = jax.lax.top_k(probs, TOP_K)
            if TOP_K > 1:
                rw = rw / jnp.maximum(rw.sum(-1, keepdims=True), 1e-12)
            rw = rw.astype(tokens.dtype)
            combine = jnp.zeros((N, E), tokens.dtype).at[jnp.arange(N)[:, None], re].set(rw)
            out = tokens
            for e in range(E):
                h = jax.nn.gelu(tokens @ w1[e] + b1[e], approximate=False)
                y = h @ w2[e] + b2[e]
                out = out + combine[:, e:e + 1] * y
            return out
        key = jax.random.key(seed)
        ks = jax.random.split(key, 4)
        scale = 1.0 / np.sqrt(D).astype(np.float32)
        return {'input_embeddings': jax.random.normal(ks[0], (B, S, D), jnp.float32), 'router_w': jax.random.normal(ks[1], (NUM_EXPERTS, D), jnp.float32) * scale, 'w1': jax.random.normal(ks[2], (NUM_EXPERTS, D, D), jnp.float32) * scale, 'b1': jnp.zeros((NUM_EXPERTS, D), jnp.float32), 'w2': jax.random.normal(ks[3], (NUM_EXPERTS, D, D), jnp.float32) * scale, 'b2': jnp.zeros((NUM_EXPERTS, D), jnp.float32)}
    _L1_ffn_all = _L1_ffn_setup()
    _L1_ffn_in = {k: v for k, v in _L1_ffn_all.items() if k in ('router_w', 'w1', 'b1', 'w2', 'b2')}
    del _L1_ffn_all
    return {'x': x, 'L0_tok_emb_table': _L0_tok_in['emb_table'], 'L0_tok_geo_table': _L0_tok_in['geo_table'], 'L0_tok_visit_table': _L0_tok_in['visit_table'], 'L0_tok_w_item': _L0_tok_in['w_item'], 'L0_tok_b_item': _L0_tok_in['b_item'], 'L0_tok_w_geo': _L0_tok_in['w_geo'], 'L0_tok_b_geo': _L0_tok_in['b_geo'], 'L0_tok_w_visit': _L0_tok_in['w_visit'], 'L0_tok_b_visit': _L0_tok_in['b_visit'], 'L0_tok_w_fuse': _L0_tok_in['w_fuse'], 'L0_tok_b_fuse': _L0_tok_in['b_fuse'], 'L0_tok_ln_gamma': _L0_tok_in['ln_gamma'], 'L0_tok_ln_beta': _L0_tok_in['ln_beta'], 'L0_attn_ln1_g': _L0_attn_in['ln1_g'], 'L0_attn_ln1_b': _L0_attn_in['ln1_b'], 'L0_attn_mln_g': _L0_attn_in['mln_g'], 'L0_attn_mln_b': _L0_attn_in['mln_b'], 'L0_attn_w_in': _L0_attn_in['w_in'], 'L0_attn_conv_w': _L0_attn_in['conv_w'], 'L0_attn_conv_b': _L0_attn_in['conv_b'], 'L0_attn_w_xproj': _L0_attn_in['w_xproj'], 'L0_attn_w_dt': _L0_attn_in['w_dt'], 'L0_attn_b_dt': _L0_attn_in['b_dt'], 'L0_attn_A_log': _L0_attn_in['A_log'], 'L0_attn_D': _L0_attn_in['D'], 'L0_attn_w_out': _L0_attn_in['w_out'], 'L0_attn_ln2_g': _L0_attn_in['ln2_g'], 'L0_attn_ln2_b': _L0_attn_in['ln2_b'], 'L0_attn_fc1_w': _L0_attn_in['fc1_w'], 'L0_attn_bn1_s': _L0_attn_in['bn1_s'], 'L0_attn_bn1_b': _L0_attn_in['bn1_b'], 'L0_attn_Wr': _L0_attn_in['Wr'], 'L0_attn_Wi': _L0_attn_in['Wi'], 'L0_attn_rb': _L0_attn_in['rb'], 'L0_attn_ib': _L0_attn_in['ib'], 'L0_attn_fc2_w': _L0_attn_in['fc2_w'], 'L0_attn_bn2_s': _L0_attn_in['bn2_s'], 'L0_attn_bn2_b': _L0_attn_in['bn2_b'], 'L0_ffn_sW1': _L0_ffn_in['sW1'], 'L0_ffn_sb1': _L0_ffn_in['sb1'], 'L0_ffn_sW2': _L0_ffn_in['sW2'], 'L0_ffn_sb2': _L0_ffn_in['sb2'], 'L0_ffn_sW3': _L0_ffn_in['sW3'], 'L0_ffn_sb3': _L0_ffn_in['sb3'], 'L0_ffn_eW1': _L0_ffn_in['eW1'], 'L0_ffn_eb1': _L0_ffn_in['eb1'], 'L0_ffn_eW2': _L0_ffn_in['eW2'], 'L0_ffn_eb2': _L0_ffn_in['eb2'], 'L0_ffn_eW3': _L0_ffn_in['eW3'], 'L0_ffn_eb3': _L0_ffn_in['eb3'], 'L0_ffn_gW': _L0_ffn_in['gW'], 'L0_ffn_gb': _L0_ffn_in['gb'], 'L1_attn_edge_index': _L1_attn_in['edge_index'], 'L1_attn_edge_attr': _L1_attn_in['edge_attr'], 'L1_attn_Wq': _L1_attn_in['Wq'], 'L1_attn_bq': _L1_attn_in['bq'], 'L1_attn_Wk': _L1_attn_in['Wk'], 'L1_attn_bk': _L1_attn_in['bk'], 'L1_attn_Wv': _L1_attn_in['Wv'], 'L1_attn_bv': _L1_attn_in['bv'], 'L1_attn_Wo': _L1_attn_in['Wo'], 'L1_attn_bo': _L1_attn_in['bo'], 'L1_attn_We': _L1_attn_in['We'], 'L1_attn_be': _L1_attn_in['be'], 'L1_ffn_router_w': _L1_ffn_in['router_w'], 'L1_ffn_w1': _L1_ffn_in['w1'], 'L1_ffn_b1': _L1_ffn_in['b1'], 'L1_ffn_w2': _L1_ffn_in['w2'], 'L1_ffn_b2': _L1_ffn_in['b2']}

def reference(x, L0_tok_emb_table, L0_tok_geo_table, L0_tok_visit_table, L0_tok_w_item, L0_tok_b_item, L0_tok_w_geo, L0_tok_b_geo, L0_tok_w_visit, L0_tok_b_visit, L0_tok_w_fuse, L0_tok_b_fuse, L0_tok_ln_gamma, L0_tok_ln_beta, L0_attn_ln1_g, L0_attn_ln1_b, L0_attn_mln_g, L0_attn_mln_b, L0_attn_w_in, L0_attn_conv_w, L0_attn_conv_b, L0_attn_w_xproj, L0_attn_w_dt, L0_attn_b_dt, L0_attn_A_log, L0_attn_D, L0_attn_w_out, L0_attn_ln2_g, L0_attn_ln2_b, L0_attn_fc1_w, L0_attn_bn1_s, L0_attn_bn1_b, L0_attn_Wr, L0_attn_Wi, L0_attn_rb, L0_attn_ib, L0_attn_fc2_w, L0_attn_bn2_s, L0_attn_bn2_b, L0_ffn_sW1, L0_ffn_sb1, L0_ffn_sW2, L0_ffn_sb2, L0_ffn_sW3, L0_ffn_sb3, L0_ffn_eW1, L0_ffn_eb1, L0_ffn_eW2, L0_ffn_eb2, L0_ffn_eW3, L0_ffn_eb3, L0_ffn_gW, L0_ffn_gb, L1_attn_edge_index, L1_attn_edge_attr, L1_attn_Wq, L1_attn_bq, L1_attn_Wk, L1_attn_bk, L1_attn_Wv, L1_attn_bv, L1_attn_Wo, L1_attn_bo, L1_attn_We, L1_attn_be, L1_ffn_router_w, L1_ffn_w1, L1_ffn_b1, L1_ffn_w2, L1_ffn_b2):
    import jax
    import jax.numpy as jnp

    def _L0_tok_ref(item_ids, emb_table, geo_table, visit_table, w_item, b_item, w_geo, b_geo, w_visit, b_visit, w_fuse, b_fuse, ln_gamma, ln_beta):
        import jax, jax.numpy as jnp
        import numpy as np
        NUM_ITEMS = 25000
        D = 64
        FOURIER_DIM = 64
        VISIT_DIM = 24
        RESIDUAL_SCALE = 0.1
        LN_EPS = 1e-05

        def _layer_norm(x, gamma, beta):
            mu = jnp.mean(x, axis=-1, keepdims=True)
            var = jnp.mean(jnp.square(x - mu), axis=-1, keepdims=True)
            return (x - mu) * jax.lax.rsqrt(var + LN_EPS) * gamma + beta
        gelu = lambda x: jax.nn.gelu(x, approximate=False)
        safe_ids = jnp.clip(item_ids, 0, emb_table.shape[0] - 1)
        item_emb = emb_table[safe_ids]
        fourier_feat = geo_table[safe_ids]
        visit_feat = visit_table[safe_ids]
        item_h = gelu(item_emb @ w_item + b_item)
        geo_h = gelu(fourier_feat @ w_geo + b_geo)
        visit_h = gelu(visit_feat @ w_visit + b_visit)
        cat = jnp.concatenate([item_h, geo_h, visit_h], axis=-1)
        fused = _layer_norm(gelu(cat @ w_fuse + b_fuse), ln_gamma, ln_beta)
        valid_mask = (item_ids != 0)[..., None].astype(fused.dtype)
        fused = fused * valid_mask
        return item_emb + RESIDUAL_SCALE * fused

    def _L0_attn_ref(x, ln1_g, ln1_b, mln_g, mln_b, w_in, conv_w, conv_b, w_xproj, w_dt, b_dt, A_log, D, w_out, ln2_g, ln2_b, fc1_w, bn1_s, bn1_b, Wr, Wi, rb, ib, fc2_w, bn2_s, bn2_b):
        import jax, jax.numpy as jnp
        import numpy as np
        B0, L0, C0 = (4, 144, 64)
        DST, DCONV, EXP = (48, 4, 2)
        DIN = EXP * C0
        DTR = C0 // 16
        FD = 2 * C0

        def _ln(x, g, b, eps=0.001):
            m = jnp.mean(x, -1, keepdims=True)
            v = jnp.mean((x - m) ** 2, -1, keepdims=True)
            return (x - m) / jnp.sqrt(v + eps) * g + b

        def _selective_scan(u, delta, A, Bm, Cm, D):
            dA = jnp.einsum('bld,dn->bldn', delta, A)
            dB_u = jnp.einsum('bld,bld,bln->bldn', delta, u, Bm)
            shifted = jnp.pad(dA[:, 1:], ((0, 0), (1, 1), (0, 0), (0, 0)))[:, 1:]
            dA_cumsum = jnp.exp(jnp.cumsum(shifted[:, ::-1], axis=1))[:, ::-1]
            xs = jnp.cumsum(dB_u * dA_cumsum, axis=1) / (dA_cumsum + 1e-12)
            y = jnp.einsum('bldn,bln->bld', xs, Cm)
            return y + u * D

        def _forward(x, ln1_g, ln1_b, mln_g, mln_b, w_in, conv_w, conv_b, w_xproj, w_dt, b_dt, A_log, D, w_out, ln2_g, ln2_b, fc1_w, bn1_s, bn1_b, Wr, Wi, rb, ib, fc2_w, bn2_s, bn2_b):
            h = _ln(_ln(x, ln1_g, ln1_b), mln_g, mln_b)
            xr = h @ w_in
            xm, res = (xr[..., :DIN], xr[..., DIN:])
            xp = jnp.pad(xm, ((0, 0), (DCONV - 1, 0), (0, 0)))
            xc = jax.lax.conv_general_dilated(xp, conv_w[:, None, :], (1,), 'VALID', dimension_numbers=('NLC', 'LIO', 'NLC'), feature_group_count=DIN) + conv_b
            xc = jax.nn.silu(xc)
            A = -jnp.exp(A_log)
            x_dbl = xc @ w_xproj
            dt, Bm, Cm = (x_dbl[..., :DTR], x_dbl[..., DTR:DTR + DST], x_dbl[..., DTR + DST:])
            delta = jax.nn.softplus(dt @ w_dt + b_dt)
            y = _selective_scan(xc, delta, A, Bm, Cm, D)
            y = y * jax.nn.silu(res)
            x = x + y @ w_out
            h2 = _ln(x, ln2_g, ln2_b)
            f = jax.nn.relu(h2 @ fc1_w * bn1_s + bn1_b)
            L = f.shape[1]
            scale = L ** 0.5
            fr = jnp.fft.rfft(f, axis=1)
            real, imag = (fr.real / scale, fr.imag / scale)
            xre = jax.nn.relu(jnp.einsum('bnc,cd->bnd', real, Wr) - jnp.einsum('bnc,cd->bnd', imag, Wi) + rb)
            xim = jax.nn.relu(jnp.einsum('bnc,cd->bnd', imag, Wr) + jnp.einsum('bnc,cd->bnd', real, Wi) + ib)
            ff = jnp.fft.irfft((xre + 1j * xim) * scale, n=L, axis=1)
            out2 = ff @ fc2_w * bn2_s + bn2_b
            return x + out2
        return _forward(x, ln1_g, ln1_b, mln_g, mln_b, w_in, conv_w, conv_b, w_xproj, w_dt, b_dt, A_log, D, w_out, ln2_g, ln2_b, fc1_w, bn1_s, bn1_b, Wr, Wi, rb, ib, fc2_w, bn2_s, bn2_b)

    def _L0_ffn_ref(x, sW1, sb1, sW2, sb2, sW3, sb3, eW1, eb1, eW2, eb2, eW3, eb3, gW, gb):
        import jax, jax.numpy as jnp
        import numpy as np
        B, A = (1024, 8)
        IN, OUT = (64, 64)
        SH1, SH2 = (64, 128)
        EH1, EH2 = (128, 64)
        E, TOPK = (4, 2)

        def _shared_mlp(x, W1, b1, W2, b2, W3, b3):
            h = jax.nn.relu(x @ W1 + b1)
            h = jax.nn.relu(h @ W2 + b2)
            return h @ W3 + b3

        def _experts_mlp(x, eW1, eb1, eW2, eb2, eW3, eb3):
            h = jax.nn.relu(jnp.einsum('baf,efh->ebah', x, eW1) + eb1[:, None, None, :])
            h = jax.nn.relu(jnp.einsum('ebah,ehg->ebag', h, eW2) + eb2[:, None, None, :])
            o = jnp.einsum('ebag,ego->ebao', h, eW3) + eb3[:, None, None, :]
            return jnp.moveaxis(o, 0, -1)
        all_out = _experts_mlp(x, eW1, eb1, eW2, eb2, eW3, eb3)
        shared = _shared_mlp(x, sW1, sb1, sW2, sb2, sW3, sb3)
        gates = jax.nn.softmax(x @ gW + gb, axis=-1)
        topv, topi = jax.lax.top_k(gates, TOPK)
        topw = jax.nn.softmax(topv, axis=-1)
        sel = jnp.take_along_axis(all_out, topi[:, :, None, :], axis=-1)
        gated = jnp.sum(sel * topw[:, :, None, :], axis=-1)
        return shared + gated

    def _L1_attn_ref(x, edge_index, edge_attr, Wq, bq, Wk, bk, Wv, bv, Wo, bo, We, be):
        import jax, jax.numpy as jnp
        import numpy as np
        H = 8
        B, N, D = x.shape
        hd = D // H
        q = (x @ Wq + bq).reshape(B, N, H, hd)
        k = (x @ Wk + bk).reshape(B, N, H, hd)
        v = (x @ Wv + bv).reshape(B, N, H, hd)
        scores = jnp.einsum('bihd,bjhd->bhij', q, k) / jnp.sqrt(jnp.asarray(hd, x.dtype))
        eb = edge_attr @ We + be
        edge_tgt = edge_index[1]
        col_bias = jnp.zeros((H, N), x.dtype).at[:, edge_tgt].set(eb.T)
        scores = scores + col_bias[None, :, None, :]
        attn = jax.nn.softmax(scores, axis=-1)
        out = jnp.einsum('bhij,bjhd->bihd', attn, v).reshape(B, N, D)
        return out @ Wo + bo

    def _L1_ffn_ref(input_embeddings, router_w, w1, b1, w2, b2):
        import jax, jax.numpy as jnp
        import numpy as np
        NUM_EXPERTS = 8
        TOP_K = 2
        B, S, D = (8, 2048, 64)

        def _moe(tokens, router_w, w1, b1, w2, b2):
            N = tokens.shape[0]
            E = router_w.shape[0]
            logits = tokens.astype(jnp.float32) @ router_w.astype(jnp.float32).T
            probs = jax.nn.softmax(logits, axis=-1)
            rw, re = jax.lax.top_k(probs, TOP_K)
            if TOP_K > 1:
                rw = rw / jnp.maximum(rw.sum(-1, keepdims=True), 1e-12)
            rw = rw.astype(tokens.dtype)
            combine = jnp.zeros((N, E), tokens.dtype).at[jnp.arange(N)[:, None], re].set(rw)
            out = tokens
            for e in range(E):
                h = jax.nn.gelu(tokens @ w1[e] + b1[e], approximate=False)
                y = h @ w2[e] + b2[e]
                out = out + combine[:, e:e + 1] * y
            return out
        b, s, d = input_embeddings.shape
        tokens = input_embeddings.reshape(b * s, d)
        return _moe(tokens, router_w, w1, b1, w2, b2).reshape(b, s, d)
    h = _L0_tok_ref(x, L0_tok_emb_table, L0_tok_geo_table, L0_tok_visit_table, L0_tok_w_item, L0_tok_b_item, L0_tok_w_geo, L0_tok_b_geo, L0_tok_w_visit, L0_tok_b_visit, L0_tok_w_fuse, L0_tok_b_fuse, L0_tok_ln_gamma, L0_tok_ln_beta)
    h = h + _L0_attn_ref(_layernorm(h, axis=-1), L0_attn_ln1_g, L0_attn_ln1_b, L0_attn_mln_g, L0_attn_mln_b, L0_attn_w_in, L0_attn_conv_w, L0_attn_conv_b, L0_attn_w_xproj, L0_attn_w_dt, L0_attn_b_dt, L0_attn_A_log, L0_attn_D, L0_attn_w_out, L0_attn_ln2_g, L0_attn_ln2_b, L0_attn_fc1_w, L0_attn_bn1_s, L0_attn_bn1_b, L0_attn_Wr, L0_attn_Wi, L0_attn_rb, L0_attn_ib, L0_attn_fc2_w, L0_attn_bn2_s, L0_attn_bn2_b)
    h = h + _L0_ffn_ref(_layernorm(h, axis=-1), L0_ffn_sW1, L0_ffn_sb1, L0_ffn_sW2, L0_ffn_sb2, L0_ffn_sW3, L0_ffn_sb3, L0_ffn_eW1, L0_ffn_eb1, L0_ffn_eW2, L0_ffn_eb2, L0_ffn_eW3, L0_ffn_eb3, L0_ffn_gW, L0_ffn_gb)
    h = h + _L1_attn_ref(_layernorm(h, axis=-1), L1_attn_edge_index, L1_attn_edge_attr, L1_attn_Wq, L1_attn_bq, L1_attn_Wk, L1_attn_bk, L1_attn_Wv, L1_attn_bv, L1_attn_Wo, L1_attn_bo, L1_attn_We, L1_attn_be)
    h = h + _L1_ffn_ref(_layernorm(h, axis=-1), L1_ffn_router_w, L1_ffn_w1, L1_ffn_b1, L1_ffn_w2, L1_ffn_b2)
    return h

_drawn_inputs = setup_inputs


def setup_inputs(seed=0):
    import zlib

    import numpy as np

    out = dict(_drawn_inputs(seed))
    spreads = {'L0_tok_b_item': (0.0, 0.1),
     'L0_tok_b_geo': (0.0, 0.1),
     'L0_tok_b_visit': (0.0, 0.1),
     'L0_tok_b_fuse': (0.0, 0.1),
     'L0_tok_ln_gamma': (1.0, 0.2),
     'L0_tok_ln_beta': (0.0, 0.1),
     'L0_attn_ln1_g': (1.0, 0.6),
     'L0_attn_ln1_b': (0.0, 0.8),
     'L0_attn_mln_g': (1.0, 0.6),
     'L0_attn_mln_b': (0.0, 0.8),
     'L0_attn_conv_b': (0.0, 0.8),
     'L0_attn_b_dt': (0.0, 0.8),
     'L0_attn_D': (1.0, 0.6),
     'L0_attn_ln2_g': (1.0, 0.6),
     'L0_attn_ln2_b': (0.0, 0.8),
     'L0_attn_bn1_s': (1.0, 0.6),
     'L0_attn_bn1_b': (0.0, 0.8),
     'L0_attn_bn2_s': (1.0, 0.6),
     'L0_attn_bn2_b': (0.0, 0.443),
     'L0_ffn_sb1': (0.0, 2.0),
     'L0_ffn_sb2': (0.0, 0.8),
     'L0_ffn_sb3': (0.0, 0.496),
     'L0_ffn_eb1': (0.0, 2.0),
     'L0_ffn_eb2': (0.0, 2.0),
     'L0_ffn_eb3': (0.0, 0.678),
     'L0_ffn_gb': (0.0, 1.948),
     'L1_attn_bq': (0.0, 2.0),
     'L1_attn_bk': (0.0, 2.0),
     'L1_attn_bv': (0.0, 2.0),
     'L1_attn_bo': (0.0, 0.494),
     'L1_attn_be': (0.0, 2.0),
     'L1_ffn_b1': (0.0, 1.418),
     'L1_ffn_b2': (0.0, 0.8)}
    factors = {'L0_attn_w_in': 8.0,
     'L0_attn_conv_w': 8.0,
     'L0_attn_w_xproj': 8.0,
     'L0_attn_w_dt': 8.0,
     'L0_attn_A_log': 8.0,
     'L0_attn_w_out': 8.0,
     'L0_attn_fc1_w': 8.0,
     'L0_attn_Wr': 6.627,
     'L0_attn_Wi': 8.0,
     'L0_attn_rb': 8.0,
     'L0_attn_ib': 8.0,
     'L0_attn_fc2_w': 5.912,
     'L0_ffn_eW1': 14.619,
     'L1_attn_edge_attr': 64.0,
     'L1_attn_Wq': 64.0,
     'L1_attn_Wk': 64.0,
     'L1_attn_We': 64.0,
     'L0_ffn_sW1': 7.214,
     'L0_ffn_sW2': 4.975,
     'L0_ffn_sW3': 4.244,
     'L0_ffn_eW2': 3.634,
     'L0_ffn_gW': 3.565,
     'L1_attn_Wv': 8.0,
     'L1_attn_Wo': 4.109}
    for name, (base, spread) in spreads.items():
        noise = np.random.default_rng([zlib.crc32(name.encode()), seed]).standard_normal(out[name].shape)
        drawn = base * np.exp(spread * noise) if base else spread * noise
        out[name] = jnp.asarray(drawn.astype(out[name].dtype))
    for name, factor in factors.items():
        out[name] = (out[name] * factor).astype(out[name].dtype)
    return out
```

```python
from contextlib import ExitStack

import concourse.bass as bass
from concourse import mybir

F32 = mybir.dt.float32
BF16 = mybir.dt.bfloat16
I32 = mybir.dt.int32
ALU = mybir.AluOpType
ACT = mybir.ActivationFunctionType
AX = mybir.AxisListType

P = 128
SEQS, L, D = 32, 512, 64
C = L // P
G = SEQS * C
ITEMS = 25000
VISIT = 24
ROW = 2 * D + VISIT
DIN, DST, DTR = 128, 48, 4
CONV = 4
FD = 128
HEADS, HD = 8, 8
EDGES = 16384
E0, E1 = 4, 8
ds = bass.ds


class Count:

    def __init__(self, base=0):
        self.base, self.n = base, 0

    def up(self):
        self.n += 1
        return 1

    @property
    def value(self):
        return self.base + self.n


def past(n):
    return n + 1


def arm(nc, sems):
    with nc.Block() as block:
        @block.sync
        def _(sp):
            for s in sems:
                sp.sem_inc(s, 1)


def renew(nc):
    with nc.Block() as block:
        @block.sync
        def _(sp):
            numbers = sorted(nc.released_uncleared_semaphores)
            sp.sem_clear(range(numbers[0], numbers[-1] + 1))


def rows3(tile, g0, n):
    return tile[:, ds(g0, n), :]


def layer_norm(nc, name, src, dst, eps, gamma=None, beta=None):
    W = 16
    steps = G // W
    with ExitStack() as ctx:
        sq = [ctx.enter_context(nc.sbuf_tensor(f"{name}_sq{i}", [P, W, D], F32)) for i in range(2)]
        total = ctx.enter_context(nc.sbuf_tensor(f"{name}_total", [P, G], F32))
        var = ctx.enter_context(nc.sbuf_tensor(f"{name}_var", [P, G], F32))
        rstd = ctx.enter_context(nc.sbuf_tensor(f"{name}_rstd", [P, G], F32))
        eps_col = ctx.enter_context(nc.sbuf_tensor(f"{name}_eps", [P, 1], F32))
        summed = ctx.enter_context(nc.semaphore(f"{name}_summed"))
        centred = ctx.enter_context(nc.semaphore(f"{name}_centred"))
        squared = ctx.enter_context(nc.semaphore(f"{name}_squared"))
        spread = ctx.enter_context(nc.semaphore(f"{name}_spread"))
        rooted = ctx.enter_context(nc.semaphore(f"{name}_rooted"))
        scaled = ctx.enter_context(nc.semaphore(f"{name}_scaled"))
        block = ctx.enter_context(nc.Block())

        def over(stat, g0, n):
            return stat[:, ds(g0, n)].unsqueeze(2).to_broadcast([P, n, D])

        @block.vector
        def _(vec):
            vec.memset(eps_col[:], eps).then_inc(spread, 1)
            with vec.Fori(0, steps // 2) as i:
                for p in range(2):
                    k = i * 2 + p
                    vec.tensor_reduce(total[:, ds(k * W, W)], rows3(src, k * W, W), AX.X, ALU.add).then_inc(summed, 1)
                for p in range(2):
                    k = i * 2 + p
                    vec.wait_ge(summed, k + 1)
                    vec.scalar_tensor_tensor(rows3(dst, k * W, W), over(total, k * W, W), -1.0 / D,
                                             rows3(src, k * W, W), ALU.mult, ALU.add).then_inc(centred, 1)
                for p in range(2):
                    k = i * 2 + p
                    vec.wait_ge(squared, k + 1)
                    vec.tensor_reduce(var[:, ds(k * W, W)], sq[p][:], AX.X, ALU.add).then_inc(spread, 1)
            vec.wait_ge(rooted, 2)
            with vec.Fori(0, steps) as k:
                vec.wait_ge(centred, steps)
                vec.tensor_tensor(rows3(dst, k * W, W), rows3(dst, k * W, W), over(rstd, k * W, W),
                                  ALU.mult).then_inc(scaled, 1)
                if gamma is not None:
                    vec.wait_ge(scaled, k * 3 + 1)
                    vec.tensor_tensor(rows3(dst, k * W, W), rows3(dst, k * W, W),
                                      gamma[:].unsqueeze(1).to_broadcast([P, W, D]), ALU.mult).then_inc(scaled, 1)
                    vec.wait_ge(scaled, k * 3 + 2)
                    vec.tensor_tensor(rows3(dst, k * W, W), rows3(dst, k * W, W),
                                      beta[:].unsqueeze(1).to_broadcast([P, W, D]), ALU.add).then_inc(scaled, 1)

        @block.scalar
        def _(act):
            with act.Fori(0, steps // 2) as i:
                for p in range(2):
                    k = i * 2 + p
                    act.wait_ge(centred, k + 1)
                    act.wait_ge(spread, i * 2 + 1)
                    nc.scalar.activation(sq[p][:], rows3(dst, k * W, W), ACT.Square).then_inc(squared, 1)
            act.wait_ge(spread, steps + 1)
            nc.scalar.activation(rstd[:], var[:], ACT.Ln, scale=1.0 / D, bias=eps_col[:]).then_inc(rooted, 1)
            act.wait_ge(rooted, 1)
            nc.scalar.activation(rstd[:], rstd[:], ACT.Exp, scale=-0.5).then_inc(rooted, 1)


def load(nc, name, pairs, gpsimd_pairs=()):
    with ExitStack() as ctx:
        landed = ctx.enter_context(nc.semaphore(f"{name}_landed"))
        block = ctx.enter_context(nc.Block())

        @block.sync
        def _(sp):
            for dst, src in pairs[::2]:
                sp.dma_start(dst, src).then_inc(landed, 16)
            sp.wait_ge(landed, 16 * len(pairs))

        @block.scalar
        def _(act):
            for dst, src in pairs[1::2]:
                act.dma_start(dst, src).then_inc(landed, 16)


def column(vector):
    return vector.rearrange("(n o) -> n o", o=1)


def row(vector):
    return vector.rearrange("(o n) -> o n", o=1)


def spread_row(vector):
    return row(vector).to_broadcast([P, vector.shape[0]])


def embed(nc, w, H):
    with ExitStack() as ctx:
        def sb(name, shape, dt=F32):
            return ctx.enter_context(nc.sbuf_tensor(name, shape, dt))

        ids = sb("ids", [P, G], I32)
        rows_at = sb("rows_at", [P, G], I32)
        keep = sb("keep", [P, G])
        emb = sb("emb", [P, G, D])
        w_pair = sb("w_pair", [P, P])
        w_visit = sb("w_visit", [VISIT, D])
        b_pair = sb("b_pair", [P, 1])
        b_visit = sb("b_visit", [D, 1])
        fuse_a = sb("fuse_a", [P, D])
        fuse_b = sb("fuse_b", [D + 1, D])
        gamma = sb("tok_gamma", [P, D])
        beta = sb("tok_beta", [P, D])
        at = [sb(f"at{p}", [P, C], I32) for p in range(2)]
        rows = [sb(f"rows{p}", [P, C, ROW]) for p in range(2)]
        pairT = sb("pairT", [P, L])
        visitT = sb("visitT", [VISIT, L])
        pair_h = sb("pair_h", [P, L])
        visit_h = sb("visit_h", [D + 1, L])

        with ExitStack() as zero:
            zeroed = zero.enter_context(nc.semaphore("tok_zeroed"))
            block = zero.enter_context(nc.Block())

            @block.vector
            def _(vec):
                vec.memset(w_pair[:], 0.0).then_inc(zeroed, 1)
                vec.memset(visit_h[D:D + 1, :], 1.0).then_inc(zeroed, 1)

        load(nc, "tok_w", [
            (ids[:], w["ids"]), (w_pair[0:D, 0:D], w["L0_tok_w_item"]), (w_pair[D:P, D:P], w["L0_tok_w_geo"]),
            (w_visit[:], w["L0_tok_w_visit"]), (b_pair[0:D, :], column(w["L0_tok_b_item"])),
            (b_pair[D:P, :], column(w["L0_tok_b_geo"])), (b_visit[:], column(w["L0_tok_b_visit"])),
            (fuse_a[:], w["L0_tok_w_fuse"][0:P, :]), (fuse_b[0:D, :], w["L0_tok_w_fuse"][P:P + D, :]),
            (fuse_b[D:D + 1, :], row(w["L0_tok_b_fuse"])),
            (gamma[:], spread_row(w["L0_tok_ln_gamma"])), (beta[:], spread_row(w["L0_tok_ln_beta"]))])

        with ExitStack() as run:
            sems = []

            def sem(name):
                sems.append(run.enter_context(nc.semaphore(name)))
                return sems[-1]

            ps_pair = run.enter_context(nc.psum_tensor("ps_pair", [P, L], F32))
            ps_visit = run.enter_context(nc.psum_tensor("ps_visit", [VISIT, L], F32))
            ps_ph = run.enter_context(nc.psum_tensor("ps_ph", [P, L], F32))
            ps_vh = run.enter_context(nc.psum_tensor("ps_vh", [D, L], F32))
            ps_fuse = run.enter_context(nc.psum_tensor("ps_fuse", [P, C, D], F32))
            passed, ids_ready, at_ready = sem("tok_passed"), sem("ids_ready"), sem("at_ready")
            gathered = w["gathered"][0:2]
            turned = [sem(f"turned{p}") for p in range(2)]
            emb_kept = [sem(f"emb_kept{p}") for p in range(2)]
            pair_copied, visit_copied = sem("pair_copied"), sem("visit_copied")
            projected, gelus, fused, stored = sem("projected"), sem("gelus"), sem("fused"), sem("stored")
            arm(nc, sems)
            block = run.enter_context(nc.Block())

            @block.gpsimd
            def _(pool):
                pool.wait_ge(ids_ready, past(1))
                with pool.Fori(0, SEQS // 2) as i:
                    for p in range(2):
                        b = i * 2 + p
                        pool.wait_ge(turned[p], past(i))
                        pool.wait_ge(emb_kept[p], past(i))
                        nc.gpsimd.tensor_copy(at[p][:], rows_at[:, ds(b * C, C)]).then_inc(at_ready, 1)
                        pool.wait_ge(at_ready, past(b + 1))
                        pool.sem_inc(passed, 1)
                        for c in range(C):
                            nc.gpsimd.indirect_dma_start(
                                out=rows[p][:, c, :], out_offset=None, in_=w["table"],
                                in_offset=bass.IndirectOffsetOnAxis(ap=at[p][:, c:c + 1], axis=0),
                            ).then_inc(gathered[p], 16)

            @block.tensor
            def _(pe):
                with pe.Fori(0, SEQS // 2) as i:
                    for p in range(2):
                        b = i * 2 + p
                        pe.wait_ge(gathered[p], i * (16 * C) + 16 * C)
                        pe.wait_ge(pair_copied, past(b))
                        pe.wait_ge(visit_copied, past(b))
                        pe.sem_inc(passed, 1)
                        for c in range(C):
                            nc.tensor.transpose(ps_pair[:, c * P:(c + 1) * P], rows[p][:, c, 0:P], w["ident"][:])
                        for c in range(C):
                            last = nc.tensor.transpose(ps_visit[:, c * P:(c + 1) * P], rows[p][:, c, P:ROW],
                                                       w["ident"][:])
                        last.then_inc(turned[p], 1)
                        pe.wait_ge(pair_copied, past(b + 1))
                        pe.wait_ge(gelus, past(b))
                        nc.tensor.matmul(ps_ph[:], w_pair[:], pairT[:], start=True, stop=True)
                        pe.wait_ge(visit_copied, past(b + 1))
                        nc.tensor.matmul(ps_vh[:], w_visit[:], visitT[:], start=True, stop=True).then_inc(projected, 1)
                        pe.wait_ge(gelus, past(b + 1))
                        pe.wait_ge(stored, past(b))
                        pe.sem_inc(passed, 1)
                        for c in range(C):
                            nc.tensor.matmul(ps_fuse[:, c, :], pair_h[:, c * P:(c + 1) * P], fuse_a[:],
                                             start=True, stop=False)
                            last = nc.tensor.matmul(ps_fuse[:, c, :], visit_h[:, c * P:(c + 1) * P], fuse_b[:],
                                                    start=False, stop=True)
                        last.then_inc(fused, 1)

            @block.vector
            def _(vec):
                vec.tensor_scalar(rows_at[:], ids[:], 0.0, float(ITEMS), ALU.max, ALU.min).then_inc(ids_ready, 1)
                vec.tensor_scalar(keep[:], ids[:], 0.0, 0.1, ALU.not_equal, ALU.mult).then_inc(ids_ready, 1)
                with vec.Fori(0, SEQS // 2) as i:
                    for p in range(2):
                        b = i * 2 + p
                        vec.wait_ge(turned[p], past(i + 1))
                        nc.vector.tensor_copy(pairT[:], ps_pair[:]).then_inc(pair_copied, 1)
                        nc.vector.tensor_copy(rows3(emb, b * C, C), rows[p][:, :, 0:D]).then_inc(emb_kept[p], 1)

            @block.scalar
            def _(act):
                with act.Fori(0, SEQS // 2) as i:
                    for p in range(2):
                        b = i * 2 + p
                        act.wait_ge(turned[p], past(i + 1))
                        nc.scalar.activation(visitT[:], ps_visit[:], ACT.Copy).then_inc(visit_copied, 1)
                        act.wait_ge(projected, past(b + 1))
                        act.wait_ge(fused, past(b))
                        nc.scalar.activation(pair_h[:], ps_ph[:], ACT.Gelu, bias=b_pair[:])
                        nc.scalar.activation(visit_h[0:D, :], ps_vh[:], ACT.Gelu, bias=b_visit[:]).then_inc(gelus, 1)
                        act.wait_ge(fused, past(b + 1))
                        act.sem_inc(passed, 1)
                        nc.scalar.activation(rows3(H, b * C, C), ps_fuse[:], ACT.Gelu).then_inc(stored, 1)

        layer_norm(nc, "tok_ln", H, H, 1e-5, gamma, beta)

        with ExitStack() as run:
            masked = run.enter_context(nc.semaphore("tok_masked"))
            block = run.enter_context(nc.Block())

            @block.vector
            def _(vec):
                W = 16
                with vec.Fori(0, G // W) as k:
                    vec.tensor_tensor(rows3(H, k * W, W), rows3(H, k * W, W),
                                      keep[:, ds(k * W, W)].unsqueeze(2).to_broadcast([P, W, D]),
                                      ALU.mult).then_inc(masked, 1)
                    vec.wait_ge(masked, k * 2 + 1)
                    vec.tensor_tensor(rows3(H, k * W, W), rows3(H, k * W, W), rows3(emb, k * W, W),
                                      ALU.add).then_inc(masked, 1)


def move(nc, name, dst, src):
    with ExitStack() as ctx:
        moved = ctx.enter_context(nc.semaphore(f"{name}_moved"))
        block = ctx.enter_context(nc.Block())

        @block.sync
        def _(sp):
            sp.dma_start(dst, src).then_inc(moved, 16)
            sp.wait_ge(moved, 16)


def clear(nc, name, tile):
    with ExitStack() as ctx:
        cleared = ctx.enter_context(nc.semaphore(f"{name}_cleared"))
        block = ctx.enter_context(nc.Block())

        @block.vector
        def _(vec):
            vec.memset(tile, 0.0).then_inc(cleared, 1)


def mamba_inputs(nc, w, H, X, scr):
    with ExitStack() as ctx:
        def sb(name, shape, dt=F32):
            return ctx.enter_context(nc.sbuf_tensor(name, shape, dt))

        T = sb("pre_T", [P, G, D])
        norms = [sb(f"pre_{n}", [P, D]) for n in ("g1", "b1", "g2", "b2")]
        w_in = sb("pre_w_in", [D, 2 * DIN])
        w_bc = sb("pre_w_bc", [DIN, 2 * DST])
        w_dtin = sb("pre_w_dtin", [DIN, DTR])
        w_dt = sb("pre_w_dt", [DTR, DIN])
        taps = sb("pre_taps", [DIN, CONV])
        conv_b = sb("pre_conv_b", [DIN, 1])
        dt_b = sb("pre_dt_b", [DIN, 1])
        load(nc, "pre_w", [
            (norms[0][:], spread_row(w["L0_attn_ln1_g"])), (norms[1][:], spread_row(w["L0_attn_ln1_b"])),
            (norms[2][:], spread_row(w["L0_attn_mln_g"])), (norms[3][:], spread_row(w["L0_attn_mln_b"])),
            (w_in[:], w["L0_attn_w_in"]), (w_bc[:], w["L0_attn_w_xproj"][:, DTR:]),
            (w_dtin[:], w["L0_attn_w_xproj"][:, 0:DTR]), (w_dt[:], w["L0_attn_w_dt"]),
            (taps[:], w["conv_taps"]), (conv_b[:], column(w["L0_attn_conv_b"])),
            (dt_b[:], column(w["L0_attn_b_dt"]))])
        layer_norm(nc, "ln_x", H, X, 1e-5)
        layer_norm(nc, "ln_1", X, T, 1e-3, norms[0], norms[1])
        layer_norm(nc, "ln_2", T, T, 1e-3, norms[2], norms[3])

        sems = []

        def sem(name):
            sems.append(ctx.enter_context(nc.semaphore(name)))
            return sems[-1]

        cur = [sb(f"pre_cur{p}", [P, C, D]) for p in range(2)]
        mT = sb("pre_mT", [D, L])
        conv = sb("pre_conv", [DIN, L])
        u = [sb(f"pre_u{p}", [DIN, L]) for p in range(2)]
        gate = [sb(f"pre_gate{p}", [DIN, L]) for p in range(2)]
        delta = [sb(f"pre_delta{p}", [DIN, L]) for p in range(2)]
        parts = [sb(f"pre_parts{p}", [2 * DST, 3, L], BF16) for p in range(2)]
        rest = sb("pre_rest", [2 * DST, L])
        dts = sb("pre_dts", [DTR, L])
        size = sb("pre_size", [DIN, L])
        soft = sb("pre_soft", [DIN, L])
        ps_m = ctx.enter_context(nc.psum_tensor("ps_m", [D, L], F32))
        ps_xm = ctx.enter_context(nc.psum_tensor("ps_xm", [DIN, L], F32))
        ps_res = ctx.enter_context(nc.psum_tensor("ps_res", [DIN, L], F32))
        ps_bc = ctx.enter_context(nc.psum_tensor("ps_bc", [2 * DST, L], F32))
        ps_dt = ctx.enter_context(nc.psum_tensor("ps_dt", [DTR, L], F32))
        ps_delta = ctx.enter_context(nc.psum_tensor("ps_delta", [DIN, L], F32))
        cur_ready = [sem(f"pre_cur_ready{p}") for p in range(2)]
        turned = [sem(f"pre_turned{p}") for p in range(2)]
        passed, m_copied, projected, convolved = sem("pre_passed"), sem("pre_m_copied"), sem("pre_projected"), sem("pre_convolved")
        tap_done, gated, u_ready = sem("pre_tap_done"), sem("pre_gated"), sem("pre_u_ready")
        xdbl, dt_copied, dt_spread = sem("pre_xdbl"), sem("pre_dt_copied"), sem("pre_dt_spread")
        soft_step, softened, delta_ready = sem("pre_soft_step"), sem("pre_softened"), sem("pre_delta_ready")
        soft_max = sem("pre_soft_max")
        high, mid, split, rest_ready = sem("pre_high"), sem("pre_mid"), sem("pre_split"), sem("pre_rest_ready")
        saved = [sem(f"pre_saved{p}") for p in range(2)]
        arm(nc, sems)
        block = ctx.enter_context(nc.Block())
        SAVES = 4

        @block.gpsimd
        def _(pool):
            with pool.Fori(0, SEQS // 2) as i:
                for p in range(2):
                    pool.wait_ge(turned[p], past(i))
                    nc.gpsimd.tensor_copy(cur[p][:], rows3(T, (i * 2 + p) * C, C)).then_inc(cur_ready[p], 1)

        @block.tensor
        def _(pe):
            with pe.Fori(0, SEQS // 2) as i:
                for p in range(2):
                    b = i * 2 + p
                    pe.wait_ge(cur_ready[p], past(i + 1))
                    pe.wait_ge(m_copied, past(b))
                    pe.sem_inc(passed, 1)
                    for c in range(C):
                        last = nc.tensor.transpose(ps_m[:, c * P:(c + 1) * P], cur[p][:, c, :], w["ident"][:])
                    last.then_inc(turned[p], 1)
                    pe.wait_ge(m_copied, past(b + 1))
                    pe.wait_ge(convolved, past(b))
                    pe.wait_ge(gated, past(b))
                    nc.tensor.matmul(ps_xm[:], w_in[:, 0:DIN], mT[:], start=True, stop=True)
                    nc.tensor.matmul(ps_res[:], w_in[:, DIN:], mT[:], start=True, stop=True).then_inc(projected, 1)
                    pe.wait_ge(u_ready, past(b + 1))
                    pe.wait_ge(dt_copied, past(b))
                    pe.wait_ge(split, past(b))
                    nc.tensor.matmul(ps_dt[:], w_dtin[:], u[p][:], start=True, stop=True)
                    nc.tensor.matmul(ps_bc[:], w_bc[:], u[p][:], start=True, stop=True).then_inc(xdbl, 1)
                    pe.wait_ge(dt_copied, past(b + 1))
                    pe.wait_ge(delta_ready, past(b))
                    nc.tensor.matmul(ps_delta[:], w_dt[:], dts[:], start=True, stop=True).then_inc(dt_spread, 1)

        @block.vector
        def _(vec):
            with vec.Fori(0, SEQS // 2) as i:
                for p in range(2):
                    b = i * 2 + p
                    vec.wait_ge(turned[p], past(i + 1))
                    nc.vector.tensor_copy(mT[:], ps_m[:]).then_inc(m_copied, 1)
                    vec.wait_ge(projected, past(b + 1))
                    vec.wait_ge(u_ready, past(b))
                    step = Count(b * (CONV - 1))
                    vec.tensor_scalar(conv[:], ps_xm[:], taps[:, CONV - 1:CONV], None,
                                      ALU.mult).then_inc(tap_done, step.up())
                    for k in range(CONV - 2, -1, -1):
                        lag = CONV - 1 - k
                        vec.wait_ge(tap_done, past(step.value))
                        done = vec.scalar_tensor_tensor(conv[:, lag:], ps_xm[:, 0:L - lag], taps[:, k:k + 1],
                                                        conv[:, lag:], ALU.mult, ALU.add)
                        if k:
                            done.then_inc(tap_done, step.up())
                        else:
                            done.then_inc(convolved, 1)
                    vec.wait_ge(xdbl, past(b + 1))
                    nc.vector.tensor_copy(dts[:], ps_dt[:]).then_inc(dt_copied, 1)
                    vec.wait_ge(high, past(b + 1))
                    vec.tensor_tensor(rest[:], ps_bc[:], parts[p][:, 0, :], ALU.subtract).then_inc(rest_ready, 1)
                    vec.wait_ge(mid, past(b + 1))
                    vec.tensor_tensor(parts[p][:, 2, :], rest[:], parts[p][:, 1, :], ALU.subtract).then_inc(split, 1)
                    vec.wait_ge(softened, past(b + 1))
                    vec.wait_ge(saved[p], past(i * (16 * SAVES)))
                    vec.tensor_scalar(size[:], ps_delta[:], dt_b[:], 0.0, ALU.add, ALU.max).then_inc(soft_max, 1)
                    vec.wait_ge(soft_max, past(b + 1))
                    vec.tensor_tensor(delta[p][:], size[:], soft[:], ALU.add).then_inc(delta_ready, 1)

        @block.scalar
        def _(act):
            with act.Fori(0, SEQS // 2) as i:
                for p in range(2):
                    b = i * 2 + p
                    act.wait_ge(projected, past(b + 1))
                    act.wait_ge(saved[p], past(i * (16 * SAVES)))
                    nc.scalar.activation(gate[p][:], ps_res[:], ACT.Silu).then_inc(gated, 1)
                    act.wait_ge(convolved, past(b + 1))
                    nc.scalar.activation(u[p][:], conv[:], ACT.Silu, bias=conv_b[:]).then_inc(u_ready, 1)
                    act.wait_ge(xdbl, past(b + 1))
                    nc.scalar.activation(parts[p][:, 0, :], ps_bc[:], ACT.Copy).then_inc(high, 1)
                    act.wait_ge(rest_ready, past(b + 1))
                    nc.scalar.activation(parts[p][:, 1, :], rest[:], ACT.Copy).then_inc(mid, 1)
                    act.wait_ge(dt_spread, past(b + 1))
                    act.wait_ge(delta_ready, past(b))
                    step = Count(b * 2)
                    nc.scalar.activation(soft[:], ps_delta[:], ACT.Abs, bias=dt_b[:]).then_inc(soft_step, step.up())
                    act.wait_ge(soft_step, past(step.value))
                    nc.scalar.activation(soft[:], soft[:], ACT.Exp, scale=-1.0).then_inc(soft_step, step.up())
                    act.wait_ge(soft_step, past(step.value))
                    nc.scalar.activation(soft[:], soft[:], ACT.Ln, bias=1.0).then_inc(softened, 1)

        @block.sync
        def _(sp):
            with sp.Fori(0, SEQS // 2) as i:
                for p in range(2):
                    b = i * 2 + p
                    sp.wait_ge(gated, past(b + 1))
                    sp.dma_start(scr["gate"][:, ds(b, 1), :], gate[p][:].unsqueeze(1)).then_inc(saved[p], 16)
                    sp.wait_ge(u_ready, past(b + 1))
                    sp.dma_start(scr["u"][:, ds(b, 1), :], u[p][:].unsqueeze(1)).then_inc(saved[p], 16)
                    sp.wait_ge(split, past(b + 1))
                    sp.sem_inc(passed, 1)
                    sp.dma_start(scr["bc"][:, :, ds(b, 1), :], parts[p][:].unsqueeze(2)).then_inc(saved[p], 16)
                    sp.wait_ge(delta_ready, past(b + 1))
                    sp.dma_start(scr["delta"][:, ds(b, 1), :], delta[p][:].unsqueeze(1)).then_inc(saved[p], 16)
            for p in range(2):
                sp.wait_ge(saved[p], past(16 * SAVES * (SEQS // 2)))


NR = 12
ROUNDS = DST // NR
PAIRS = SEQS // 2
AHEAD = 8
LOG_EPS = -27.631021115928547


def selective_scan(nc, w, X, scr):
    with ExitStack() as ctx:
        def sb(name, shape, dt=F32):
            return ctx.enter_context(nc.sbuf_tensor(name, shape, dt))

        sems = []

        def sem(name):
            sems.append(ctx.enter_context(nc.semaphore(name)))
            return sems[-1]

        A = sb("A", [DIN, DST])
        skip = sb("skip", [DIN, 1])
        w_out = sb("w_out", [DIN, D])
        sel_f = sb("sel_f", [3 * NR, NR, P])
        sel = sb("sel", [3 * NR, NR, P], BF16)
        ones = sb("scan_ones", [P, L])
        bias = sb("scan_bias", [P, 1])
        load(nc, "scan_w", [(A[:], w["L0_attn_A_log"]), (skip[:], column(w["L0_attn_D"])),
                            (w_out[:], w["L0_attn_w_out"]), (sel_f[:], w["scan_select"])])
        T2 = 2 * L
        delta = [sb(f"delta{p}", [DIN, 2, L]) for p in range(2)]
        u = [sb(f"u{p}", [DIN, 2, L]) for p in range(2)]
        gate = sb("gate", [DIN, 2, L])
        bc = [sb(f"bc{p}", [3 * NR, 2 * ROUNDS, 2, L], BF16) for p in range(2)]
        du = sb("du", [DIN, 2, L])
        after = sb("after", [DIN, 2, L])
        GA = 3
        decay = [sb(f"decay{k}", [DIN, 2, L]) for k in range(2 * GA)]
        guard = [sb(f"guard{k}", [DIN, 2, L]) for k in range(2 * GA)]
        h = [sb(f"h{k}", [DIN, 2, L]) for k in range(2)]
        hg = [sb(f"hg{k}", [DIN, 2, L]) for k in range(3)]
        ch = [sb(f"ch{k}", [DIN, 2, L]) for k in range(2)]
        y = sb("y", [DIN, 2, L])
        ps_b = [ctx.enter_context(nc.psum_tensor(f"ps_b{k}", [DIN, 2, L], F32)) for k in range(2)]
        ps_c = ctx.enter_context(nc.psum_tensor("ps_c", [DIN, 2, L], F32))
        ps_y = ctx.enter_context(nc.psum_tensor("ps_y", [DIN, 2, L], F32))
        ps_o = ps_c[:, 0, :].rearrange("p (g d) -> p g d", d=D)

        passed, a_step = sem("scan_passed"), sem("a_step")
        loaded = [sem(f"scan_loaded{p}") for p in range(2)]
        gate_in = sem("gate_in")
        y_step = [sem(f"y_step{p}") for p in range(2)]
        prepared, b_ready, c_ready = sem("prepared"), sem("b_ready"), sem("c_ready")
        decayed, guarded, fed = sem("decayed"), sem("guarded"), sem("fed")
        scanned, multiplied, weighted, summed = sem("scanned"), sem("multiplied"), sem("weighted"), sem("h_summed")
        y_done, projected, added = sem("y_done"), sem("out_projected"), sem("x_added")
        arm(nc, sems)
        block = ctx.enter_context(nc.Block())

        def done(n):
            return past(n + (AHEAD + 1))

        LOADS = 2 + 6
        @block.sync
        def _(sp):
            with sp.Fori(0, PAIRS // 2) as i:
                for p in range(2):
                    pair = i * 2 + p
                    sp.wait_ge(y_step[p], past(i))
                    sp.dma_start(delta[p][:], scr["delta"][:, ds(pair * 2, 2), :]).then_inc(loaded[p], 16)
                    sp.dma_start(u[p][:], scr["u"][:, ds(pair * 2, 2), :]).then_inc(loaded[p], 16)
                    for part in range(3):
                        for half in range(2):
                            src = scr["bc"][half * DST:(half + 1) * DST, part, ds(pair * 2, 2), :]
                            sp.dma_start(bc[p][part * NR:(part + 1) * NR, half * ROUNDS:(half + 1) * ROUNDS],
                                         src.rearrange("(j r) s t -> r j (s t)", r=NR)
                                         .rearrange("r j (s t) -> r j s t", s=2)).then_inc(loaded[p], 16)
                    sp.wait_ge(y_done, past(pair))
                    sp.dma_start(gate[:], scr["gate"][:, ds(pair * 2, 2), :]).then_inc(gate_in, 16)

        @block.tensor
        def _(pe):
            def spread(dst, p, r, j, half):
                for s in range(2):
                    last = nc.tensor.matmul(dst[:, s, :], sel[:, r, :], bc[p][:, ds(half * ROUNDS + j, 1), s, :],
                                            start=True, stop=True)
                return last

            pe.sem_inc(b_ready, AHEAD)
            pe.sem_inc(c_ready, AHEAD)
            pe.sem_inc(summed, AHEAD)
            pe.wait_ge(a_step, past(7))
            with pe.Fori(0, PAIRS // 2) as i:
                for p in range(2):
                    pair = i * 2 + p
                    pe.wait_ge(loaded[p], past(i * (16 * LOADS) + 16 * LOADS))

                    def b_item(r, j):
                        pe.wait_ge(scanned, done(pair * DST + j * NR + r - 2))
                        pe.sem_inc(passed, 1)
                        spread(ps_b[r % 2], p, r, j, 0).then_inc(b_ready, 1)

                    def c_item(r, j):
                        n = pair * DST + j * NR + r
                        pe.wait_ge(weighted, done(n - 1))
                        pe.sem_inc(passed, 1)
                        spread(ps_c, p, r, j, 1).then_inc(c_ready, 1)

                    def y_item(r, j, first=False, final=False):
                        n = pair * DST + j * NR + r
                        pe.wait_ge(weighted, done(n))
                        for s in range(2):
                            last = nc.tensor.matmul(ps_y[:, s, :], w["ident"][:], ch[r % 2][:, s, :],
                                                    start=first, stop=final)
                        last.then_inc(summed, 1)

                    def step(r, j, peeled=False):
                        if r < NR - 1:
                            b_item(r + 1, j)
                        elif peeled or j is not None:
                            b_next(j)
                        if not (peeled and r < 1):
                            c_item((r - 1) % NR, j if r >= 1 else j - 1)
                        if not (peeled and r < 2):
                            y_item((r - 2) % NR, j if r >= 2 else j - 1, first=peeled and r == 2)

                    def b_next(j):
                        b_item(0, j + 1)

                    pe.wait_ge(added, past(pair))
                    b_item(0, 0)
                    for r in range(NR):
                        step(r, 0, peeled=True)
                    with pe.Fori(1, ROUNDS - 1) as j:
                        for r in range(NR):
                            step(r, j)
                    for r in range(NR):
                        j = ROUNDS - 1
                        if r < NR - 1:
                            b_item(r + 1, j)
                        c_item((r - 1) % NR, j if r >= 1 else j - 1)
                        y_item((r - 2) % NR, j if r >= 2 else j - 1)
                    j = ROUNDS - 1
                    c_item(NR - 1, j)
                    y_item(NR - 2, j)
                    y_item(NR - 1, j, final=True)
                    pe.wait_ge(y_done, past(pair + 1))
                    for g in range(2 * C):
                        last = nc.tensor.matmul(ps_o[:, g, :], y[:, g // C, (g % C) * P:(g % C + 1) * P], w_out[:],
                                                start=True, stop=True)
                    last.then_inc(projected, 1)

        @block.scalar
        def _(act):
            act.sem_inc(decayed, AHEAD)
            act.sem_inc(guarded, AHEAD)
            nc.scalar.activation(A[:], A[:], ACT.Exp).then_inc(a_step, 1)
            act.wait_ge(a_step, past(7))
            with act.Fori(0, PAIRS // 2) as i:
                for p in range(2):
                    pair = i * 2 + p
                    act.wait_ge(loaded[p], past(i * (16 * LOADS) + 16 * LOADS))
                    act.wait_ge(prepared, past((pair + 1) * 3))

                    def round_(j):
                        for k in range(NR // GA):
                            for r in range(k * GA, k * GA + GA):
                                n = pair * DST + j * NR + r
                                act.wait_ge(scanned, done(n - 2 * GA))
                                act.sem_inc(passed, 1)
                                nc.scalar.activation(decay[r % (2 * GA)][:, :, 1:], delta[p][:, :, 1:], ACT.Exp,
                                                     scale=A[:, ds(j * NR + r, 1)]).then_inc(decayed, 1)
                            for r in range(k * GA, k * GA + GA):
                                n = pair * DST + j * NR + r
                                act.wait_ge(multiplied, done(n - 2 * GA))
                                act.sem_inc(passed, 1)
                                nc.scalar.activation(guard[r % (2 * GA)][:], after[:], ACT.Sigmoid,
                                                     scale=A[:, ds(j * NR + r, 1)],
                                                     bias=bias[:]).then_inc(guarded, 1)

                    with act.Fori(0, ROUNDS) as j:
                        round_(j)

        @block.gpsimd
        def _(pool):
            pool.sem_inc(multiplied, AHEAD)
            with pool.Fori(0, PAIRS) as pair:
                with pool.Fori(0, ROUNDS) as j:
                    for r in range(NR):
                        n = pair * DST + j * NR + r
                        pool.wait_ge(guarded, done(n))
                        pool.wait_ge(weighted, done(n - 3))
                        pool.wait_ge(scanned, done(n))
                        nc.gpsimd.tensor_tensor(hg[r % 3][:], h[r % 2][:], guard[r % (2 * GA)][:],
                                                ALU.mult).then_inc(multiplied, 1)

        @block.vector
        def _(vec):
            vec.sem_inc(scanned, AHEAD)
            vec.sem_inc(weighted, AHEAD)
            vec.sem_inc(fed, AHEAD)
            nc.vector.tensor_copy(sel[:], sel_f[:]).then_inc(a_step, 1)
            vec.memset(ones[:], 1.0).then_inc(a_step, 1)
            vec.memset(bias[:], -LOG_EPS).then_inc(a_step, 1)
            vec.memset(after[:, :, L - 1:L], 0.0).then_inc(a_step, 1)
            for k in range(2 * GA):
                last = vec.memset(decay[k][:, :, 0:1], 0.0)
            last.then_inc(a_step, 1)
            vec.wait_ge(a_step, past(6))
            vec.tensor_scalar(A[:], A[:], -1.0, None, ALU.mult).then_inc(a_step, 1)
            vec.wait_ge(a_step, past(7))
            with vec.Fori(0, PAIRS // 2) as i:
                for p in range(2):
                    pair = i * 2 + p
                    vec.wait_ge(loaded[p], past(i * (16 * LOADS) + 16 * LOADS))
                    vec.wait_ge(guarded, done(pair * DST - 1))
                    for s in range(2):
                        vec.tensor_tensor_scan(after[:, s, L - 2::-1], ones[:, 0:L - 1], delta[p][:, s, L - 1:0:-1],
                                               0.0, ALU.mult, ALU.add).then_inc(prepared, 1)
                    vec.wait_ge(fed, done(pair * DST - 1))
                    vec.tensor_tensor(du[:], delta[p][:], u[p][:], ALU.mult).then_inc(prepared, 1)
                    vec.wait_ge(prepared, past((pair + 1) * 3))

                    def feed(r, j):
                        vec.wait_ge(b_ready, done(pair * DST + j * NR + r))
                        vec.tensor_tensor(ps_b[r % 2][:], du[:], ps_b[r % 2][:], ALU.mult).then_inc(fed, 1)

                    def scan(r, j):
                        n = pair * DST + j * NR + r
                        vec.wait_ge(decayed, done(n))
                        vec.wait_ge(multiplied, done(n - 2))
                        vec.wait_ge(fed, done(n))
                        vec.tensor_tensor_scan(h[r % 2][:].rearrange("p s t -> p (s t)"),
                                               decay[r % (2 * GA)][:].rearrange("p s t -> p (s t)"),
                                               ps_b[r % 2][:].rearrange("p s t -> p (s t)"),
                                               0.0, ALU.mult, ALU.add).then_inc(scanned, 1)

                    def weight(r, j):
                        n = pair * DST + j * NR + r
                        vec.wait_ge(multiplied, done(n))
                        vec.wait_ge(c_ready, done(n))
                        vec.wait_ge(summed, done(n - 2))
                        vec.tensor_tensor(ch[r % 2][:], hg[r % 3][:], ps_c[:], ALU.mult).then_inc(weighted, 1)

                    for r in range(NR):
                        feed(r, 0)
                        if r >= 2:
                            weight(r - 2, 0)
                        scan(r, 0)
                    with vec.Fori(1, ROUNDS) as j:
                        for r in range(NR):
                            feed(r, j)
                            weight((r - 2) % NR, j if r >= 2 else j - 1)
                            scan(r, j)
                    weight(NR - 2, ROUNDS - 1)
                    weight(NR - 1, ROUNDS - 1)
                    vec.wait_ge(summed, done(pair * DST + DST - 1))
                    vec.scalar_tensor_tensor(y[:], u[p][:], skip[:], ps_y[:], ALU.mult, ALU.add).then_inc(y_step[p], 1)
                    vec.wait_ge(gate_in, past((pair + 1) * 16))
                    vec.wait_ge(y_step[p], past(i + 1))
                    vec.tensor_tensor(y[:], y[:], gate[:], ALU.mult).then_inc(y_done, 1)
                    vec.wait_ge(projected, past(pair + 1))
                    vec.tensor_tensor(rows3(X, pair * (2 * C), 2 * C), rows3(X, pair * (2 * C), 2 * C), ps_o,
                                      ALU.add).then_inc(added, 1)


def add_rows(nc, name, dst, src):
    with ExitStack() as ctx:
        summed = ctx.enter_context(nc.semaphore(f"{name}_summed"))
        block = ctx.enter_context(nc.Block())
        W = 32

        @block.vector
        def _(vec):
            with vec.Fori(0, G // W) as k:
                vec.tensor_tensor(rows3(dst, k * W, W), rows3(dst, k * W, W), rows3(src, k * W, W),
                                  ALU.add).then_inc(summed, 1)


class Stage:

    def __init__(self, nc, ctx, name):
        self.nc, self.ctx, self.name, self.sems = nc, ctx, name, []

    def one(self, name, shape, dt=F32):
        return self.ctx.enter_context(self.nc.sbuf_tensor(f"{self.name}_{name}", shape, dt))

    def two(self, name, shape, dt=F32):
        return [self.one(f"{name}{p}", shape, dt) for p in range(2)]

    def bank(self, name, shape, dt=F32):
        return self.ctx.enter_context(self.nc.psum_tensor(f"{self.name}_{name}", shape, dt))

    def banks(self, name, shape, dt=F32):
        return [self.bank(f"{name}{p}", shape, dt) for p in range(2)]

    def counter(self, name):
        self.sems.append(self.ctx.enter_context(self.nc.semaphore(f"{self.name}_{name}")))
        return self.sems[-1]

    def counters(self, name):
        return [self.counter(f"{name}{p}") for p in range(2)]

    def block(self):
        arm(self.nc, self.sems)
        return self.ctx.enter_context(self.nc.Block())


def fourier_mixer(nc, w, H):
    with ExitStack() as ctx:
        s = Stage(nc, ctx, "fft")
        T = s.one("T", [P, G, D])
        held = s.one("held", [P, G, D])
        gamma, beta = s.one("gamma", [P, D]), s.one("beta", [P, D])
        fc1 = s.one("fc1", [D + 1, FD])
        bn1 = s.one("bn1", [D, FD])
        fc2 = s.one("fc2", [FD, D])
        bn2 = s.one("bn2", [FD, D])
        bias2 = s.one("bias2", [1, D])
        ones = s.one("ones", [1, P])
        wr, wi = s.one("wr", [FD, FD]), s.one("wi", [FD, FD])
        bins_bias = s.one("bins_bias", [P, C, FD])
        dft, idft = s.one("dft", [P, C, L]), s.one("idft", [P, C, L])
        rb = row(w["L0_attn_rb"]).to_broadcast([P, FD])
        ib = row(w["L0_attn_ib"]).to_broadcast([P, FD])
        load(nc, "fft_w", [
            (held[:], w["scr_H"]),
            (gamma[:], spread_row(w["L0_attn_ln2_g"])), (beta[:], spread_row(w["L0_attn_ln2_b"])),
            (fc1[0:D, :], w["L0_attn_fc1_w"]), (fc1[D:D + 1, :], row(w["L0_attn_bn1_b"])),
            (bn1[:], row(w["L0_attn_bn1_s"]).to_broadcast([D, FD])), (fc2[:], w["L0_attn_fc2_w"]),
            (bn2[:], row(w["L0_attn_bn2_s"]).to_broadcast([FD, D])), (bias2[:], row(w["L0_attn_bn2_b"])),
            (wr[:], w["L0_attn_Wr"]), (wi[:], w["L0_attn_Wi"]),
            (bins_bias[:, 0, :], rb), (bins_bias[:, 1, :], rb), (bins_bias[1:P, 2, :], ib[1:P, :]),
            (bins_bias[0:1, 2, :], row(w["L0_attn_rb"])), (bins_bias[:, 3, :], ib),
            (dft[:], w["dft"]), (idft[:], w["idft"])])
        layer_norm(nc, "ln_f", H, T, 1e-3, gamma, beta)
        add_rows(nc, "fft_residual", H, held)

        rowsT = s.two("rowsT", [D + 1, L])
        f = s.two("f", [P, C, FD])
        spec = s.two("spec", [FD, L])
        minus_im = s.two("minus_im", [FD, L // 2])
        real = s.two("real", [FD, L // 2])
        z = s.two("z", [P, C, FD])
        back = s.two("back", [FD, L])
        cur = s.two("cur", [P, C, D])
        ps_a, ps_b = s.banks("ps_a", [P, L]), s.banks("ps_b", [P, L])
        ps_c, ps_d = s.banks("ps_c", [P, C, FD]), s.banks("ps_d", [P, L])
        passed, ready = s.counter("passed"), s.counter("ready")
        cur_ready, turned, rowsT_ready = s.counters("cur_ready"), s.counters("turned"), s.counters("rowsT_ready")
        fc1_done, f_ready, rfft_done = s.counters("fc1_done"), s.counters("f_ready"), s.counters("rfft_done")
        spec_ready, halves_ready, mixed = s.counters("spec_ready"), s.counters("halves_ready"), s.counters("mixed")
        biased, z_ready, irfft_done = s.counters("biased"), s.counters("z_ready"), s.counters("irfft_done")
        back_ready, fc2_done, added = s.counters("back_ready"), s.counters("fc2_done"), s.counters("added")
        block = s.block()

        @block.gpsimd
        def _(pool):
            with pool.Fori(0, SEQS // 2) as i:
                for p in range(2):
                    pool.wait_ge(turned[p], past(i))
                    nc.gpsimd.tensor_copy(cur[p][:], rows3(T, (i * 2 + p) * C, C)).then_inc(cur_ready[p], 1)

        @block.tensor
        def _(pe):
            pe.wait_ge(ready, past(7))
            with pe.Fori(0, SEQS // 2) as i:
                for p in range(2):
                    pe.wait_ge(cur_ready[p], past(i + 1))
                    pe.wait_ge(added[p], past(i))
                    pe.sem_inc(passed, 1)
                    for c in range(C):
                        last = nc.tensor.transpose(ps_a[p][0:D, c * P:(c + 1) * P], cur[p][:, c, :], w["ident"][:])
                    last.then_inc(turned[p], 1)
                for p in range(2):
                    pe.wait_ge(rowsT_ready[p], past(i + 1))
                    for c in range(C):
                        last = nc.tensor.matmul(ps_a[p][:, c * P:(c + 1) * P], rowsT[p][:, c * P:(c + 1) * P], fc1[:],
                                                start=True, stop=True)
                    last.then_inc(fc1_done[p], 1)
                for p in range(2):
                    pe.wait_ge(f_ready[p], past(i + 1))
                    for c in range(C):
                        last = nc.tensor.matmul(ps_b[p][:], f[p][:, c, :], dft[:, c, :], start=(c == 0),
                                                stop=(c == C - 1))
                    last.then_inc(rfft_done[p], 1)
                for p in range(2):
                    pe.wait_ge(spec_ready[p], past(i + 1))
                    pe.wait_ge(halves_ready[p], past(i * 2 + 2))
                    for k in range(C):
                        other = (minus_im, real)[k // 2][p]
                        nc.tensor.matmul(ps_c[p][:, k, :], spec[p][:, k * P:(k + 1) * P], wr[:], start=True, stop=False)
                        last = nc.tensor.matmul(ps_c[p][:, k, :], other[:, k % 2 * P:(k % 2 + 1) * P], wi[:],
                                                start=False, stop=True)
                    last.then_inc(mixed[p], 1)
                for p in range(2):
                    pe.wait_ge(z_ready[p], past(i + 1))
                    for k in range(C):
                        last = nc.tensor.matmul(ps_d[p][:], z[p][:, k, :], idft[:, k, :], start=(k == 0),
                                                stop=(k == C - 1))
                    last.then_inc(irfft_done[p], 1)
                for p in range(2):
                    pe.wait_ge(back_ready[p], past(i + 1))
                    for c in range(C):
                        to = ps_a[p][:, c * D:(c + 1) * D]
                        nc.tensor.matmul(to, back[p][:, c * P:(c + 1) * P], fc2[:], start=True, stop=False)
                        last = nc.tensor.matmul(to, ones[:], bias2[:], start=False, stop=True)
                    last.then_inc(fc2_done[p], 1)

        @block.scalar
        def _(act):
            with act.Fori(0, SEQS // 2) as i:
                for p in range(2):
                    act.wait_ge(fc1_done[p], past(i + 1))
                    nc.scalar.activation(f[p][:].rearrange("p c f -> p (c f)"), ps_a[p][:],
                                         ACT.Relu).then_inc(f_ready[p], 1)
                for p in range(2):
                    act.wait_ge(rfft_done[p], past(i + 1))
                    nc.scalar.activation(spec[p][:], ps_b[p][:], ACT.Copy).then_inc(spec_ready[p], 1)
                for p in range(2):
                    act.wait_ge(biased[p], past(i + 1))
                    nc.scalar.activation(z[p][:], z[p][:], ACT.Relu).then_inc(z_ready[p], 1)
                for p in range(2):
                    act.wait_ge(irfft_done[p], past(i + 1))
                    nc.scalar.activation(back[p][:], ps_d[p][:], ACT.Copy).then_inc(back_ready[p], 1)

        @block.vector
        def _(vec):
            vec.tensor_tensor(fc1[0:D, :], fc1[0:D, :], bn1[:], ALU.mult).then_inc(ready, 1)
            vec.tensor_tensor(fc2[:], fc2[:], bn2[:], ALU.mult).then_inc(ready, 1)
            vec.memset(ones[:], 1.0).then_inc(ready, 1)
            for p in range(2):
                vec.memset(rowsT[p][D:D + 1, :], 1.0).then_inc(ready, 1)
                vec.memset(minus_im[p][:, 0:1], 0.0)
                vec.memset(real[p][:, 0:1], 0.0).then_inc(ready, 1)
            with vec.Fori(0, SEQS // 2) as i:
                for p in range(2):
                    vec.wait_ge(turned[p], past(i + 1))
                    nc.vector.tensor_copy(rowsT[p][0:D, :], ps_a[p][0:D, :]).then_inc(rowsT_ready[p], 1)
                for p in range(2):
                    vec.wait_ge(spec_ready[p], past(i + 1))
                    vec.tensor_scalar(minus_im[p][:, 1:], spec[p][:, L // 2 + 1:], -1.0, None,
                                      ALU.mult).then_inc(halves_ready[p], 1)
                    nc.vector.tensor_copy(real[p][:, 1:], spec[p][:, 1:L // 2]).then_inc(halves_ready[p], 1)
                for p in range(2):
                    vec.wait_ge(mixed[p], past(i + 1))
                    vec.tensor_tensor(z[p][:], ps_c[p][:], bins_bias[:], ALU.add).then_inc(biased[p], 1)
                for p in range(2):
                    vec.wait_ge(fc2_done[p], past(i + 1))
                    g0 = (i * 2 + p) * C
                    vec.tensor_tensor(rows3(H, g0, C), rows3(H, g0, C),
                                      ps_a[p][:, 0:C * D].rearrange("p (c d) -> p c d", d=D),
                                      ALU.add).then_inc(added[p], 1)


def router(nc, w, name, T, xT, route_w, experts):
    with ExitStack() as ctx:
        s = Stage(nc, ctx, f"{name}_route")
        logits = route_w["logits"]
        cur = s.two("cur", [P, C, D])
        xc = s.two("xc", [D + 1, L])
        ps_t = s.banks("ps_t", [D, L])
        ps_l = s.banks("ps_l", [P, C, experts])
        passed, ready = s.counter("passed"), s.counter("ready")
        cur_ready, turned = s.counters("cur_ready"), s.counters("turned")
        kept, copied = s.counters("kept"), s.counters("copied")
        scored, saved = s.counters("scored"), s.counters("saved")
        block = s.block()

        @block.gpsimd
        def _(pool):
            with pool.Fori(0, SEQS // 2) as i:
                for p in range(2):
                    pool.wait_ge(turned[p], past(i))
                    nc.gpsimd.tensor_copy(cur[p][:], rows3(T, (i * 2 + p) * C, C)).then_inc(cur_ready[p], 1)

        @block.tensor
        def _(pe):
            pe.wait_ge(ready, past(3))
            with pe.Fori(0, SEQS // 2) as i:
                for p in range(2):
                    pe.wait_ge(cur_ready[p], past(i + 1))
                    pe.wait_ge(copied[p], past(i))
                    pe.sem_inc(passed, 1)
                    for c in range(C):
                        last = nc.tensor.transpose(ps_t[p][:, c * P:(c + 1) * P], cur[p][:, c, :], w["ident"][:])
                    last.then_inc(turned[p], 1)
                for p in range(2):
                    pe.wait_ge(copied[p], past(i + 1))
                    pe.wait_ge(saved[p], past(i))
                    pe.sem_inc(passed, 1)
                    for c in range(C):
                        last = nc.tensor.matmul(ps_l[p][:, c, :], xc[p][:, c * P:(c + 1) * P], route_w["weights"][:],
                                                start=True, stop=True)
                    last.then_inc(scored[p], 1)

        @block.scalar
        def _(act):
            with act.Fori(0, SEQS // 2) as i:
                for p in range(2):
                    act.wait_ge(copied[p], past(i + 1))
                    act.sem_inc(passed, 1)
                    nc.scalar.activation(xT[0:D, ds((i * 2 + p) * L, L)], xc[p][0:D, :], ACT.Copy).then_inc(kept[p], 1)

        @block.vector
        def _(vec):
            for p in range(2):
                vec.memset(xc[p][D:D + 1, :], 1.0).then_inc(ready, 1)
            vec.memset(xT[D:D + 1, :], 1.0).then_inc(ready, 1)
            with vec.Fori(0, SEQS // 2) as i:
                for p in range(2):
                    vec.wait_ge(turned[p], past(i + 1))
                    vec.wait_ge(scored[p], past(i))
                    vec.wait_ge(kept[p], past(i))
                    nc.vector.tensor_copy(xc[p][0:D, :], ps_t[p][:]).then_inc(copied[p], 1)
                for p in range(2):
                    vec.wait_ge(scored[p], past(i + 1))
                    nc.vector.tensor_copy(logits[:, ds((i * 2 + p) * C, C), :], ps_l[p][:]).then_inc(saved[p], 1)


def top_two(nc, w, name, probs, comb, experts, soften):
    with ExitStack() as ctx:
        def sb(n, shape):
            return ctx.enter_context(nc.sbuf_tensor(f"{name}_{n}", shape, F32))

        pref = sb("pref", [P, experts])
        best, total = sb("best", [P, G]), sb("total", [P, G])
        top = [sb("top0", [P, G]), sb("top1", [P, G])]
        hot = [sb("hot0", [P, G, experts]), sb("hot1", [P, G, experts])]
        rank = sb("rank", [P, G])
        even = sb("even", [P, G])
        load(nc, f"{name}_pref", [(pref[:], row(w["preference"][0:experts]).to_broadcast([P, experts]))])
        made = ctx.enter_context(nc.semaphore(f"{name}_made"))
        powered = ctx.enter_context(nc.semaphore(f"{name}_powered"))
        block = ctx.enter_context(nc.Block())

        def over(stat):
            return stat[:].unsqueeze(2).to_broadcast([P, G, experts])

        first_pass, second_pass = 2, 4

        @block.vector
        def _(vec):
            made_n = Count()

            def tt(out, a, b, op):
                vec.tensor_tensor(out, a, b, op).then_inc(made, made_n.up())
                vec.wait_ge(made, made_n.value)

            def reduced(out, a, op):
                vec.tensor_reduce(out, a, AX.X, op).then_inc(made, made_n.up())
                vec.wait_ge(made, made_n.value)

            def reciprocal(x):
                vec.reciprocal(x, x).then_inc(made, made_n.up())
                vec.wait_ge(made, made_n.value)

            reduced(best[:], probs[:], ALU.max)
            tt(probs[:], probs[:], over(best), ALU.subtract)
            vec.wait_ge(powered, 1)
            reduced(total[:], probs[:], ALU.add)
            reciprocal(total[:])
            tt(probs[:], probs[:], over(total), ALU.mult)
            for k in range(2):
                reduced(top[k][:], probs[:], ALU.max)
                tt(hot[k][:], probs[:], over(top[k]), ALU.is_equal)
                tt(hot[k][:], hot[k][:], pref[:].unsqueeze(1).to_broadcast([P, G, experts]), ALU.mult)
                reduced(rank[:], hot[k][:], ALU.max)
                tt(hot[k][:], hot[k][:], over(rank), ALU.is_equal)
                if k == 0:
                    vec.scalar_tensor_tensor(probs[:], hot[0][:], -2.0, probs[:], ALU.mult,
                                             ALU.add).then_inc(made, made_n.up())
                    vec.wait_ge(made, made_n.value)
            if soften:
                tt(even[:], top[1][:], top[0][:], ALU.subtract)
                vec.sem_inc(powered, 1)
                vec.wait_ge(powered, 3)
                vec.tensor_scalar(total[:], even[:], 1.0, None, ALU.add).then_inc(made, made_n.up())
                vec.wait_ge(made, made_n.value)
                reciprocal(total[:])
                nc.vector.tensor_copy(top[0][:], total[:]).then_inc(made, made_n.up())
                tt(top[1][:], even[:], total[:], ALU.mult)
            else:
                tt(total[:], top[0][:], top[1][:], ALU.add)
                vec.tensor_scalar(total[:], total[:], 1e-12, None, ALU.max).then_inc(made, made_n.up())
                vec.wait_ge(made, made_n.value)
                reciprocal(total[:])
                for k in range(2):
                    tt(top[k][:], top[k][:], total[:], ALU.mult)
            for k in range(2):
                tt(hot[k][:], hot[k][:], over(top[k]), ALU.mult)
            tt(comb[:], hot[0][:], hot[1][:], ALU.add)

        @block.scalar
        def _(act):
            act.wait_ge(made, 2)
            nc.scalar.activation(probs[:], probs[:], ACT.Exp).then_inc(powered, 1)
            if soften:
                act.wait_ge(powered, 2)
                nc.scalar.activation(even[:], even[:], ACT.Exp).then_inc(powered, 1)


def expert_ffn(nc, w, H):
    with ExitStack() as outer:
        xT = outer.enter_context(nc.sbuf_tensor("ffn_xT", [D + 1, SEQS * L], F32))
        comb = outer.enter_context(nc.sbuf_tensor("ffn_comb", [P, G, E0], F32))
        with ExitStack() as ctx:
            T = ctx.enter_context(nc.sbuf_tensor("ffn_T", [P, G, D], F32))
            logits = ctx.enter_context(nc.sbuf_tensor("ffn_logits", [P, G, E0], F32))
            gw = ctx.enter_context(nc.sbuf_tensor("ffn_gw", [D + 1, E0], F32))
            load(nc, "ffn_gate_w", [(gw[0:D, :], w["L0_ffn_gW"]), (gw[D:D + 1, :], row(w["L0_ffn_gb"]))])
            layer_norm(nc, "ln_e", H, T, 1e-5)
            router(nc, w, "ffn", T, xT, {"logits": logits, "weights": gw}, E0)
            top_two(nc, w, "ffn_top", logits, comb, E0, True)

        with ExitStack() as ctx:
            s = Stage(nc, ctx, "ffn")
            ew1 = s.one("ew1", [D, E0, P])
            ew2 = s.one("ew2", [P, E0, D])
            ew3 = s.one("ew3", [P, E0 // 2, D])
            eb1 = s.one("eb1", [P, E0])
            eb2 = s.one("eb2", [P, E0 // 2])
            eb3 = s.one("eb3", [E0 + 1, D])
            sw1, sw2, sw3 = s.one("sw1", [D, P]), s.one("sw2", [D, P]), s.one("sw3", [P, D])
            sb1, sb2 = s.one("sb1", [D, 1]), s.one("sb2", [P, 1])
            pick = s.one("pick", [E0, E0 // 2, P])
            clear(nc, "ffn_sw1", sw1[:, D:])
            load(nc, "ffn_w", [
                (ew1[:], w["L0_ffn_eW1"].rearrange("e f h -> f e h")), (ew2[:], w["L0_ffn_eW2"].rearrange("e h g -> h e g")),
                (ew3[:], w["L0_ffn_eW3"].rearrange("(q a) g o -> (a g) q o", a=2)),
                (eb1[:], w["eb1_columns"]), (eb2[:], w["eb2_columns"]),
                (eb3[0:E0, :], w["L0_ffn_eb3"]), (eb3[E0:E0 + 1, :], row(w["L0_ffn_sb3"])),
                (sw1[:, 0:D], w["L0_ffn_sW1"]), (sw2[:], w["L0_ffn_sW2"]), (sw3[:], w["L0_ffn_sW3"]),
                (sb1[:], column(w["L0_ffn_sb1"])), (sb2[:], column(w["L0_ffn_sb2"])),
                (pick[:], w["pick_pairs"][0:E0, 0:E0 // 2, :])])
            cur = s.two("cur", [P, C, E0])
            gT = s.two("gT", [E0 + 1, L])
            h1 = [s.two(f"h1_{e}", [P, L]) for e in range(2)]
            h2 = [s.two(f"h2_{q}", [P, L]) for q in range(2)]
            s1, s2 = s.two("s1", [D, L]), s.two("s2", [P, L])
            ps_g = s.bank("ps_g", [P, L])
            ps_t = s.bank("ps_t", [E0, L])
            ps_1 = s.banks("ps_1", [P, L])
            ps_2 = s.banks("ps_2", [P, L])
            ps_o = s.banks("ps_o", [P, C, D])
            passed, ready = s.counter("passed"), s.counter("ready")
            cur_ready, turned, gT_ready = s.counters("cur_ready"), s.counters("turned"), s.counters("gT_ready")
            first, first_act = s.counter("first"), s.counter("first_act")
            second, second_act = s.counter("second"), s.counter("second_act")
            spread, gated = s.counter("spread"), s.counter("gated")
            out_done, added = s.counters("out_done"), s.counters("added")
            block = s.block()
            N1, N2 = E0 + 1, E0 // 2 + 1

            @block.gpsimd
            def _(pool):
                with pool.Fori(0, SEQS // 2) as i:
                    for p in range(2):
                        pool.wait_ge(turned[p], past(i))
                        nc.gpsimd.tensor_copy(cur[p][:], comb[:, ds((i * 2 + p) * C, C), :]).then_inc(cur_ready[p], 1)

            @block.tensor
            def _(pe):
                pe.wait_ge(ready, past(2))
                with pe.Fori(0, SEQS // 2) as i:
                    for p in range(2):
                        b = i * 2 + p
                        x = xT[0:D, ds(b * L, L)]
                        pe.wait_ge(cur_ready[p], past(i + 1))
                        pe.wait_ge(gT_ready[1 - p], past(i + p))
                        pe.sem_inc(passed, 1)
                        for c in range(C):
                            last = nc.tensor.transpose(ps_t[:, c * P:(c + 1) * P], cur[p][:, c, :], w["ident"][:])
                        last.then_inc(turned[p], 1)

                        def layer_1(n, weights):
                            k = b * N1 + n
                            pe.wait_ge(first_act, done_1(k - 2))
                            pe.sem_inc(passed, 1)
                            nc.tensor.matmul(ps_1[(p * N1 + n) % 2][:], weights, x, start=True,
                                             stop=True).then_inc(first, 1)

                        def done_1(k):
                            return k + (2 + 1 + 1)

                        def layer_2(n):
                            k = b * N2 + n
                            pe.wait_ge(second_act, done_1(k - 2))
                            to = ps_2[(p * N2 + n) % 2]
                            if n < E0 // 2:
                                pe.wait_ge(first_act, done_1(b * N1 + n * 2 + 1))
                                pe.sem_inc(passed, 1)
                                for a in range(2):
                                    last = nc.tensor.matmul(to[a * D:(a + 1) * D, :], ew2[:, n * 2 + a, :],
                                                            h1[a][(p * N1 + n * 2 + a) // 2 % 2][:], start=True, stop=True)
                            else:
                                pe.wait_ge(first_act, done_1(b * N1 + E0))
                                pe.sem_inc(passed, 1)
                                last = nc.tensor.matmul(to[:], sw2[:], s1[p][:], start=True, stop=True)
                            last.then_inc(second, 1)

                        layer_1(0, ew1[:, 0, :])
                        layer_1(1, ew1[:, 1, :])
                        layer_1(2, ew1[:, 2, :])
                        layer_2(0)
                        layer_1(3, ew1[:, 3, :])
                        layer_1(E0, sw1[:])
                        layer_2(1)
                        pe.wait_ge(gT_ready[p], past(i + 1))
                        for q in range(E0 // 2):
                            pe.wait_ge(gated, done_1(b * 2 + q - 1) - 1)
                            pe.sem_inc(passed, 1)
                            nc.tensor.matmul(ps_g[:], pick[:, q, :], gT[p][0:E0, :], start=True,
                                             stop=True).then_inc(spread, 1)
                            if q == 0:
                                layer_2(2)
                        pe.wait_ge(second_act, done_1(b * N2 + 2))
                        pe.wait_ge(gated, done_1(b * 2 + 1) - 1)
                        pe.wait_ge(added[p], past(i))
                        pe.sem_inc(passed, 1)
                        for c in range(C):
                            at = slice(c * P, (c + 1) * P)
                            for n, (left, right) in enumerate(((h2[0][p][:, at], ew3[:, 0, :]), (h2[1][p][:, at], ew3[:, 1, :]),
                                                              (s2[p][:, at], sw3[:]), (gT[p][:, at], eb3[:]))):
                                last = nc.tensor.matmul(ps_o[p][:, c, :], left, right, start=(n == 0), stop=(n == 3))
                        last.then_inc(out_done[p], 1)

            @block.scalar
            def _(act):
                def done(k):
                    return k + 4

                with act.Fori(0, SEQS // 2) as i:
                    for p in range(2):
                        b = i * 2 + p

                        def act_1(n):
                            k = b * N1 + n
                            act.wait_ge(first, past(k + 1))
                            to, bias = (s1[p], sb1) if n == E0 else (h1[n % 2][(p * N1 + n) // 2 % 2], eb1)
                            m = D if n == E0 else P
                            at = 0 if n == E0 else n
                            nc.scalar.activation(to[:], ps_1[(p * N1 + n) % 2][0:m, :], ACT.Relu,
                                                 bias=bias[:, at:at + 1]).then_inc(first_act, 1)

                        def act_2(n):
                            k = b * N2 + n
                            act.wait_ge(second, past(k + 1))
                            if n == 0:
                                act.wait_ge(out_done[p], past(i))
                            to, bias = (h2[n][p], eb2[:, n:n + 1]) if n < 2 else (s2[p], sb2[:])
                            nc.scalar.activation(to[:], ps_2[(p * N2 + n) % 2][:], ACT.Relu,
                                                 bias=bias).then_inc(second_act, 1)

                        for step, n in ((act_1, 0), (act_1, 1), (act_1, 2), (act_2, 0), (act_1, 3), (act_1, 4),
                                        (act_2, 1), (act_2, 2)):
                            step(n)

            @block.vector
            def _(vec):
                vec.sem_inc(first_act, 2)
                vec.sem_inc(second_act, 2)
                vec.sem_inc(gated, 1)
                for p in range(2):
                    vec.memset(gT[p][:], 1.0).then_inc(ready, 1)
                vec.wait_ge(ready, past(2))
                with vec.Fori(0, SEQS // 2) as i:
                    for p in range(2):
                        b = i * 2 + p
                        vec.wait_ge(turned[p], past(i + 1))
                        vec.wait_ge(out_done[p], past(i))
                        nc.vector.tensor_copy(gT[p][0:E0, :], ps_t[:]).then_inc(gT_ready[p], 1)
                        for q in range(2):
                            vec.wait_ge(spread, past(b * 2 + q + 1))
                            vec.wait_ge(second_act, b * N2 + q + 4)
                            vec.tensor_tensor(h2[q][p][:], h2[q][p][:], ps_g[:], ALU.mult).then_inc(gated, 1)
                        vec.wait_ge(out_done[p], past(i + 1))
                        g0 = b * C
                        vec.tensor_tensor(rows3(H, g0, C), rows3(H, g0, C), ps_o[p][:], ALU.add).then_inc(added[p], 1)


def edge_bias(nc, w, bias_scr):
    W = 2048
    steps = EDGES // W
    with ExitStack() as ctx:
        s = Stage(nc, ctx, "edge")
        target, number = s.two("target", [P, W], I32), s.two("number", [P, W])
        wrapped = s.one("wrapped", [P, W])
        fixed = s.one("fixed", [P, W])
        match = s.two("match", [P, W])
        token = s.one("token", [P, C])
        last_of = s.one("last_of", [P, steps * C])
        last, found = s.one("last", [P, C]), s.one("found", [P, C])
        at = s.one("at", [P, C], I32)
        attr = s.one("attr", [P, C, 3])
        we, be = s.one("we", [P, 3, HEADS]), s.one("be", [P, HEADS])
        value, term = s.one("value", [P, HEADS, C]), s.one("term", [P, HEADS, C])
        parts, rest = s.one("parts", [HEADS * C, 3, P], BF16), s.one("rest", [HEADS * C, P])
        ps_v = s.bank("ps_v", [HEADS * C, P])
        load(nc, "edge_w", [(token[:], w["token_columns"]),
                            (we[:], row(w["L1_attn_We"].rearrange("k h -> (k h)")).to_broadcast([P, 3 * HEADS])
                             .rearrange("p (k h) -> p k h", h=HEADS)),
                            (be[:], spread_row(w["L1_attn_be"]))])
        landed, matched, shrunk = s.counters("landed"), s.counters("matched"), s.counters("shrunk")
        passed, made, used = s.counter("passed"), s.counter("made"), s.counters("used")
        fix_step = s.counter("fix_step")
        turned, high, rest_ready, mid = s.counter("turned"), s.counter("high"), s.counter("rest_ready"), s.counter("mid")
        gathered = w["gathered"][2]
        stored = s.counter("stored")
        block = s.block()
        half = C // 2

        @block.sync
        def _(sp):
            with sp.Fori(0, steps // 2) as i:
                for p in range(2):
                    sp.wait_ge(used[p], past(i))
                    sp.sem_inc(passed, 1)
                    at_edges = ds((i * 2 + p) * W, W)
                    sp.dma_start(target[p][:], w["L1_attn_edge_index"][1:2, at_edges].to_broadcast([P, W])).then_inc(landed[p], 16)
                    sp.dma_start(number[p][:], w["edge_numbers"][0:1, at_edges].to_broadcast([P, W])).then_inc(landed[p], 16)
            sp.wait_ge(made, past(12))
            sp.dma_start(bias_scr.rearrange("a (r p) -> r a p", p=P), parts[:]).then_inc(stored, 16)
            sp.wait_ge(stored, past(16))

        @block.vector
        def _(vec):
            with vec.Fori(0, steps // 2) as i:
                for p in range(2):
                    k = i * 2 + p
                    vec.wait_ge(landed[p], past((i + 1) * 32))
                    vec.wait_ge(matched[0], past(k * half))
                    vec.wait_ge(matched[1], past(k * half))
                    vec.wait_ge(fix_step, past(k * 2))
                    vec.tensor_scalar(wrapped[:], target[p][:], 0.0, float(L), ALU.is_lt, ALU.mult).then_inc(fix_step, 1)
                    vec.wait_ge(fix_step, past(k * 2 + 1))
                    vec.tensor_tensor(fixed[:], target[p][:], wrapped[:], ALU.add).then_inc(fix_step, 1)
                    vec.wait_ge(fix_step, past(k * 2 + 2))
                    for c in range(C):
                        n = k * half + c // 2
                        vec.wait_ge(shrunk[c % 2], past(n))
                        step = vec.scalar_tensor_tensor(match[c % 2][:], fixed[:], token[:, c:c + 1], number[p][:],
                                                        ALU.is_equal, ALU.mult)
                        step.then_inc(matched[c % 2], 1)
                        if c % 2:
                            for q in range(2):
                                vec.wait_ge(matched[q], past(n + 1))
                                done = vec.tensor_reduce(last_of[:, ds(k * C + c - 1 + q, 1)], match[q][:], AX.X, ALU.max)
                                done.then_inc(shrunk[q], 1)
                    for q in range(2):
                        vec.wait_ge(shrunk[q], past((k + 1) * half))
                    vec.sem_inc(used[p], 1)
            n = Count(1)

            def then(step):
                step.then_inc(made, n.up())
                vec.wait_ge(made, n.value)

            then(vec.tensor_reduce(last[:], last_of[:].rearrange("p (k c) -> p c k", c=C), AX.X, ALU.max))
            then(vec.tensor_scalar(found[:], last[:], 0.0, None, ALU.is_gt))
            then(vec.tensor_scalar(at[:], last[:], -1.0, 0.0, ALU.add, ALU.max))
            vec.wait_ge(gathered, 16 * C)

            def attribute(k):
                return attr[:, :, k].unsqueeze(1).to_broadcast([P, HEADS, C])

            def weight(x):
                return x.unsqueeze(2).to_broadcast([P, HEADS, C])

            then(vec.tensor_tensor(value[:], attribute(0), weight(we[:, 0, :]), ALU.mult))
            for k in range(1, 3):
                then(vec.tensor_tensor(term[:], attribute(k), weight(we[:, k, :]), ALU.mult))
                then(vec.tensor_tensor(value[:], value[:], term[:], ALU.add))
            then(vec.tensor_tensor(value[:], value[:], weight(be[:]), ALU.add))
            then(vec.tensor_tensor(value[:], value[:], found[:].unsqueeze(1).to_broadcast([P, HEADS, C]), ALU.mult))
            vec.wait_ge(high, past(1))
            vec.tensor_tensor(rest[:], ps_v[:], parts[:, 0, :], ALU.subtract).then_inc(rest_ready, 1)
            vec.wait_ge(mid, past(1))
            then(vec.tensor_tensor(parts[:, 2, :], rest[:], parts[:, 1, :], ALU.subtract))
            then(vec.memset(found[:], 0.0))

        @block.gpsimd
        def _(pool):
            pool.wait_ge(made, past(3))
            for c in range(C):
                nc.gpsimd.indirect_dma_start(
                    out=attr[:, c, :], out_offset=None, in_=w["L1_attn_edge_attr"],
                    in_offset=bass.IndirectOffsetOnAxis(ap=at[:, c:c + 1], axis=0)).then_inc(gathered, 16)

        @block.tensor
        def _(pe):
            pe.wait_ge(made, past(10))
            nc.tensor.transpose(ps_v[:], value[:].rearrange("p h c -> p (h c)"), w["ident"][:]).then_inc(turned, 1)

        @block.scalar
        def _(act):
            act.wait_ge(turned, past(1))
            nc.scalar.activation(parts[:, 0, :], ps_v[:], ACT.Copy).then_inc(high, 1)
            act.wait_ge(rest_ready, past(1))
            nc.scalar.activation(parts[:, 1, :], rest[:], ACT.Copy).then_inc(mid, 1)


PARTS = 3
CROSS = PARTS * PARTS * HD
BIAS, PEAK = CROSS, CROSS + PARTS
STACK = PEAK + PARTS
QUAD = 4
UNROLL = 3


def edge_attention(nc, w, H):
    bias_scr = nc.dram_tensor("scratch_bias", (PARTS, HEADS * L), BF16).ap()
    peak_scr = nc.dram_tensor("scratch_peak", (PARTS, HEADS * L), BF16).ap()
    rows_scr = nc.dram_tensor("scratch_rows", (P, G, D), F32).ap()
    q_scr = nc.dram_tensor("scratch_q", (PARTS, PARTS, HD, HEADS * L), BF16).ap()
    k_scr = nc.dram_tensor("scratch_k", (PARTS, HD, HEADS * L), BF16).ap()
    edge_bias(nc, w, bias_scr)
    with ExitStack() as ctx:
        T = ctx.enter_context(nc.sbuf_tensor("attn_T", [P, G, D], F32))
        layer_norm(nc, "ln_a", H, T, 1e-5)
        move(nc, "attn_rows", rows_scr, T[:])
    with ExitStack() as ctx:
        s = Stage(nc, ctx, "attn")
        wqk, wv, wo = s.one("wqk", [D + 1, 2 * D]), s.one("wv", [D + 1, D]), s.one("wo", [D + 1, D])
        ks = [s.one(f"ks{m}", [STACK, HEADS, L], BF16) for m in range(UNROLL)]
        qs = [s.one(f"qs{m}", [STACK, HEADS, L], BF16) for m in range(UNROLL)]
        values = [s.one(f"values{m}", [P, C, HEADS, 32]) for m in range(UNROLL)]
        xT, oT = s.one("xT", [D + 1, L]), s.one("oT", [D + 1, L])
        with ExitStack() as zero:
            made = zero.enter_context(nc.semaphore("attn_made"))
            block = zero.enter_context(nc.Block())

            @block.vector
            def _(vec):
                for m in range(UNROLL):
                    vec.memset(ks[m][:], 1.0).then_inc(made, 1)
                vec.memset(xT[D:D + 1, :], 1.0).then_inc(made, 1)
                vec.memset(oT[D:D + 1, :], 1.0).then_inc(made, 1)

            @block.gpsimd
            def _(pool):
                for m in range(UNROLL):
                    pool.memset(qs[m][:], 1.0).then_inc(made, 1)
                for m in range(UNROLL):
                    pool.memset(values[m][:, :, :, 0:HD], 0.0)
                    pool.memset(values[m][:, :, :, HD:HD + 1], 1.0)
                    pool.memset(values[m][:, :, :, HD + 1:], 0.0).then_inc(made, 1)

        load(nc, "attn_w", [
            (wqk[0:D, 0:D], w["wq_columns"]), (wqk[0:D, D:], w["wk_columns"]),
            (wqk[D:D + 1, 0:D], row(w["bq_columns"])), (wqk[D:D + 1, D:], row(w["bk_columns"])),
            (wv[0:D, :], w["L1_attn_Wv"]), (wv[D:D + 1, :], row(w["L1_attn_bv"])),
            (wo[0:D, :], w["L1_attn_Wo"]), (wo[D:D + 1, :], row(w["L1_attn_bo"]))]
            + [(ks[m][BIAS:PEAK, :, :].rearrange("a h t -> a (h t)"), bias_scr) for m in range(UNROLL)])

        cur = s.one("cur", [P, C, D])
        parts, rest = s.one("parts", [P, PARTS, L], BF16), s.one("rest", [P, L])
        peaks = [s.one(f"peaks{m}", [P, HEADS * C]) for m in range(UNROLL)]
        peak_parts = s.one("peak_parts", [HEADS * C, PARTS, P], BF16)
        peak_rest = s.one("peak_rest", [HEADS * C, P])
        probs = s.two("probs", [P, QUAD, C, L])
        o_rows = s.two("o_rows", [P, L])
        share = s.one("share", [P, C, QUAD])
        o_norm = s.one("o_norm", [P, C, 2, QUAD * HD])
        ps_row = s.banks("ps_row", [P, L])
        ps_col = s.banks("ps_col", [P, 2, L])
        ps_o = s.bank("ps_o", [P, L])
        ps_m = s.bank("ps_m", [P, L])
        passed, ready = s.counter("passed"), s.counter("ready")
        cur_in, qk_stored, peak_stored = s.counter("cur_in"), s.counter("qk_stored"), s.counter("peak_stored")
        stack_in = [s.counter(f"stack_in{m}") for m in range(UNROLL)]
        peak_in = [s.counter(f"peak_in{m}") for m in range(UNROLL)]
        turned, x_copied = s.counter("turned"), s.counter("x_copied")
        qk_done, qk_high, qk_rest, qk_mid, qk_low = (s.counter(f"qk_{n}") for n in ("done", "high", "rest", "mid", "low"))
        v_done, v_copied = s.counter("v_done"), s.counter("v_copied")
        row_scored, row_maxed = s.counter("row_scored"), s.counter("row_maxed")
        pk_done, pk_high, pk_rest, pk_mid, pk_low = (s.counter(f"pk_{n}") for n in ("done", "high", "rest", "mid", "low"))
        col_scored, powered = s.counter("col_scored"), s.counter("powered")
        o_done, o_copied, o_turned = s.counter("o_done"), s.counter("o_copied"), s.counter("o_turned")
        shared, normed, n_turned = s.counter("shared"), s.counter("normed"), s.counter("n_turned")
        n_copied, out_done, added = s.counter("n_copied"), s.counter("out_done"), s.counter("added")
        arm(nc, s.sems)
        block = ctx.enter_context(nc.Block())

        ROWS, COLS = HEADS * C, HEADS * C // 2
        STEPS = ROWS // 2
        COL_START = 4
        STACK_DMAS = 1 + PARTS
        FULL = (SEQS - 1 - 2) // UNROLL

        def slots(eng, slot):
            for k in range(-1, 2):
                slot(0, k)
            with eng.Fori(0, FULL) as i:
                for k in range(2, 2 + UNROLL):
                    slot(i, k)
            for k in range(2 + FULL * UNROLL, SEQS + 2):
                slot(0, k)

        def live(i, k):
            return not isinstance(i, int) or 0 <= k < SEQS

        def before(i, k):
            return max(0, min(k, SEQS)) if isinstance(i, int) else i * UNROLL + k

        def through(i, k):
            return before(i, k + 1)

        def round_of(i, k):
            return i + k // UNROLL

        def wait(eng, sem, n):
            if not isinstance(n, int) or n > 0:
                eng.wait_ge(sem, past(n))

        def col_items(step):
            first = max(0, step - COL_START) * 4 // 3
            return range(first, max(0, step + 1 - COL_START) * 4 // 3)

        @block.sync
        def _(sp):
            def fetch(i, k):
                wait(sp, turned, before(i, k))
                sp.sem_inc(passed, 1)
                sp.dma_start(cur[:], rows_scr[:, ds(before(i, k) * C, C), :]).then_inc(cur_in, 16)

            def slot(i, k):
                if live(i, k - 1):
                    m = (k - 1) % UNROLL
                    wait(sp, pk_low, through(i, k - 1))
                    sp.dma_start(peak_scr.rearrange("a (r p) -> r a p", p=P), peak_parts[:]).then_inc(peak_stored, 16)
                    wait(sp, peak_stored, through(i, k - 1) * 16)
                    sp.dma_start(qs[m][PEAK:STACK, :, :].rearrange("a h t -> a (h t)"), peak_scr).then_inc(peak_in[m], 16)
                    wait(sp, peak_in[m], (round_of(i, k - 1) + 1) * 16)
                    sp.sem_inc(passed, 1)
                if live(i, k + 1):
                    m = (k + 1) % UNROLL
                    wait(sp, qk_low, through(i, k + 1))
                    wait(sp, qk_mid, through(i, k + 1))
                    for copy in range(PARTS):
                        sp.dma_start(q_scr[:, copy].rearrange("a c (h t) -> (c h) a t", t=L),
                                     parts[0:D]).then_inc(qk_stored, 16)
                    sp.dma_start(k_scr.rearrange("b c (h t) -> (c h) b t", t=L), parts[D:]).then_inc(qk_stored, 16)
                    wait(sp, qk_stored, through(i, k + 1) * (16 * STACK_DMAS))
                    wait(sp, col_scored, before(i, k - 1) * COLS)
                    sp.sem_inc(passed, 1)
                    sp.dma_start(qs[m][0:CROSS].rearrange("r h t -> r (h t)"),
                                 q_scr.rearrange("a b c x -> (a b c) x")).then_inc(stack_in[m], 16)
                    for copy in range(PARTS):
                        rows = ks[m][copy * PARTS * HD:(copy + 1) * PARTS * HD]
                        sp.dma_start(rows.rearrange("r h t -> r (h t)"),
                                     k_scr.rearrange("b c x -> (b c) x")).then_inc(stack_in[m], 16)
                    if live(i, k + 2):
                        fetch(i, k + 2)
                    wait(sp, stack_in[m], (round_of(i, k + 1) + 1) * (16 * STACK_DMAS))
                    sp.sem_inc(passed, 1)

            fetch(0, 0)
            slots(sp, slot)

        @block.tensor
        def _(pe):
            def row_item(i, k, n):
                m = k % UNROLL
                if n == 0:
                    wait(pe, stack_in[m], (round_of(i, k) + 1) * (16 * STACK_DMAS))
                wait(pe, row_maxed, before(i, k) * ROWS + (n - 1))
                h, c = n // C, n % C
                nc.tensor.matmul(ps_row[n % 2][:], qs[m][0:PEAK, h, c * P:(c + 1) * P], ks[m][0:PEAK, h, :],
                                 start=True, stop=True).then_inc(row_scored, 1)

            def col_item(i, k, n):
                m = k % UNROLL
                if n == 0:
                    wait(pe, peak_in[m], (round_of(i, k) + 1) * 16)
                wait(pe, powered, before(i, k) * COLS + (n - 1))
                h, c = n // 2, n % 2 * 2
                for j in range(2):
                    last = nc.tensor.matmul(ps_col[n % 2][:, j, :], ks[m][:, h, (c + j) * P:(c + j + 1) * P],
                                            qs[m][:, h, :], start=True, stop=True)
                last.then_inc(col_scored, 1)

            def weigh(i, k, quad, c):
                if c == 0:
                    wait(pe, powered, before(i, k) * COLS + (quad + 1) * (COLS // 2))
                    wait(pe, o_copied, before(i, k) * 2 + quad)
                    if quad == 0:
                        wait(pe, v_copied, through(i, k))
                for hh in range(QUAD):
                    last = nc.tensor.matmul(ps_o[32 * hh:32 * hh + 32, :], values[k % UNROLL][:, c, quad * QUAD + hh, :],
                                            probs[quad][:, hh, c, :], start=(c == 0), stop=(c == C - 1))
                if c == C - 1:
                    last.then_inc(o_done, 1)

            def turn_out(i, k, quad):
                wait(pe, o_copied, before(i, k) * 2 + quad + 1)
                pe.sem_inc(passed, 1)
                for c in range(C):
                    last = nc.tensor.transpose(ps_m[:, c * P:(c + 1) * P], o_rows[quad][:, c * P:(c + 1) * P], w["ident"][:])
                last.then_inc(o_turned, 1)

            def slot(i, k):
                for step in range(STEPS):
                    if live(i, k):
                        row_item(i, k, step * 2)
                        row_item(i, k, step * 2 + 1)
                    if step == 0 and live(i, k - 1):
                        wait(pe, row_maxed, before(i, k - 1) * ROWS + ROWS)
                        wait(pe, normed, before(i, k - 2) * 2 + 1 if live(i, k - 2) else 0)
                        pe.sem_inc(passed, 1)
                        nc.tensor.transpose(ps_m[0:ROWS, 0:P], peaks[(k - 1) % UNROLL][:], w["ident"][:]).then_inc(pk_done, 1)
                    if step < C and live(i, k - 2):
                        weigh(i, k - 2, 1, step)
                    if step == 1 and live(i, k + 1):
                        wait(pe, cur_in, through(i, k + 1) * 16)
                        wait(pe, pk_rest, through(i, k - 1))
                        pe.sem_inc(passed, 1)
                        for c in range(C):
                            last = nc.tensor.transpose(ps_m[0:D, c * P:(c + 1) * P], cur[:, c, :], w["ident"][:])
                        last.then_inc(turned, 1)
                    if step == 2 and live(i, k + 1):
                        wait(pe, x_copied, through(i, k + 1))
                        pe.sem_inc(passed, 1)
                        nc.tensor.matmul(ps_m[:], wqk[:], xT[:], start=True, stop=True).then_inc(qk_done, 1)
                    if step == 3 and live(i, k + 1):
                        wait(pe, qk_rest, through(i, k + 1))
                        pe.sem_inc(passed, 1)
                        for c in range(C):
                            last = nc.tensor.matmul(ps_m[:, c * D:(c + 1) * D], xT[:, c * P:(c + 1) * P], wv[:],
                                                    start=True, stop=True)
                        last.then_inc(v_done, 1)
                    if step == 4 and live(i, k - 2):
                        wait(pe, v_copied, through(i, k + 1))
                        wait(pe, normed, before(i, k - 2) * 2 + 1)
                        turn_out(i, k - 2, 1)
                    if step == 6 and live(i, k - 2):
                        wait(pe, normed, through(i, k - 2) * 2)
                        pe.sem_inc(passed, 1)
                        for c in range(C):
                            last = nc.tensor.transpose(ps_m[0:D, c * P:(c + 1) * P],
                                                       o_norm[:, c, :, :].rearrange("p q x -> p (q x)"), w["ident"][:])
                        last.then_inc(n_turned, 1)
                    if step == 8 and live(i, k - 2):
                        wait(pe, n_copied, through(i, k - 2))
                        pe.sem_inc(passed, 1)
                        for c in range(C):
                            last = nc.tensor.matmul(ps_m[:, c * D:(c + 1) * D], oT[:, c * P:(c + 1) * P], wo[:],
                                                    start=True, stop=True)
                        last.then_inc(out_done, 1)
                    if live(i, k - 1):
                        for n in col_items(step):
                            col_item(i, k - 1, n)
                        if 10 <= step < 10 + C:
                            weigh(i, k - 1, 0, step - 10)
                        if step == 14:
                            wait(pe, added, through(i, k - 2))
                            turn_out(i, k - 1, 0)

            wait(pe, ready, 1)
            slots(pe, slot)

        @block.scalar
        def _(act):
            def copy_out(i, k, quad):
                wait(act, o_done, before(i, k) * 2 + quad + 1)
                wait(act, o_turned, before(i, k) * 2 + quad - 1)
                nc.scalar.activation(o_rows[quad][:], ps_o[:], ACT.Copy).then_inc(o_copied, 1)

            def slot(i, k):
                if live(i, k - 1):
                    wait(act, pk_done, through(i, k - 1))
                    wait(act, peak_stored, before(i, k - 1) * 16)
                    nc.scalar.activation(peak_parts[:, 0, :], ps_m[0:ROWS, 0:P], ACT.Copy, scale=-1.0).then_inc(pk_high, 1)
                    wait(act, pk_rest, through(i, k - 1))
                    nc.scalar.activation(peak_parts[:, 1, :], peak_rest[:], ACT.Copy).then_inc(pk_mid, 1)
                if live(i, k + 1):
                    wait(act, qk_done, through(i, k + 1))
                    wait(act, qk_stored, before(i, k + 1) * (16 * STACK_DMAS))
                    nc.scalar.activation(parts[:, 0, :], ps_m[:], ACT.Copy).then_inc(qk_high, 1)
                    wait(act, qk_rest, through(i, k + 1))
                    nc.scalar.activation(parts[:, 1, :], rest[:], ACT.Copy).then_inc(qk_mid, 1)
                if live(i, k - 2):
                    copy_out(i, k - 2, 1)
                if live(i, k - 1):
                    for step in range(STEPS):
                        for n in col_items(step):
                            wait(act, col_scored, before(i, k - 1) * COLS + n + 1)
                            quad, h, c = n // (COLS // 2), n // 2 % QUAD, n % 2 * 2
                            if n % (COLS // 2) == 0:
                                wait(act, o_done, before(i, k - 1) * 2 + quad - 1)
                            nc.scalar.activation(probs[quad][:, h, c:c + 2, :], ps_col[n % 2][:], ACT.Exp).then_inc(powered, 1)
                        if step == 14:
                            copy_out(i, k - 1, 0)

            slots(act, slot)

        @block.vector
        def _(vec):
            def normalise(i, k, quad):
                n = before(i, k) * 2 + quad
                wait(vec, o_turned, n + 1)
                wait(vec, normed, n)
                wait(vec, n_turned, before(i, k))
                o = ps_m[:].rearrange("p (c h x) -> p c h x", c=C, x=32)
                vec.reciprocal(share[:], o[:, :, :, HD]).then_inc(shared, 1)
                wait(vec, shared, n + 1)
                vec.tensor_tensor(o_norm[:, :, quad, :].rearrange("p c (h x) -> p c h x", x=HD), o[:, :, :, 0:HD],
                                  share[:].unsqueeze(3).to_broadcast([P, C, QUAD, HD]), ALU.mult).then_inc(normed, 1)

            def slot(i, k):
                for step in range(STEPS):
                    if live(i, k):
                        for n in (step * 2, step * 2 + 1):
                            wait(vec, row_scored, before(i, k) * ROWS + n + 1)
                            if n == 0:
                                wait(vec, pk_done, before(i, k - 2))
                            vec.tensor_reduce(peaks[k % UNROLL][:, n:n + 1], ps_row[n % 2][:], AX.X,
                                              ALU.max).then_inc(row_maxed, 1)
                    if step == 0 and live(i, k - 1):
                        wait(vec, pk_high, through(i, k - 1))
                        wait(vec, pk_low, before(i, k - 1))
                        vec.scalar_tensor_tensor(peak_rest[:], ps_m[0:ROWS, 0:P], -1.0, peak_parts[:, 0, :], ALU.mult,
                                                 ALU.subtract).then_inc(pk_rest, 1)
                    if step == 1 and live(i, k - 1):
                        wait(vec, pk_mid, through(i, k - 1))
                        vec.tensor_tensor(peak_parts[:, 2, :], peak_rest[:], peak_parts[:, 1, :],
                                          ALU.subtract).then_inc(pk_low, 1)
                    if step == 1 and live(i, k + 1):
                        wait(vec, turned, through(i, k + 1))
                        wait(vec, v_done, before(i, k + 1))
                        nc.vector.tensor_copy(xT[0:D, :], ps_m[0:D, :]).then_inc(x_copied, 1)
                    if step == 2 and live(i, k + 1):
                        wait(vec, qk_high, through(i, k + 1))
                        wait(vec, qk_low, before(i, k + 1))
                        vec.tensor_tensor(rest[:], ps_m[:], parts[:, 0, :], ALU.subtract).then_inc(qk_rest, 1)
                    if step == 3 and live(i, k + 1):
                        wait(vec, qk_mid, through(i, k + 1))
                        vec.tensor_tensor(parts[:, 2, :], rest[:], parts[:, 1, :], ALU.subtract).then_inc(qk_low, 1)
                        wait(vec, v_done, through(i, k + 1))
                        wait(vec, o_done, before(i, k - 2) * 2)
                        nc.vector.tensor_copy(values[(k + 1) % UNROLL][:, :, :, 0:HD],
                                              ps_m[:, 0:C * D].rearrange("p (c h x) -> p c h x", c=C, x=HD)
                                              ).then_inc(v_copied, 1)
                    if live(i, k - 2):
                        if step == 5:
                            normalise(i, k - 2, 1)
                        if step == 7:
                            wait(vec, n_turned, through(i, k - 2))
                            wait(vec, out_done, before(i, k - 2))
                            nc.vector.tensor_copy(oT[0:D, :], ps_m[0:D, :]).then_inc(n_copied, 1)
                        if step == 9:
                            wait(vec, out_done, through(i, k - 2))
                            g0 = before(i, k - 2) * C
                            vec.tensor_tensor(rows3(H, g0, C), rows3(H, g0, C),
                                              ps_m[:, 0:C * D].rearrange("p (c d) -> p c d", d=D), ALU.add).then_inc(added, 1)
                    if step == 15 and live(i, k - 1):
                        normalise(i, k - 1, 0)

            vec.tensor_scalar(wqk[:, 0:D], wqk[:, 0:D], HD ** -0.5, None, ALU.mult).then_inc(ready, 1)
            slots(vec, slot)


def gelu_experts(nc, w, H):
    pairs = E1 // 2
    with ExitStack() as outer:
        xT = outer.enter_context(nc.sbuf_tensor("moe_xT", [D + 1, SEQS * L], F32))
        comb = outer.enter_context(nc.sbuf_tensor("moe_comb", [P, G, E1], F32))
        with ExitStack() as ctx:
            T = ctx.enter_context(nc.sbuf_tensor("moe_T", [P, G, D], F32))
            logits = ctx.enter_context(nc.sbuf_tensor("moe_logits", [P, G, E1], F32))
            route = ctx.enter_context(nc.sbuf_tensor("moe_route", [D + 1, E1], F32))
            clear(nc, "moe_route", route[D:D + 1, :])
            load(nc, "moe_route_w", [(route[0:D, :], w["router_columns"])])
            layer_norm(nc, "ln_m", H, T, 1e-5)
            router(nc, w, "moe", T, xT, {"logits": logits, "weights": route}, E1)
            add_rows(nc, "moe_tokens", H, T)
            top_two(nc, w, "moe_top", logits, comb, E1, False)

        with ExitStack() as ctx:
            s = Stage(nc, ctx, "moe")
            w1 = s.one("w1", [D, E1, D])
            w2 = s.one("w2", [P, pairs, D])
            b1 = s.one("b1", [P, pairs])
            b2 = s.one("b2", [E1, D])
            pick = s.one("pick", [E1, pairs, P])
            load(nc, "moe_w", [
                (w1[:], w["L1_ffn_w1"].rearrange("e f h -> f e h")),
                (w2[:], w["L1_ffn_w2"].rearrange("(q a) g o -> (a g) q o", a=2)),
                (b1[:], w["moe_b1_columns"]), (b2[:], w["L1_ffn_b2"]), (pick[:], w["pick_pairs"])])
            cur = s.two("cur", [P, C, E1])
            gT = s.two("gT", [E1, L])
            h = [s.two(f"h{q}", [P, L]) for q in range(pairs)]
            hg = [s.two(f"hg{q}", [P, L]) for q in range(pairs)]
            ps_t = s.bank("ps_t", [E1, L])
            ps_1, ps_g = s.banks("ps_1", [P, L]), s.banks("ps_g", [P, L])
            ps_o = s.banks("ps_o", [P, C, D])
            passed = s.counter("passed")
            cur_ready, turned, gT_ready = s.counters("cur_ready"), s.counters("turned"), s.counter("gT_ready")
            first, gelus = s.counters("first"), s.counters("gelus")
            spread, gated = s.counters("spread"), s.counters("gated")
            out_done, added = s.counters("out_done"), s.counters("added")
            block = s.block()
            half = pairs // 2

            @block.gpsimd
            def _(pool):
                with pool.Fori(0, SEQS // 2) as i:
                    for p in range(2):
                        pool.wait_ge(turned[p], past(i))
                        nc.gpsimd.tensor_copy(cur[p][:], comb[:, ds((i * 2 + p) * C, C), :]).then_inc(cur_ready[p], 1)

            @block.tensor
            def _(pe):
                with pe.Fori(0, SEQS // 2) as i:
                    for p in range(2):
                        b = i * 2 + p
                        pe.wait_ge(cur_ready[p], past(i + 1))
                        pe.wait_ge(gT_ready, past(b))
                        pe.sem_inc(passed, 1)
                        for c in range(C):
                            last = nc.tensor.transpose(ps_t[:, c * P:(c + 1) * P], cur[p][:, c, :], w["ident"][:])
                        last.then_inc(turned[p], 1)
                        for q in range(pairs):
                            n = b * half + q // 2
                            pe.wait_ge(gelus[q % 2], past(n))
                            pe.sem_inc(passed, 1)
                            nc.tensor.matmul(ps_1[q % 2][:], w1[:, q * 2:q * 2 + 2, :].rearrange("d a h -> d (a h)"),
                                             xT[0:D, ds(b * L, L)], start=True, stop=True).then_inc(first[q % 2], 1)
                            pe.wait_ge(gT_ready, past(b + 1))
                            pe.wait_ge(gated[q % 2], past(n))
                            pe.sem_inc(passed, 1)
                            nc.tensor.matmul(ps_g[q % 2][:], pick[:, q, :], gT[p][:], start=True,
                                             stop=True).then_inc(spread[q % 2], 1)
                    for p in range(2):
                        b = i * 2 + p
                        for q in range(2):
                            pe.wait_ge(gated[q], past(b * half + half))
                        pe.wait_ge(added[p], past(i))
                        pe.sem_inc(passed, 1)
                        for c in range(C):
                            at = slice(c * P, (c + 1) * P)
                            for q in range(pairs):
                                nc.tensor.matmul(ps_o[p][:, c, :], hg[q][p][:, at], w2[:, q, :], start=(q == 0), stop=False)
                            last = nc.tensor.matmul(ps_o[p][:, c, :], gT[p][:, at], b2[:], start=False, stop=True)
                        last.then_inc(out_done[p], 1)

            @block.scalar
            def _(act):
                with act.Fori(0, SEQS // 2) as i:
                    for p in range(2):
                        b = i * 2 + p
                        for q in range(pairs):
                            n = b * half + q // 2
                            act.wait_ge(first[q % 2], past(n + 1))
                            act.wait_ge(gated[q % 2], past(i * (2 * half)) if p == 0 else past(b * half - half))
                            nc.scalar.activation(h[q][p][:], ps_1[q % 2][:], ACT.Gelu, bias=b1[:, q:q + 1]).then_inc(gelus[q % 2], 1)

            @block.vector
            def _(vec):
                with vec.Fori(0, SEQS // 2) as i:
                    for p in range(2):
                        b = i * 2 + p
                        vec.wait_ge(turned[p], past(i + 1))
                        vec.wait_ge(out_done[p], past(i))
                        nc.vector.tensor_copy(gT[p][:], ps_t[:]).then_inc(gT_ready, 1)
                        for q in range(pairs):
                            n = b * half + q // 2
                            vec.wait_ge(spread[q % 2], past(n + 1))
                            vec.wait_ge(gelus[q % 2], past(n + 1))
                            vec.tensor_tensor(hg[q][p][:], h[q][p][:], ps_g[q % 2][:], ALU.mult).then_inc(gated[q % 2], 1)
                    for p in range(2):
                        b = i * 2 + p
                        vec.wait_ge(out_done[p], past(i + 1))
                        vec.tensor_tensor(rows3(H, b * C, C), rows3(H, b * C, C), ps_o[p][:], ALU.add).then_inc(added[p], 1)


def program(nc, w, out):
    with ExitStack() as ctx:
        w["gathered"] = [ctx.enter_context(nc.semaphore(f"gathered{n}")) for n in range(3)]
        ident = ctx.enter_context(nc.sbuf_tensor("ident", [P, P], F32))
        load(nc, "consts", [(ident[:], w["identity"])])
        w["ident"] = ident
        H = ctx.enter_context(nc.sbuf_tensor("H", [P, G, D], F32))
        embed(nc, w, H)
        scr = {n: nc.dram_tensor(f"scratch_{n}", shape, dt).ap() for n, shape, dt in (
            ("H", (P, G, D), F32), ("gate", (DIN, SEQS, L), F32), ("u", (DIN, SEQS, L), F32),
            ("delta", (DIN, SEQS, L), F32), ("bc", (2 * DST, 3, SEQS, L), BF16))}
        move(nc, "spill", scr["H"], H[:])
        mamba_inputs(nc, w, H, H, scr)
        selective_scan(nc, w, H, scr)
        w["scr_H"] = scr["H"]
        renew(nc)
        fourier_mixer(nc, w, H)
        renew(nc)
        expert_ffn(nc, w, H)
        renew(nc)
        edge_attention(nc, w, H)
        renew(nc)
        gelu_experts(nc, w, H)
        with ExitStack() as run:
            written = run.enter_context(nc.semaphore("written"))
            block = run.enter_context(nc.Block())

            @block.sync
            def _(sp):
                sp.dma_start(out.rearrange("b (c p) d -> p (b c) d", p=P), H[:]).then_inc(written, 16)
                sp.wait_ge(written, 16)


def layouts(inputs):
    import numpy as np
    a = {}
    for name, x in inputs.items():
        a[name] = np.ascontiguousarray(np.asarray(x))
    ids = a.pop("x")
    a["ids"] = np.ascontiguousarray(ids.reshape(G, P).T)
    a["table"] = np.concatenate([a.pop("L0_tok_emb_table"), a.pop("L0_tok_geo_table"), a.pop("L0_tok_visit_table")], axis=1)
    a["conv_taps"] = np.ascontiguousarray(a.pop("L0_attn_conv_w").T)
    a["scan_select"] = np.tile(np.repeat(np.eye(NR, dtype=np.float32)[:, :, None], P, axis=2), (3, 1, 1))
    a["eb1_columns"] = np.ascontiguousarray(a.pop("L0_ffn_eb1").T)
    a["eb2_columns"] = np.ascontiguousarray(a.pop("L0_ffn_eb2").reshape(E0 // 2, P).T)
    a["router_columns"] = np.ascontiguousarray(a.pop("L1_ffn_router_w").T)
    a["moe_b1_columns"] = np.ascontiguousarray(a.pop("L1_ffn_b1").reshape(E1 // 2, P).T)
    for n in ("q", "k"):
        a[f"w{n}_columns"] = np.ascontiguousarray(a.pop(f"L1_attn_W{n}").reshape(D, HEADS, HD).transpose(0, 2, 1)).reshape(D, D)
        a[f"b{n}_columns"] = np.ascontiguousarray(a.pop(f"L1_attn_b{n}").reshape(HEADS, HD).T).reshape(D)
    a["token_columns"] = np.ascontiguousarray(np.arange(L, dtype=np.float32).reshape(C, P).T)
    a["edge_numbers"] = np.arange(1, EDGES + 1, dtype=np.float32).reshape(1, EDGES)
    a["preference"] = np.arange(E1, 0, -1, dtype=np.float32)
    a["pick_pairs"] = np.ascontiguousarray(np.repeat(np.eye(E1, dtype=np.float32).reshape(E1, E1 // 2, 2), D, axis=2))
    t = np.arange(L)
    k = np.arange(L // 2 + 1)
    angle = 2 * np.pi / L * (t[:, None] * k[None, :] % L)
    cos, sin = np.cos(angle), np.sin(angle)
    root = L ** 0.5
    forward = np.concatenate([cos, -sin[:, 1:L // 2]], axis=1) / root
    weight = np.where((k == 0) | (k == L // 2), 1.0, 2.0)[:, None] * root / L
    inverse = np.concatenate([(weight * cos.T)[0:L // 2], (weight * cos.T)[L // 2:], -(weight * sin.T)[1:L // 2]])
    a["dft"] = np.ascontiguousarray(forward.reshape(C, P, L).transpose(1, 0, 2).astype(np.float32))
    a["idft"] = np.ascontiguousarray(inverse.reshape(C, P, L).transpose(1, 0, 2).astype(np.float32))
    a["identity"] = np.eye(P, dtype=np.float32)
    return a


def kernel(**inputs):
    import concourse.bacc as _bacc
    from concourse.bass_utils import run_bass_kernel_spmd as _run

    nc = _bacc.Bacc("TRN2", target_bir_lowering=False, num_devices=1)
    arrays = layouts(inputs)
    w = {n: nc.dram_tensor(f"in_{n}", a.shape, mybir.dt.from_np(a.dtype), kind="ExternalInput").ap() for n, a in arrays.items()}
    out = nc.dram_tensor("out", (SEQS, L, D), F32, kind="ExternalOutput").ap()
    program(nc, w, out)
    r = _run(nc, [{f"in_{n}": a for n, a in arrays.items()}], core_ids=[0])
    return r.results[0]["out"]
```

```python
from contextlib import ExitStack

import concourse.bass as bass
from concourse import mybir

F32 = mybir.dt.float32
BF16 = mybir.dt.bfloat16
I32 = mybir.dt.int32
ALU = mybir.AluOpType
ACT = mybir.ActivationFunctionType
AX = mybir.AxisListType

P = 128
SEQS, L, D = 32, 512, 64
C = L // P
G = SEQS * C
ITEMS = 25000
VISIT = 24
ROW = 2 * D + VISIT
DIN, DST, DTR = 128, 48, 4
CONV = 4
FD = 128
HEADS, HD = 8, 8
EDGES = 16384
E0, E1 = 4, 8
ds = bass.ds


class Count:

    def __init__(self, base=0):
        self.base, self.n = base, 0

    def up(self):
        self.n += 1
        return 1

    @property
    def value(self):
        return self.base + self.n


def past(n):
    return n + 1


def arm(nc, sems):
    with nc.Block() as block:
        @block.sync
        def _(sp):
            for s in sems:
                sp.sem_inc(s, 1)


def renew(nc):
    with nc.Block() as block:
        @block.sync
        def _(sp):
            numbers = sorted(nc.released_uncleared_semaphores)
            sp.sem_clear(range(numbers[0], numbers[-1] + 1))


def rows3(tile, g0, n):
    return tile[:, ds(g0, n), :]


def layer_norm(nc, name, src, dst, eps, gamma=None, beta=None):
    W = 16
    steps = G // W
    with ExitStack() as ctx:
        sq = [ctx.enter_context(nc.sbuf_tensor(f"{name}_sq{i}", [P, W, D], F32)) for i in range(2)]
        total = ctx.enter_context(nc.sbuf_tensor(f"{name}_total", [P, G], F32))
        var = ctx.enter_context(nc.sbuf_tensor(f"{name}_var", [P, G], F32))
        rstd = ctx.enter_context(nc.sbuf_tensor(f"{name}_rstd", [P, G], F32))
        eps_col = ctx.enter_context(nc.sbuf_tensor(f"{name}_eps", [P, 1], F32))
        summed = ctx.enter_context(nc.semaphore(f"{name}_summed"))
        centred = ctx.enter_context(nc.semaphore(f"{name}_centred"))
        squared = ctx.enter_context(nc.semaphore(f"{name}_squared"))
        spread = ctx.enter_context(nc.semaphore(f"{name}_spread"))
        rooted = ctx.enter_context(nc.semaphore(f"{name}_rooted"))
        scaled = ctx.enter_context(nc.semaphore(f"{name}_scaled"))
        block = ctx.enter_context(nc.Block())

        def over(stat, g0, n):
            return stat[:, ds(g0, n)].unsqueeze(2).to_broadcast([P, n, D])

        @block.vector
        def _(vec):
            vec.memset(eps_col[:], eps).then_inc(spread, 1)
            with vec.Fori(0, steps // 2) as i:
                for p in range(2):
                    k = i * 2 + p
                    vec.tensor_reduce(total[:, ds(k * W, W)], rows3(src, k * W, W), AX.X, ALU.add).then_inc(summed, 1)
                for p in range(2):
                    k = i * 2 + p
                    vec.wait_ge(summed, k + 1)
                    vec.scalar_tensor_tensor(rows3(dst, k * W, W), over(total, k * W, W), -1.0 / D,
                                             rows3(src, k * W, W), ALU.mult, ALU.add).then_inc(centred, 1)
                for p in range(2):
                    k = i * 2 + p
                    vec.wait_ge(squared, k + 1)
                    vec.tensor_reduce(var[:, ds(k * W, W)], sq[p][:], AX.X, ALU.add).then_inc(spread, 1)
            vec.wait_ge(rooted, 2)
            with vec.Fori(0, steps) as k:
                vec.wait_ge(centred, steps)
                vec.tensor_tensor(rows3(dst, k * W, W), rows3(dst, k * W, W), over(rstd, k * W, W),
                                  ALU.mult).then_inc(scaled, 1)
                if gamma is not None:
                    vec.wait_ge(scaled, k * 3 + 1)
                    vec.tensor_tensor(rows3(dst, k * W, W), rows3(dst, k * W, W),
                                      gamma[:].unsqueeze(1).to_broadcast([P, W, D]), ALU.mult).then_inc(scaled, 1)
                    vec.wait_ge(scaled, k * 3 + 2)
                    vec.tensor_tensor(rows3(dst, k * W, W), rows3(dst, k * W, W),
                                      beta[:].unsqueeze(1).to_broadcast([P, W, D]), ALU.add).then_inc(scaled, 1)

        @block.scalar
        def _(act):
            with act.Fori(0, steps // 2) as i:
                for p in range(2):
                    k = i * 2 + p
                    act.wait_ge(centred, k + 1)
                    act.wait_ge(spread, i * 2 + 1)
                    nc.scalar.activation(sq[p][:], rows3(dst, k * W, W), ACT.Square).then_inc(squared, 1)
            act.wait_ge(spread, steps + 1)
            nc.scalar.activation(rstd[:], var[:], ACT.Ln, scale=1.0 / D, bias=eps_col[:]).then_inc(rooted, 1)
            act.wait_ge(rooted, 1)
            nc.scalar.activation(rstd[:], rstd[:], ACT.Exp, scale=-0.5).then_inc(rooted, 1)


def load(nc, name, pairs, gpsimd_pairs=()):
    with ExitStack() as ctx:
        landed = ctx.enter_context(nc.semaphore(f"{name}_landed"))
        block = ctx.enter_context(nc.Block())

        @block.sync
        def _(sp):
            for dst, src in pairs[::2]:
                sp.dma_start(dst, src).then_inc(landed, 16)
            sp.wait_ge(landed, 16 * len(pairs))

        @block.scalar
        def _(act):
            for dst, src in pairs[1::2]:
                act.dma_start(dst, src).then_inc(landed, 16)


def column(vector):
    return vector.rearrange("(n o) -> n o", o=1)


def row(vector):
    return vector.rearrange("(o n) -> o n", o=1)


def spread_row(vector):
    return row(vector).to_broadcast([P, vector.shape[0]])


def embed(nc, w, H):
    with ExitStack() as ctx:
        def sb(name, shape, dt=F32):
            return ctx.enter_context(nc.sbuf_tensor(name, shape, dt))

        ids = sb("ids", [P, G], I32)
        rows_at = sb("rows_at", [P, G], I32)
        keep = sb("keep", [P, G])
        emb = sb("emb", [P, G, D])
        w_pair = sb("w_pair", [P, P])
        w_visit = sb("w_visit", [VISIT, D])
        b_pair = sb("b_pair", [P, 1])
        b_visit = sb("b_visit", [D, 1])
        fuse_a = sb("fuse_a", [P, D])
        fuse_b = sb("fuse_b", [D + 1, D])
        gamma = sb("tok_gamma", [P, D])
        beta = sb("tok_beta", [P, D])
        at = [sb(f"at{p}", [P, C], I32) for p in range(2)]
        rows = [sb(f"rows{p}", [P, C, ROW]) for p in range(2)]
        pairT = sb("pairT", [P, L])
        visitT = sb("visitT", [VISIT, L])
        pair_h = sb("pair_h", [P, L])
        visit_h = sb("visit_h", [D + 1, L])

        with ExitStack() as zero:
            zeroed = zero.enter_context(nc.semaphore("tok_zeroed"))
            block = zero.enter_context(nc.Block())

            @block.vector
            def _(vec):
                vec.memset(w_pair[:], 0.0).then_inc(zeroed, 1)
                vec.memset(visit_h[D:D + 1, :], 1.0).then_inc(zeroed, 1)

        load(nc, "tok_w", [
            (ids[:], w["ids"]), (w_pair[0:D, 0:D], w["L0_tok_w_item"]), (w_pair[D:P, D:P], w["L0_tok_w_geo"]),
            (w_visit[:], w["L0_tok_w_visit"]), (b_pair[0:D, :], column(w["L0_tok_b_item"])),
            (b_pair[D:P, :], column(w["L0_tok_b_geo"])), (b_visit[:], column(w["L0_tok_b_visit"])),
            (fuse_a[:], w["L0_tok_w_fuse"][0:P, :]), (fuse_b[0:D, :], w["L0_tok_w_fuse"][P:P + D, :]),
            (fuse_b[D:D + 1, :], row(w["L0_tok_b_fuse"])),
            (gamma[:], spread_row(w["L0_tok_ln_gamma"])), (beta[:], spread_row(w["L0_tok_ln_beta"]))])

        with ExitStack() as run:
            sems = []

            def sem(name):
                sems.append(run.enter_context(nc.semaphore(name)))
                return sems[-1]

            ps_pair = run.enter_context(nc.psum_tensor("ps_pair", [P, L], F32))
            ps_visit = run.enter_context(nc.psum_tensor("ps_visit", [VISIT, L], F32))
            ps_ph = run.enter_context(nc.psum_tensor("ps_ph", [P, L], F32))
            ps_vh = run.enter_context(nc.psum_tensor("ps_vh", [D, L], F32))
            ps_fuse = run.enter_context(nc.psum_tensor("ps_fuse", [P, C, D], F32))
            passed, ids_ready, at_ready = sem("tok_passed"), sem("ids_ready"), sem("at_ready")
            gathered = w["gathered"][0:2]
            turned = [sem(f"turned{p}") for p in range(2)]
            emb_kept = [sem(f"emb_kept{p}") for p in range(2)]
            pair_copied, visit_copied = sem("pair_copied"), sem("visit_copied")
            projected, gelus, fused, stored = sem("projected"), sem("gelus"), sem("fused"), sem("stored")
            arm(nc, sems)
            block = run.enter_context(nc.Block())

            @block.gpsimd
            def _(pool):
                pool.wait_ge(ids_ready, past(1))
                with pool.Fori(0, SEQS // 2) as i:
                    for p in range(2):
                        b = i * 2 + p
                        pool.wait_ge(turned[p], past(i))
                        pool.wait_ge(emb_kept[p], past(i))
                        nc.gpsimd.tensor_copy(at[p][:], rows_at[:, ds(b * C, C)]).then_inc(at_ready, 1)
                        pool.wait_ge(at_ready, past(b + 1))
                        pool.sem_inc(passed, 1)
                        for c in range(C):
                            nc.gpsimd.indirect_dma_start(
                                out=rows[p][:, c, :], out_offset=None, in_=w["table"],
                                in_offset=bass.IndirectOffsetOnAxis(ap=at[p][:, c:c + 1], axis=0),
                            ).then_inc(gathered[p], 16)

            @block.tensor
            def _(pe):
                with pe.Fori(0, SEQS // 2) as i:
                    for p in range(2):
                        b = i * 2 + p
                        pe.wait_ge(gathered[p], i * (16 * C) + 16 * C)
                        pe.wait_ge(pair_copied, past(b))
                        pe.wait_ge(visit_copied, past(b))
                        pe.sem_inc(passed, 1)
                        for c in range(C):
                            nc.tensor.transpose(ps_pair[:, c * P:(c + 1) * P], rows[p][:, c, 0:P], w["ident"][:])
                        for c in range(C):
                            last = nc.tensor.transpose(ps_visit[:, c * P:(c + 1) * P], rows[p][:, c, P:ROW],
                                                       w["ident"][:])
                        last.then_inc(turned[p], 1)
                        pe.wait_ge(pair_copied, past(b + 1))
                        pe.wait_ge(gelus, past(b))
                        nc.tensor.matmul(ps_ph[:], w_pair[:], pairT[:], start=True, stop=True)
                        pe.wait_ge(visit_copied, past(b + 1))
                        nc.tensor.matmul(ps_vh[:], w_visit[:], visitT[:], start=True, stop=True).then_inc(projected, 1)
                        pe.wait_ge(gelus, past(b + 1))
                        pe.wait_ge(stored, past(b))
                        pe.sem_inc(passed, 1)
                        for c in range(C):
                            nc.tensor.matmul(ps_fuse[:, c, :], pair_h[:, c * P:(c + 1) * P], fuse_a[:],
                                             start=True, stop=False)
                            last = nc.tensor.matmul(ps_fuse[:, c, :], visit_h[:, c * P:(c + 1) * P], fuse_b[:],
                                                    start=False, stop=True)
                        last.then_inc(fused, 1)

            @block.vector
            def _(vec):
                vec.tensor_scalar(rows_at[:], ids[:], 0.0, float(ITEMS), ALU.max, ALU.min).then_inc(ids_ready, 1)
                vec.tensor_scalar(keep[:], ids[:], 0.0, 0.1, ALU.not_equal, ALU.mult).then_inc(ids_ready, 1)
                with vec.Fori(0, SEQS // 2) as i:
                    for p in range(2):
                        b = i * 2 + p
                        vec.wait_ge(turned[p], past(i + 1))
                        nc.vector.tensor_copy(pairT[:], ps_pair[:]).then_inc(pair_copied, 1)
                        nc.vector.tensor_copy(rows3(emb, b * C, C), rows[p][:, :, 0:D]).then_inc(emb_kept[p], 1)

            @block.scalar
            def _(act):
                with act.Fori(0, SEQS // 2) as i:
                    for p in range(2):
                        b = i * 2 + p
                        act.wait_ge(turned[p], past(i + 1))
                        nc.scalar.activation(visitT[:], ps_visit[:], ACT.Copy).then_inc(visit_copied, 1)
                        act.wait_ge(projected, past(b + 1))
                        act.wait_ge(fused, past(b))
                        nc.scalar.activation(pair_h[:], ps_ph[:], ACT.Gelu, bias=b_pair[:])
                        nc.scalar.activation(visit_h[0:D, :], ps_vh[:], ACT.Gelu, bias=b_visit[:]).then_inc(gelus, 1)
                        act.wait_ge(fused, past(b + 1))
                        act.sem_inc(passed, 1)
                        nc.scalar.activation(rows3(H, b * C, C), ps_fuse[:], ACT.Gelu).then_inc(stored, 1)

        layer_norm(nc, "tok_ln", H, H, 1e-5, gamma, beta)

        with ExitStack() as run:
            masked = run.enter_context(nc.semaphore("tok_masked"))
            block = run.enter_context(nc.Block())

            @block.vector
            def _(vec):
                W = 16
                with vec.Fori(0, G // W) as k:
                    vec.tensor_tensor(rows3(H, k * W, W), rows3(H, k * W, W),
                                      keep[:, ds(k * W, W)].unsqueeze(2).to_broadcast([P, W, D]),
                                      ALU.mult).then_inc(masked, 1)
                    vec.wait_ge(masked, k * 2 + 1)
                    vec.tensor_tensor(rows3(H, k * W, W), rows3(H, k * W, W), rows3(emb, k * W, W),
                                      ALU.add).then_inc(masked, 1)


def move(nc, name, dst, src):
    with ExitStack() as ctx:
        moved = ctx.enter_context(nc.semaphore(f"{name}_moved"))
        block = ctx.enter_context(nc.Block())

        @block.sync
        def _(sp):
            sp.dma_start(dst, src).then_inc(moved, 16)
            sp.wait_ge(moved, 16)


def clear(nc, name, tile):
    with ExitStack() as ctx:
        cleared = ctx.enter_context(nc.semaphore(f"{name}_cleared"))
        block = ctx.enter_context(nc.Block())

        @block.vector
        def _(vec):
            vec.memset(tile, 0.0).then_inc(cleared, 1)


def mamba_inputs(nc, w, H, X, scr):
    with ExitStack() as ctx:
        def sb(name, shape, dt=F32):
            return ctx.enter_context(nc.sbuf_tensor(name, shape, dt))

        T = sb("pre_T", [P, G, D])
        norms = [sb(f"pre_{n}", [P, D]) for n in ("g1", "b1", "g2", "b2")]
        w_in = sb("pre_w_in", [D, 2 * DIN])
        w_bc = sb("pre_w_bc", [DIN, 2 * DST])
        w_dtin = sb("pre_w_dtin", [DIN, DTR])
        w_dt = sb("pre_w_dt", [DTR, DIN])
        taps = sb("pre_taps", [DIN, CONV])
        conv_b = sb("pre_conv_b", [DIN, 1])
        dt_b = sb("pre_dt_b", [DIN, 1])
        load(nc, "pre_w", [
            (norms[0][:], spread_row(w["L0_attn_ln1_g"])), (norms[1][:], spread_row(w["L0_attn_ln1_b"])),
            (norms[2][:], spread_row(w["L0_attn_mln_g"])), (norms[3][:], spread_row(w["L0_attn_mln_b"])),
            (w_in[:], w["L0_attn_w_in"]), (w_bc[:], w["L0_attn_w_xproj"][:, DTR:]),
            (w_dtin[:], w["L0_attn_w_xproj"][:, 0:DTR]), (w_dt[:], w["L0_attn_w_dt"]),
            (taps[:], w["conv_taps"]), (conv_b[:], column(w["L0_attn_conv_b"])),
            (dt_b[:], column(w["L0_attn_b_dt"]))])
        layer_norm(nc, "ln_x", H, X, 1e-5)
        layer_norm(nc, "ln_1", X, T, 1e-3, norms[0], norms[1])
        layer_norm(nc, "ln_2", T, T, 1e-3, norms[2], norms[3])

        sems = []

        def sem(name):
            sems.append(ctx.enter_context(nc.semaphore(name)))
            return sems[-1]

        cur = [sb(f"pre_cur{p}", [P, C, D]) for p in range(2)]
        mT = sb("pre_mT", [D, L])
        conv = sb("pre_conv", [DIN, L])
        u = [sb(f"pre_u{p}", [DIN, L]) for p in range(2)]
        gate = [sb(f"pre_gate{p}", [DIN, L]) for p in range(2)]
        delta = [sb(f"pre_delta{p}", [DIN, L]) for p in range(2)]
        parts = [sb(f"pre_parts{p}", [2 * DST, 3, L], BF16) for p in range(2)]
        rest = sb("pre_rest", [2 * DST, L])
        dts = sb("pre_dts", [DTR, L])
        size = sb("pre_size", [DIN, L])
        soft = sb("pre_soft", [DIN, L])
        ps_m = ctx.enter_context(nc.psum_tensor("ps_m", [D, L], F32))
        ps_xm = ctx.enter_context(nc.psum_tensor("ps_xm", [DIN, L], F32))
        ps_res = ctx.enter_context(nc.psum_tensor("ps_res", [DIN, L], F32))
        ps_bc = ctx.enter_context(nc.psum_tensor("ps_bc", [2 * DST, L], F32))
        ps_dt = ctx.enter_context(nc.psum_tensor("ps_dt", [DTR, L], F32))
        ps_delta = ctx.enter_context(nc.psum_tensor("ps_delta", [DIN, L], F32))
        cur_ready = [sem(f"pre_cur_ready{p}") for p in range(2)]
        turned = [sem(f"pre_turned{p}") for p in range(2)]
        passed, m_copied, projected, convolved = sem("pre_passed"), sem("pre_m_copied"), sem("pre_projected"), sem("pre_convolved")
        tap_done, gated, u_ready = sem("pre_tap_done"), sem("pre_gated"), sem("pre_u_ready")
        xdbl, dt_copied, dt_spread = sem("pre_xdbl"), sem("pre_dt_copied"), sem("pre_dt_spread")
        soft_step, softened, delta_ready = sem("pre_soft_step"), sem("pre_softened"), sem("pre_delta_ready")
        soft_max = sem("pre_soft_max")
        high, mid, split, rest_ready = sem("pre_high"), sem("pre_mid"), sem("pre_split"), sem("pre_rest_ready")
        saved = [sem(f"pre_saved{p}") for p in range(2)]
        arm(nc, sems)
        block = ctx.enter_context(nc.Block())
        SAVES = 4

        @block.gpsimd
        def _(pool):
            with pool.Fori(0, SEQS // 2) as i:
                for p in range(2):
                    pool.wait_ge(turned[p], past(i))
                    nc.gpsimd.tensor_copy(cur[p][:], rows3(T, (i * 2 + p) * C, C)).then_inc(cur_ready[p], 1)

        @block.tensor
        def _(pe):
            with pe.Fori(0, SEQS // 2) as i:
                for p in range(2):
                    b = i * 2 + p
                    pe.wait_ge(cur_ready[p], past(i + 1))
                    pe.wait_ge(m_copied, past(b))
                    pe.sem_inc(passed, 1)
                    for c in range(C):
                        last = nc.tensor.transpose(ps_m[:, c * P:(c + 1) * P], cur[p][:, c, :], w["ident"][:])
                    last.then_inc(turned[p], 1)
                    pe.wait_ge(m_copied, past(b + 1))
                    pe.wait_ge(convolved, past(b))
                    pe.wait_ge(gated, past(b))
                    nc.tensor.matmul(ps_xm[:], w_in[:, 0:DIN], mT[:], start=True, stop=True)
                    nc.tensor.matmul(ps_res[:], w_in[:, DIN:], mT[:], start=True, stop=True).then_inc(projected, 1)
                    pe.wait_ge(u_ready, past(b + 1))
                    pe.wait_ge(dt_copied, past(b))
                    pe.wait_ge(split, past(b))
                    nc.tensor.matmul(ps_dt[:], w_dtin[:], u[p][:], start=True, stop=True)
                    nc.tensor.matmul(ps_bc[:], w_bc[:], u[p][:], start=True, stop=True).then_inc(xdbl, 1)
                    pe.wait_ge(dt_copied, past(b + 1))
                    pe.wait_ge(delta_ready, past(b))
                    nc.tensor.matmul(ps_delta[:], w_dt[:], dts[:], start=True, stop=True).then_inc(dt_spread, 1)

        @block.vector
        def _(vec):
            with vec.Fori(0, SEQS // 2) as i:
                for p in range(2):
                    b = i * 2 + p
                    vec.wait_ge(turned[p], past(i + 1))
                    nc.vector.tensor_copy(mT[:], ps_m[:]).then_inc(m_copied, 1)
                    vec.wait_ge(projected, past(b + 1))
                    vec.wait_ge(u_ready, past(b))
                    step = Count(b * (CONV - 1))
                    vec.tensor_scalar(conv[:], ps_xm[:], taps[:, CONV - 1:CONV], None,
                                      ALU.mult).then_inc(tap_done, step.up())
                    for k in range(CONV - 2, -1, -1):
                        lag = CONV - 1 - k
                        vec.wait_ge(tap_done, past(step.value))
                        done = vec.scalar_tensor_tensor(conv[:, lag:], ps_xm[:, 0:L - lag], taps[:, k:k + 1],
                                                        conv[:, lag:], ALU.mult, ALU.add)
                        if k:
                            done.then_inc(tap_done, step.up())
                        else:
                            done.then_inc(convolved, 1)
                    vec.wait_ge(xdbl, past(b + 1))
                    nc.vector.tensor_copy(dts[:], ps_dt[:]).then_inc(dt_copied, 1)
                    vec.wait_ge(high, past(b + 1))
                    vec.tensor_tensor(rest[:], ps_bc[:], parts[p][:, 0, :], ALU.subtract).then_inc(rest_ready, 1)
                    vec.wait_ge(mid, past(b + 1))
                    vec.tensor_tensor(parts[p][:, 2, :], rest[:], parts[p][:, 1, :], ALU.subtract).then_inc(split, 1)
                    vec.wait_ge(softened, past(b + 1))
                    vec.wait_ge(saved[p], past(i * (16 * SAVES)))
                    vec.tensor_scalar(size[:], ps_delta[:], dt_b[:], 0.0, ALU.add, ALU.max).then_inc(soft_max, 1)
                    vec.wait_ge(soft_max, past(b + 1))
                    vec.tensor_tensor(delta[p][:], size[:], soft[:], ALU.add).then_inc(delta_ready, 1)

        @block.scalar
        def _(act):
            with act.Fori(0, SEQS // 2) as i:
                for p in range(2):
                    b = i * 2 + p
                    act.wait_ge(projected, past(b + 1))
                    act.wait_ge(saved[p], past(i * (16 * SAVES)))
                    nc.scalar.activation(gate[p][:], ps_res[:], ACT.Silu).then_inc(gated, 1)
                    act.wait_ge(convolved, past(b + 1))
                    nc.scalar.activation(u[p][:], conv[:], ACT.Silu, bias=conv_b[:]).then_inc(u_ready, 1)
                    act.wait_ge(xdbl, past(b + 1))
                    nc.scalar.activation(parts[p][:, 0, :], ps_bc[:], ACT.Copy).then_inc(high, 1)
                    act.wait_ge(rest_ready, past(b + 1))
                    nc.scalar.activation(parts[p][:, 1, :], rest[:], ACT.Copy).then_inc(mid, 1)
                    act.wait_ge(dt_spread, past(b + 1))
                    act.wait_ge(delta_ready, past(b))
                    step = Count(b * 2)
                    nc.scalar.activation(soft[:], ps_delta[:], ACT.Abs, bias=dt_b[:]).then_inc(soft_step, step.up())
                    act.wait_ge(soft_step, past(step.value))
                    nc.scalar.activation(soft[:], soft[:], ACT.Exp, scale=-1.0).then_inc(soft_step, step.up())
                    act.wait_ge(soft_step, past(step.value))
                    nc.scalar.activation(soft[:], soft[:], ACT.Ln, bias=1.0).then_inc(softened, 1)

        @block.sync
        def _(sp):
            with sp.Fori(0, SEQS // 2) as i:
                for p in range(2):
                    b = i * 2 + p
                    sp.wait_ge(gated, past(b + 1))
                    sp.dma_start(scr["gate"][:, ds(b, 1), :], gate[p][:].unsqueeze(1)).then_inc(saved[p], 16)
                    sp.wait_ge(u_ready, past(b + 1))
                    sp.dma_start(scr["u"][:, ds(b, 1), :], u[p][:].unsqueeze(1)).then_inc(saved[p], 16)
                    sp.wait_ge(split, past(b + 1))
                    sp.sem_inc(passed, 1)
                    sp.dma_start(scr["bc"][:, :, ds(b, 1), :], parts[p][:].unsqueeze(2)).then_inc(saved[p], 16)
                    sp.wait_ge(delta_ready, past(b + 1))
                    sp.dma_start(scr["delta"][:, ds(b, 1), :], delta[p][:].unsqueeze(1)).then_inc(saved[p], 16)
            for p in range(2):
                sp.wait_ge(saved[p], past(16 * SAVES * (SEQS // 2)))


NR = 12
ROUNDS = DST // NR
PAIRS = SEQS // 2
AHEAD = 8
LOG_EPS = -27.631021115928547


def selective_scan(nc, w, X, scr):
    with ExitStack() as ctx:
        def sb(name, shape, dt=F32):
            return ctx.enter_context(nc.sbuf_tensor(name, shape, dt))

        sems = []

        def sem(name):
            sems.append(ctx.enter_context(nc.semaphore(name)))
            return sems[-1]

        A = sb("A", [DIN, DST])
        skip = sb("skip", [DIN, 1])
        w_out = sb("w_out", [DIN, D])
        sel_f = sb("sel_f", [3 * NR, NR, P])
        sel = sb("sel", [3 * NR, NR, P], BF16)
        ones = sb("scan_ones", [P, L])
        bias = sb("scan_bias", [P, 1])
        load(nc, "scan_w", [(A[:], w["L0_attn_A_log"]), (skip[:], column(w["L0_attn_D"])),
                            (w_out[:], w["L0_attn_w_out"]), (sel_f[:], w["scan_select"])])
        T2 = 2 * L
        delta = [sb(f"delta{p}", [DIN, 2, L]) for p in range(2)]
        u = [sb(f"u{p}", [DIN, 2, L]) for p in range(2)]
        gate = sb("gate", [DIN, 2, L])
        bc = [sb(f"bc{p}", [3 * NR, 2 * ROUNDS, 2, L], BF16) for p in range(2)]
        du = sb("du", [DIN, 2, L])
        after = sb("after", [DIN, 2, L])
        GA = 3
        decay = [sb(f"decay{k}", [DIN, 2, L]) for k in range(2 * GA)]
        guard = [sb(f"guard{k}", [DIN, 2, L]) for k in range(2 * GA)]
        h = [sb(f"h{k}", [DIN, 2, L]) for k in range(2)]
        hg = [sb(f"hg{k}", [DIN, 2, L]) for k in range(3)]
        ch = [sb(f"ch{k}", [DIN, 2, L]) for k in range(2)]
        y = sb("y", [DIN, 2, L])
        ps_b = [ctx.enter_context(nc.psum_tensor(f"ps_b{k}", [DIN, 2, L], F32)) for k in range(2)]
        ps_c = ctx.enter_context(nc.psum_tensor("ps_c", [DIN, 2, L], F32))
        ps_y = ctx.enter_context(nc.psum_tensor("ps_y", [DIN, 2, L], F32))
        ps_o = ps_c[:, 0, :].rearrange("p (g d) -> p g d", d=D)

        passed, a_step = sem("scan_passed"), sem("a_step")
        loaded = [sem(f"scan_loaded{p}") for p in range(2)]
        gate_in = sem("gate_in")
        y_step = [sem(f"y_step{p}") for p in range(2)]
        prepared, b_ready, c_ready = sem("prepared"), sem("b_ready"), sem("c_ready")
        decayed, guarded, fed = sem("decayed"), sem("guarded"), sem("fed")
        scanned, multiplied, weighted, summed = sem("scanned"), sem("multiplied"), sem("weighted"), sem("h_summed")
        y_done, projected, added = sem("y_done"), sem("out_projected"), sem("x_added")
        arm(nc, sems)
        block = ctx.enter_context(nc.Block())

        def done(n):
            return past(n + (AHEAD + 1))

        LOADS = 2 + 6
        @block.sync
        def _(sp):
            with sp.Fori(0, PAIRS // 2) as i:
                for p in range(2):
                    pair = i * 2 + p
                    sp.wait_ge(y_step[p], past(i))
                    sp.dma_start(delta[p][:], scr["delta"][:, ds(pair * 2, 2), :]).then_inc(loaded[p], 16)
                    sp.dma_start(u[p][:], scr["u"][:, ds(pair * 2, 2), :]).then_inc(loaded[p], 16)
                    for part in range(3):
                        for half in range(2):
                            src = scr["bc"][half * DST:(half + 1) * DST, part, ds(pair * 2, 2), :]
                            sp.dma_start(bc[p][part * NR:(part + 1) * NR, half * ROUNDS:(half + 1) * ROUNDS],
                                         src.rearrange("(j r) s t -> r j (s t)", r=NR)
                                         .rearrange("r j (s t) -> r j s t", s=2)).then_inc(loaded[p], 16)
                    sp.wait_ge(y_done, past(pair))
                    sp.dma_start(gate[:], scr["gate"][:, ds(pair * 2, 2), :]).then_inc(gate_in, 16)

        @block.tensor
        def _(pe):
            def spread(dst, p, r, j, half):
                for s in range(2):
                    last = nc.tensor.matmul(dst[:, s, :], sel[:, r, :], bc[p][:, ds(half * ROUNDS + j, 1), s, :],
                                            start=True, stop=True)
                return last

            pe.sem_inc(b_ready, AHEAD)
            pe.sem_inc(c_ready, AHEAD)
            pe.sem_inc(summed, AHEAD)
            pe.wait_ge(a_step, past(7))
            with pe.Fori(0, PAIRS // 2) as i:
                for p in range(2):
                    pair = i * 2 + p
                    pe.wait_ge(loaded[p], past(i * (16 * LOADS) + 16 * LOADS))

                    def b_item(r, j):
                        pe.wait_ge(scanned, done(pair * DST + j * NR + r - 2))
                        pe.sem_inc(passed, 1)
                        spread(ps_b[r % 2], p, r, j, 0).then_inc(b_ready, 1)

                    def c_item(r, j):
                        n = pair * DST + j * NR + r
                        pe.wait_ge(weighted, done(n - 1))
                        pe.sem_inc(passed, 1)
                        spread(ps_c, p, r, j, 1).then_inc(c_ready, 1)

                    def y_item(r, j, first=False, final=False):
                        n = pair * DST + j * NR + r
                        pe.wait_ge(weighted, done(n))
                        for s in range(2):
                            last = nc.tensor.matmul(ps_y[:, s, :], w["ident"][:], ch[r % 2][:, s, :],
                                                    start=first, stop=final)
                        last.then_inc(summed, 1)

                    def step(r, j, peeled=False):
                        if r < NR - 1:
                            b_item(r + 1, j)
                        elif peeled or j is not None:
                            b_next(j)
                        if not (peeled and r < 1):
                            c_item((r - 1) % NR, j if r >= 1 else j - 1)
                        if not (peeled and r < 2):
                            y_item((r - 2) % NR, j if r >= 2 else j - 1, first=peeled and r == 2)

                    def b_next(j):
                        b_item(0, j + 1)

                    pe.wait_ge(added, past(pair))
                    b_item(0, 0)
                    for r in range(NR):
                        step(r, 0, peeled=True)
                    with pe.Fori(1, ROUNDS - 1) as j:
                        for r in range(NR):
                            step(r, j)
                    for r in range(NR):
                        j = ROUNDS - 1
                        if r < NR - 1:
                            b_item(r + 1, j)
                        c_item((r - 1) % NR, j if r >= 1 else j - 1)
                        y_item((r - 2) % NR, j if r >= 2 else j - 1)
                    j = ROUNDS - 1
                    c_item(NR - 1, j)
                    y_item(NR - 2, j)
                    y_item(NR - 1, j, final=True)
                    pe.wait_ge(y_done, past(pair + 1))
                    for g in range(2 * C):
                        last = nc.tensor.matmul(ps_o[:, g, :], y[:, g // C, (g % C) * P:(g % C + 1) * P], w_out[:],
                                                start=True, stop=True)
                    last.then_inc(projected, 1)

        @block.scalar
        def _(act):
            act.sem_inc(decayed, AHEAD)
            act.sem_inc(guarded, AHEAD)
            nc.scalar.activation(A[:], A[:], ACT.Exp).then_inc(a_step, 1)
            act.wait_ge(a_step, past(7))
            with act.Fori(0, PAIRS // 2) as i:
                for p in range(2):
                    pair = i * 2 + p
                    act.wait_ge(loaded[p], past(i * (16 * LOADS) + 16 * LOADS))
                    act.wait_ge(prepared, past((pair + 1) * 3))

                    def round_(j):
                        for k in range(NR // GA):
                            for r in range(k * GA, k * GA + GA):
                                n = pair * DST + j * NR + r
                                act.wait_ge(scanned, done(n - 2 * GA))
                                act.sem_inc(passed, 1)
                                nc.scalar.activation(decay[r % (2 * GA)][:, :, 1:], delta[p][:, :, 1:], ACT.Exp,
                                                     scale=A[:, ds(j * NR + r, 1)]).then_inc(decayed, 1)
                            for r in range(k * GA, k * GA + GA):
                                n = pair * DST + j * NR + r
                                act.wait_ge(multiplied, done(n - 2 * GA))
                                act.sem_inc(passed, 1)
                                nc.scalar.activation(guard[r % (2 * GA)][:], after[:], ACT.Sigmoid,
                                                     scale=A[:, ds(j * NR + r, 1)],
                                                     bias=bias[:]).then_inc(guarded, 1)

                    with act.Fori(0, ROUNDS) as j:
                        round_(j)

        @block.gpsimd
        def _(pool):
            pool.sem_inc(multiplied, AHEAD)
            with pool.Fori(0, PAIRS) as pair:
                with pool.Fori(0, ROUNDS) as j:
                    for r in range(NR):
                        n = pair * DST + j * NR + r
                        pool.wait_ge(guarded, done(n))
                        pool.wait_ge(weighted, done(n - 3))
                        pool.wait_ge(scanned, done(n))
                        nc.gpsimd.tensor_tensor(hg[r % 3][:], h[r % 2][:], guard[r % (2 * GA)][:],
                                                ALU.mult).then_inc(multiplied, 1)

        @block.vector
        def _(vec):
            vec.sem_inc(scanned, AHEAD)
            vec.sem_inc(weighted, AHEAD)
            vec.sem_inc(fed, AHEAD)
            nc.vector.tensor_copy(sel[:], sel_f[:]).then_inc(a_step, 1)
            vec.memset(ones[:], 1.0).then_inc(a_step, 1)
            vec.memset(bias[:], -LOG_EPS).then_inc(a_step, 1)
            vec.memset(after[:, :, L - 1:L], 0.0).then_inc(a_step, 1)
            for k in range(2 * GA):
                last = vec.memset(decay[k][:, :, 0:1], 0.0)
            last.then_inc(a_step, 1)
            vec.wait_ge(a_step, past(6))
            vec.tensor_scalar(A[:], A[:], -1.0, None, ALU.mult).then_inc(a_step, 1)
            vec.wait_ge(a_step, past(7))
            with vec.Fori(0, PAIRS // 2) as i:
                for p in range(2):
                    pair = i * 2 + p
                    vec.wait_ge(loaded[p], past(i * (16 * LOADS) + 16 * LOADS))
                    vec.wait_ge(guarded, done(pair * DST - 1))
                    for s in range(2):
                        vec.tensor_tensor_scan(after[:, s, L - 2::-1], ones[:, 0:L - 1], delta[p][:, s, L - 1:0:-1],
                                               0.0, ALU.mult, ALU.add).then_inc(prepared, 1)
                    vec.wait_ge(fed, done(pair * DST - 1))
                    vec.tensor_tensor(du[:], delta[p][:], u[p][:], ALU.mult).then_inc(prepared, 1)
                    vec.wait_ge(prepared, past((pair + 1) * 3))

                    def feed(r, j):
                        vec.wait_ge(b_ready, done(pair * DST + j * NR + r))
                        vec.tensor_tensor(ps_b[r % 2][:], du[:], ps_b[r % 2][:], ALU.mult).then_inc(fed, 1)

                    def scan(r, j):
                        n = pair * DST + j * NR + r
                        vec.wait_ge(decayed, done(n))
                        vec.wait_ge(multiplied, done(n - 2))
                        vec.wait_ge(fed, done(n))
                        vec.tensor_tensor_scan(h[r % 2][:].rearrange("p s t -> p (s t)"),
                                               decay[r % (2 * GA)][:].rearrange("p s t -> p (s t)"),
                                               ps_b[r % 2][:].rearrange("p s t -> p (s t)"),
                                               0.0, ALU.mult, ALU.add).then_inc(scanned, 1)

                    def weight(r, j):
                        n = pair * DST + j * NR + r
                        vec.wait_ge(multiplied, done(n))
                        vec.wait_ge(c_ready, done(n))
                        vec.wait_ge(summed, done(n - 2))
                        vec.tensor_tensor(ch[r % 2][:], hg[r % 3][:], ps_c[:], ALU.mult).then_inc(weighted, 1)

                    for r in range(NR):
                        feed(r, 0)
                        if r >= 2:
                            weight(r - 2, 0)
                        scan(r, 0)
                    with vec.Fori(1, ROUNDS) as j:
                        for r in range(NR):
                            feed(r, j)
                            weight((r - 2) % NR, j if r >= 2 else j - 1)
                            scan(r, j)
                    weight(NR - 2, ROUNDS - 1)
                    weight(NR - 1, ROUNDS - 1)
                    vec.wait_ge(summed, done(pair * DST + DST - 1))
                    vec.scalar_tensor_tensor(y[:], u[p][:], skip[:], ps_y[:], ALU.mult, ALU.add).then_inc(y_step[p], 1)
                    vec.wait_ge(gate_in, past((pair + 1) * 16))
                    vec.wait_ge(y_step[p], past(i + 1))
                    vec.tensor_tensor(y[:], y[:], gate[:], ALU.mult).then_inc(y_done, 1)
                    vec.wait_ge(projected, past(pair + 1))
                    vec.tensor_tensor(rows3(X, pair * (2 * C), 2 * C), rows3(X, pair * (2 * C), 2 * C), ps_o,
                                      ALU.add).then_inc(added, 1)


def add_rows(nc, name, dst, src):
    with ExitStack() as ctx:
        summed = ctx.enter_context(nc.semaphore(f"{name}_summed"))
        block = ctx.enter_context(nc.Block())
        W = 32

        @block.vector
        def _(vec):
            with vec.Fori(0, G // W) as k:
                vec.tensor_tensor(rows3(dst, k * W, W), rows3(dst, k * W, W), rows3(src, k * W, W),
                                  ALU.add).then_inc(summed, 1)


class Stage:

    def __init__(self, nc, ctx, name):
        self.nc, self.ctx, self.name, self.sems = nc, ctx, name, []

    def one(self, name, shape, dt=F32):
        return self.ctx.enter_context(self.nc.sbuf_tensor(f"{self.name}_{name}", shape, dt))

    def two(self, name, shape, dt=F32):
        return [self.one(f"{name}{p}", shape, dt) for p in range(2)]

    def bank(self, name, shape, dt=F32):
        return self.ctx.enter_context(self.nc.psum_tensor(f"{self.name}_{name}", shape, dt))

    def banks(self, name, shape, dt=F32):
        return [self.bank(f"{name}{p}", shape, dt) for p in range(2)]

    def counter(self, name):
        self.sems.append(self.ctx.enter_context(self.nc.semaphore(f"{self.name}_{name}")))
        return self.sems[-1]

    def counters(self, name):
        return [self.counter(f"{name}{p}") for p in range(2)]

    def block(self):
        arm(self.nc, self.sems)
        return self.ctx.enter_context(self.nc.Block())


class Slots:

    def __init__(self, unroll, first, start, stop, last):
        self.unroll, self.first, self.start, self.last = unroll, first, start, last
        self.turns = (stop - start) // unroll

    def run(self, eng, slot):
        for k in range(self.first, self.start):
            slot(0, k)
        with eng.Fori(0, self.turns) as i:
            for k in range(self.start, self.start + self.unroll):
                slot(i, k)
        for k in range(self.start + self.turns * self.unroll, self.last):
            slot(0, k)

    def live(self, i, k):
        return not isinstance(i, int) or 0 <= k < SEQS

    def before(self, i, k):
        return max(0, min(k, SEQS)) if isinstance(i, int) else i * self.unroll + k

    def through(self, i, k):
        return self.before(i, k + 1)

    def round_of(self, i, k):
        return i + k // self.unroll


def wait(eng, sem, n):
    if not isinstance(n, int) or n > 0:
        eng.wait_ge(sem, past(n))


def fourier_mixer(nc, w, H):
    with ExitStack() as ctx:
        s = Stage(nc, ctx, "fft")
        T = s.one("T", [P, G, D])
        held = s.one("held", [P, G, D])
        gamma, beta = s.one("gamma", [P, D]), s.one("beta", [P, D])
        fc1 = s.one("fc1", [D + 1, FD])
        bn1 = s.one("bn1", [D, FD])
        fc2 = s.one("fc2", [FD, D])
        bn2 = s.one("bn2", [FD, D])
        bias2 = s.one("bias2", [1, D])
        ones = s.one("ones", [1, P])
        wr, wi = s.one("wr", [FD, FD]), s.one("wi", [FD, FD])
        bins_bias = s.one("bins_bias", [P, C, FD])
        dft, idft = s.one("dft", [P, C, L]), s.one("idft", [P, C, L])
        rb = row(w["L0_attn_rb"]).to_broadcast([P, FD])
        ib = row(w["L0_attn_ib"]).to_broadcast([P, FD])
        load(nc, "fft_w", [
            (held[:], w["scr_H"]),
            (gamma[:], spread_row(w["L0_attn_ln2_g"])), (beta[:], spread_row(w["L0_attn_ln2_b"])),
            (fc1[0:D, :], w["L0_attn_fc1_w"]), (fc1[D:D + 1, :], row(w["L0_attn_bn1_b"])),
            (bn1[:], row(w["L0_attn_bn1_s"]).to_broadcast([D, FD])), (fc2[:], w["L0_attn_fc2_w"]),
            (bn2[:], row(w["L0_attn_bn2_s"]).to_broadcast([FD, D])), (bias2[:], row(w["L0_attn_bn2_b"])),
            (wr[:], w["L0_attn_Wr"]), (wi[:], w["L0_attn_Wi"]),
            (bins_bias[:, 0, :], rb), (bins_bias[:, 1, :], rb), (bins_bias[1:P, 2, :], ib[1:P, :]),
            (bins_bias[0:1, 2, :], row(w["L0_attn_rb"])), (bins_bias[:, 3, :], ib),
            (dft[:], w["dft"]), (idft[:], w["idft"])])
        layer_norm(nc, "ln_f", H, T, 1e-3, gamma, beta)
        add_rows(nc, "fft_residual", H, held)

        rowsT = s.two("rowsT", [D + 1, L])
        f = s.two("f", [P, C, FD])
        spec = s.two("spec", [FD, L])
        minus_im = s.two("minus_im", [FD, L // 2])
        real = s.two("real", [FD, L // 2])
        z = s.two("z", [P, C, FD])
        back = s.two("back", [FD, L])
        cur = s.two("cur", [P, C, D])
        ps_a, ps_b = s.banks("ps_a", [P, L]), s.banks("ps_b", [P, L])
        ps_c, ps_d = s.banks("ps_c", [P, C, FD]), s.banks("ps_d", [P, L])
        passed, ready = s.counter("passed"), s.counter("ready")
        cur_ready, turned, rowsT_ready = s.counters("cur_ready"), s.counters("turned"), s.counters("rowsT_ready")
        fc1_done, f_ready, rfft_done = s.counters("fc1_done"), s.counters("f_ready"), s.counters("rfft_done")
        spec_ready, halves_ready, mixed = s.counters("spec_ready"), s.counters("halves_ready"), s.counters("mixed")
        biased, z_ready, irfft_done = s.counters("biased"), s.counters("z_ready"), s.counters("irfft_done")
        back_ready, fc2_done, added = s.counters("back_ready"), s.counters("fc2_done"), s.counters("added")
        block = s.block()

        @block.gpsimd
        def _(pool):
            with pool.Fori(0, SEQS // 2) as i:
                for p in range(2):
                    pool.wait_ge(turned[p], past(i))
                    nc.gpsimd.tensor_copy(cur[p][:], rows3(T, (i * 2 + p) * C, C)).then_inc(cur_ready[p], 1)

        @block.tensor
        def _(pe):
            pe.wait_ge(ready, past(7))
            with pe.Fori(0, SEQS // 2) as i:
                for p in range(2):
                    pe.wait_ge(cur_ready[p], past(i + 1))
                    pe.wait_ge(added[p], past(i))
                    pe.sem_inc(passed, 1)
                    for c in range(C):
                        last = nc.tensor.transpose(ps_a[p][0:D, c * P:(c + 1) * P], cur[p][:, c, :], w["ident"][:])
                    last.then_inc(turned[p], 1)
                for p in range(2):
                    pe.wait_ge(rowsT_ready[p], past(i + 1))
                    for c in range(C):
                        last = nc.tensor.matmul(ps_a[p][:, c * P:(c + 1) * P], rowsT[p][:, c * P:(c + 1) * P], fc1[:],
                                                start=True, stop=True)
                    last.then_inc(fc1_done[p], 1)
                for p in range(2):
                    pe.wait_ge(f_ready[p], past(i + 1))
                    for c in range(C):
                        last = nc.tensor.matmul(ps_b[p][:], f[p][:, c, :], dft[:, c, :], start=(c == 0),
                                                stop=(c == C - 1))
                    last.then_inc(rfft_done[p], 1)
                for p in range(2):
                    pe.wait_ge(spec_ready[p], past(i + 1))
                    pe.wait_ge(halves_ready[p], past(i * 2 + 2))
                    for k in range(C):
                        other = (minus_im, real)[k // 2][p]
                        nc.tensor.matmul(ps_c[p][:, k, :], spec[p][:, k * P:(k + 1) * P], wr[:], start=True, stop=False)
                        last = nc.tensor.matmul(ps_c[p][:, k, :], other[:, k % 2 * P:(k % 2 + 1) * P], wi[:],
                                                start=False, stop=True)
                    last.then_inc(mixed[p], 1)
                for p in range(2):
                    pe.wait_ge(z_ready[p], past(i + 1))
                    for k in range(C):
                        last = nc.tensor.matmul(ps_d[p][:], z[p][:, k, :], idft[:, k, :], start=(k == 0),
                                                stop=(k == C - 1))
                    last.then_inc(irfft_done[p], 1)
                for p in range(2):
                    pe.wait_ge(back_ready[p], past(i + 1))
                    for c in range(C):
                        to = ps_a[p][:, c * D:(c + 1) * D]
                        nc.tensor.matmul(to, back[p][:, c * P:(c + 1) * P], fc2[:], start=True, stop=False)
                        last = nc.tensor.matmul(to, ones[:], bias2[:], start=False, stop=True)
                    last.then_inc(fc2_done[p], 1)

        @block.scalar
        def _(act):
            with act.Fori(0, SEQS // 2) as i:
                for p in range(2):
                    act.wait_ge(fc1_done[p], past(i + 1))
                    nc.scalar.activation(f[p][:].rearrange("p c f -> p (c f)"), ps_a[p][:],
                                         ACT.Relu).then_inc(f_ready[p], 1)
                for p in range(2):
                    act.wait_ge(rfft_done[p], past(i + 1))
                    nc.scalar.activation(spec[p][:], ps_b[p][:], ACT.Copy).then_inc(spec_ready[p], 1)
                for p in range(2):
                    act.wait_ge(biased[p], past(i + 1))
                    nc.scalar.activation(z[p][:], z[p][:], ACT.Relu).then_inc(z_ready[p], 1)
                for p in range(2):
                    act.wait_ge(irfft_done[p], past(i + 1))
                    nc.scalar.activation(back[p][:], ps_d[p][:], ACT.Copy).then_inc(back_ready[p], 1)

        @block.vector
        def _(vec):
            vec.tensor_tensor(fc1[0:D, :], fc1[0:D, :], bn1[:], ALU.mult).then_inc(ready, 1)
            vec.tensor_tensor(fc2[:], fc2[:], bn2[:], ALU.mult).then_inc(ready, 1)
            vec.memset(ones[:], 1.0).then_inc(ready, 1)
            for p in range(2):
                vec.memset(rowsT[p][D:D + 1, :], 1.0).then_inc(ready, 1)
                vec.memset(minus_im[p][:, 0:1], 0.0)
                vec.memset(real[p][:, 0:1], 0.0).then_inc(ready, 1)
            with vec.Fori(0, SEQS // 2) as i:
                for p in range(2):
                    vec.wait_ge(turned[p], past(i + 1))
                    nc.vector.tensor_copy(rowsT[p][0:D, :], ps_a[p][0:D, :]).then_inc(rowsT_ready[p], 1)
                for p in range(2):
                    vec.wait_ge(spec_ready[p], past(i + 1))
                    vec.tensor_scalar(minus_im[p][:, 1:], spec[p][:, L // 2 + 1:], -1.0, None,
                                      ALU.mult).then_inc(halves_ready[p], 1)
                    nc.vector.tensor_copy(real[p][:, 1:], spec[p][:, 1:L // 2]).then_inc(halves_ready[p], 1)
                for p in range(2):
                    vec.wait_ge(mixed[p], past(i + 1))
                    vec.tensor_tensor(z[p][:], ps_c[p][:], bins_bias[:], ALU.add).then_inc(biased[p], 1)
                for p in range(2):
                    vec.wait_ge(fc2_done[p], past(i + 1))
                    g0 = (i * 2 + p) * C
                    vec.tensor_tensor(rows3(H, g0, C), rows3(H, g0, C),
                                      ps_a[p][:, 0:C * D].rearrange("p (c d) -> p c d", d=D),
                                      ALU.add).then_inc(added[p], 1)


def router(nc, w, name, T, xT, route_w, experts):
    with ExitStack() as ctx:
        s = Stage(nc, ctx, f"{name}_route")
        logits = route_w["logits"]
        cur = s.two("cur", [P, C, D])
        xc = s.two("xc", [D + 1, L])
        ps_t = s.banks("ps_t", [D, L])
        ps_l = s.banks("ps_l", [P, C, experts])
        passed, ready = s.counter("passed"), s.counter("ready")
        cur_ready, turned = s.counters("cur_ready"), s.counters("turned")
        kept, copied = s.counters("kept"), s.counters("copied")
        scored, saved = s.counters("scored"), s.counters("saved")
        block = s.block()

        @block.gpsimd
        def _(pool):
            with pool.Fori(0, SEQS // 2) as i:
                for p in range(2):
                    pool.wait_ge(turned[p], past(i))
                    nc.gpsimd.tensor_copy(cur[p][:], rows3(T, (i * 2 + p) * C, C)).then_inc(cur_ready[p], 1)

        @block.tensor
        def _(pe):
            pe.wait_ge(ready, past(2))
            with pe.Fori(0, SEQS // 2) as i:
                for p in range(2):
                    pe.wait_ge(cur_ready[p], past(i + 1))
                    pe.wait_ge(copied[p], past(i))
                    pe.sem_inc(passed, 1)
                    for c in range(C):
                        last = nc.tensor.transpose(ps_t[p][:, c * P:(c + 1) * P], cur[p][:, c, :], w["ident"][:])
                    last.then_inc(turned[p], 1)
                for p in range(2):
                    pe.wait_ge(copied[p], past(i + 1))
                    pe.wait_ge(saved[p], past(i))
                    pe.sem_inc(passed, 1)
                    for c in range(C):
                        last = nc.tensor.matmul(ps_l[p][:, c, :], xc[p][:, c * P:(c + 1) * P], route_w["weights"][:],
                                                start=True, stop=True)
                    last.then_inc(scored[p], 1)

        @block.scalar
        def _(act):
            with act.Fori(0, SEQS // 2) as i:
                for p in range(2):
                    act.wait_ge(copied[p], past(i + 1))
                    act.sem_inc(passed, 1)
                    nc.scalar.activation(xT[0:D, ds((i * 2 + p) * L, L)], xc[p][0:D, :], ACT.Copy)
                    nc.scalar.activation(xT[D:P, ds((i * 2 + p) * L, L)], xc[p][0:D, :], ACT.Copy).then_inc(kept[p], 1)

        @block.vector
        def _(vec):
            for p in range(2):
                vec.memset(xc[p][D:D + 1, :], 1.0).then_inc(ready, 1)
            with vec.Fori(0, SEQS // 2) as i:
                for p in range(2):
                    vec.wait_ge(turned[p], past(i + 1))
                    vec.wait_ge(scored[p], past(i))
                    vec.wait_ge(kept[p], past(i))
                    nc.vector.tensor_copy(xc[p][0:D, :], ps_t[p][:]).then_inc(copied[p], 1)
                for p in range(2):
                    vec.wait_ge(scored[p], past(i + 1))
                    nc.vector.tensor_copy(logits[:, ds((i * 2 + p) * C, C), :], ps_l[p][:]).then_inc(saved[p], 1)


def top_two(nc, w, name, probs, comb, experts, soften):
    with ExitStack() as ctx:
        def sb(n, shape):
            return ctx.enter_context(nc.sbuf_tensor(f"{name}_{n}", shape, F32))

        pref = sb("pref", [P, experts])
        best, total = sb("best", [P, G]), sb("total", [P, G])
        top = [sb("top0", [P, G]), sb("top1", [P, G])]
        hot = [sb("hot0", [P, G, experts]), sb("hot1", [P, G, experts])]
        rank = sb("rank", [P, G])
        even = sb("even", [P, G])
        load(nc, f"{name}_pref", [(pref[:], row(w["preference"][0:experts]).to_broadcast([P, experts]))])
        made = ctx.enter_context(nc.semaphore(f"{name}_made"))
        powered = ctx.enter_context(nc.semaphore(f"{name}_powered"))
        block = ctx.enter_context(nc.Block())

        def over(stat):
            return stat[:].unsqueeze(2).to_broadcast([P, G, experts])

        first_pass, second_pass = 2, 4

        @block.vector
        def _(vec):
            made_n = Count()

            def tt(out, a, b, op):
                vec.tensor_tensor(out, a, b, op).then_inc(made, made_n.up())
                vec.wait_ge(made, made_n.value)

            def reduced(out, a, op):
                vec.tensor_reduce(out, a, AX.X, op).then_inc(made, made_n.up())
                vec.wait_ge(made, made_n.value)

            def reciprocal(x):
                vec.reciprocal(x, x).then_inc(made, made_n.up())
                vec.wait_ge(made, made_n.value)

            reduced(best[:], probs[:], ALU.max)
            tt(probs[:], probs[:], over(best), ALU.subtract)
            vec.wait_ge(powered, 1)
            reduced(total[:], probs[:], ALU.add)
            reciprocal(total[:])
            tt(probs[:], probs[:], over(total), ALU.mult)
            for k in range(2):
                reduced(top[k][:], probs[:], ALU.max)
                tt(hot[k][:], probs[:], over(top[k]), ALU.is_equal)
                tt(hot[k][:], hot[k][:], pref[:].unsqueeze(1).to_broadcast([P, G, experts]), ALU.mult)
                reduced(rank[:], hot[k][:], ALU.max)
                tt(hot[k][:], hot[k][:], over(rank), ALU.is_equal)
                if k == 0:
                    vec.scalar_tensor_tensor(probs[:], hot[0][:], -2.0, probs[:], ALU.mult,
                                             ALU.add).then_inc(made, made_n.up())
                    vec.wait_ge(made, made_n.value)
            if soften:
                tt(even[:], top[1][:], top[0][:], ALU.subtract)
                vec.sem_inc(powered, 1)
                vec.wait_ge(powered, 3)
                vec.tensor_scalar(total[:], even[:], 1.0, None, ALU.add).then_inc(made, made_n.up())
                vec.wait_ge(made, made_n.value)
                reciprocal(total[:])
                nc.vector.tensor_copy(top[0][:], total[:]).then_inc(made, made_n.up())
                tt(top[1][:], even[:], total[:], ALU.mult)
            else:
                tt(total[:], top[0][:], top[1][:], ALU.add)
                vec.tensor_scalar(total[:], total[:], 1e-12, None, ALU.max).then_inc(made, made_n.up())
                vec.wait_ge(made, made_n.value)
                reciprocal(total[:])
                for k in range(2):
                    tt(top[k][:], top[k][:], total[:], ALU.mult)
            for k in range(2):
                tt(hot[k][:], hot[k][:], over(top[k]), ALU.mult)
            tt(comb[:], hot[0][:], hot[1][:], ALU.add)

        @block.scalar
        def _(act):
            act.wait_ge(made, 2)
            nc.scalar.activation(probs[:], probs[:], ACT.Exp).then_inc(powered, 1)
            if soften:
                act.wait_ge(powered, 2)
                nc.scalar.activation(even[:], even[:], ACT.Exp).then_inc(powered, 1)


PART_ROW = 32
GATE_ROWS = 2 * PART_ROW + E1


def gate_parts(nc, name, comb, parts, experts, ones):
    with ExitStack() as ctx:
        rest = ctx.enter_context(nc.sbuf_tensor(f"{name}_rest", [P, G, experts], F32))
        step = ctx.enter_context(nc.semaphore(f"{name}_step"))
        block = ctx.enter_context(nc.Block())

        @block.vector
        def _(vec):
            n = Count()

            def then(done):
                done.then_inc(step, n.up())
                vec.wait_ge(step, n.value)

            def part(k):
                return parts[:, :, k * PART_ROW:k * PART_ROW + experts]

            then(vec.memset(parts[:], 0.0))
            if ones:
                then(vec.memset(parts[:, :, experts:experts + 1], 1.0))
            then(nc.vector.tensor_copy(part(0), comb[:]))
            then(vec.tensor_tensor(rest[:], comb[:], part(0), ALU.subtract))
            then(nc.vector.tensor_copy(part(1), rest[:]))
            then(vec.tensor_tensor(part(2), rest[:], part(1), ALU.subtract))


def expert_ffn(nc, w, H):
    with ExitStack() as outer:
        xT = outer.enter_context(nc.sbuf_tensor("ffn_xT", [P, SEQS * L], F32))
        gates = outer.enter_context(nc.sbuf_tensor("ffn_gates", [P, G, GATE_ROWS], BF16))
        with ExitStack() as ctx:
            T = ctx.enter_context(nc.sbuf_tensor("ffn_T", [P, G, D], F32))
            logits = ctx.enter_context(nc.sbuf_tensor("ffn_logits", [P, G, E0], F32))
            gw = ctx.enter_context(nc.sbuf_tensor("ffn_gw", [D + 1, E0], F32))
            load(nc, "ffn_gate_w", [(gw[0:D, :], w["L0_ffn_gW"]), (gw[D:D + 1, :], row(w["L0_ffn_gb"]))])
            layer_norm(nc, "ln_e", H, T, 1e-5)
            router(nc, w, "ffn", T, xT, {"logits": logits, "weights": gw}, E0)
            comb = ctx.enter_context(nc.sbuf_tensor("ffn_comb", [P, G, E0], F32))
            top_two(nc, w, "ffn_top", logits, comb, E0, True)
            gate_parts(nc, "ffn_parts", comb, gates, E0, True)

        with ExitStack() as ctx:
            s = Stage(nc, ctx, "ffn")
            ew1 = s.one("ew1", [P, E0 // 2, P])
            ew2 = s.one("ew2", [P, E0, D])
            ew3 = s.one("ew3", [P, E0 // 2, D])
            eb1 = s.one("eb1", [P, E0])
            eb2 = s.one("eb2", [P, E0 // 2])
            eb3 = s.one("eb3", [GATE_ROWS, D])
            sw1, sw2, sw3 = s.one("sw1", [D, P]), s.one("sw2", [D, P]), s.one("sw3", [P, D])
            sb1, sb2 = s.one("sb1", [D, 1]), s.one("sb2", [P, 1])
            pick = s.one("pick", [GATE_ROWS, E0 // 2, P])
            pick_b = s.one("pick_b", [GATE_ROWS, E0 // 2, P], BF16)
            twice = s.one("twice", [P, D])
            clear(nc, "ffn_sw1", sw1[:, D:])
            clear(nc, "ffn_eb3", eb3[:])
            load(nc, "ffn_w", [
                (ew1[0:D], w["L0_ffn_eW1"].rearrange("(n a) f h -> a f n h", a=2)[0]),
                (ew1[D:P], w["L0_ffn_eW1"].rearrange("(n a) f h -> a f n h", a=2)[1]),
                (twice[:], w["stacked_identity"]), (ew2[:], w["L0_ffn_eW2"].rearrange("e h g -> h e g")),
                (ew3[:], w["L0_ffn_eW3"].rearrange("(q a) g o -> (a g) q o", a=2)),
                (eb1[:], w["eb1_columns"]), (eb2[:], w["eb2_columns"]),
                *((eb3[r * PART_ROW:r * PART_ROW + E0, :], w["L0_ffn_eb3"]) for r in range(3)),
                (eb3[E0:E0 + 1, :], row(w["L0_ffn_sb3"])),
                (sw1[:, 0:D], w["L0_ffn_sW1"]), (sw2[:], w["L0_ffn_sW2"]), (sw3[:], w["L0_ffn_sW3"]),
                (sb1[:], column(w["L0_ffn_sb1"])), (sb2[:], column(w["L0_ffn_sb2"])),
                (pick[:], w["pick_parts"][:, 0:E0 // 2, :])])
            cur = s.two("cur", [P, C, GATE_ROWS])
            gT = s.two("gT", [GATE_ROWS, L])
            gb = s.two("gb", [GATE_ROWS, L], BF16)
            gb_ready = s.counter("gb_ready")
            h1 = [s.two(f"h1_{e}", [P, L]) for e in range(2)]
            h2 = [s.two(f"h2_{q}", [P, L]) for q in range(2)]
            s1, s2 = s.two("s1", [D, L]), s.two("s2", [P, L])
            ps_g = s.bank("ps_g", [P, L])
            ps_t = s.bank("ps_t", [GATE_ROWS, L])
            ps_1 = s.banks("ps_1", [P, L])
            ps_2 = s.banks("ps_2", [P, L])
            ps_e = s.bank("ps_e", [P, L])
            ps_o = s.bank("ps_o", [P, C, D])
            halves = s.one("halves", [P, L])
            x = s.two("x", [P, L])
            x_ready = s.counter("x_ready")
            halved, halves_ready = s.counter("halved"), s.counter("halves_ready")
            passed, ready = s.counter("passed"), s.counter("ready")
            cur_ready, turned, gT_ready = s.counter("cur_ready"), s.counter("turned"), s.counter("gT_ready")
            first, first_act = s.counter("first"), s.counter("first_act")
            second, second_act = s.counter("second"), s.counter("second_act")
            spread, gated = s.counter("spread"), s.counter("gated")
            out_done, added = s.counter("out_done"), s.counter("added")
            block = s.block()
            N1, N2 = E0 + 1, E0 // 2 + 1
            pipe = Slots(2, -1, 2, SEQS - 1, SEQS + 1)
            live, before, through = pipe.live, pipe.before, pipe.through

            @block.gpsimd
            def _(pool):
                def slot(i, k):
                    if live(i, k + 1):
                        wait(pool, first, before(i, k) * N1)
                        nc.gpsimd.tensor_copy(x[(k + 1) % 2][:], xT[:, ds(before(i, k + 1) * L, L)]).then_inc(x_ready, 1)
                        wait(pool, turned, before(i, k))
                        nc.gpsimd.tensor_copy(cur[(k + 1) % 2][:], gates[:, ds(before(i, k + 1) * C, C), :]).then_inc(cur_ready, 1)

                pipe.run(pool, slot)

            @block.tensor
            def _(pe):
                def layer_1(i, k, n):
                    items = (n,) if n == E0 else (n, n + 1)
                    wait(pe, first_act, before(i, k) * N1 + items[-1] - 1)
                    if n == 0:
                        wait(pe, x_ready, through(i, k))
                    pe.sem_inc(passed, 1)
                    for n in items:
                        up = slice(D, P) if n % 2 else slice(0, D)
                        nc.tensor.matmul(ps_1[(k * N1 + n) % 2][:], sw1[:] if n == E0 else ew1[up, n // 2, :],
                                         x[k % 2][up, :], start=True, stop=True).then_inc(first, 1)

                def layer_2(i, k, n):
                    wait(pe, second_act, before(i, k) * N2 + n - 1)
                    wait(pe, first_act, before(i, k) * N1 + min(n * 2 + 2, N1))
                    pe.sem_inc(passed, 1)
                    to = ps_2[(k * N2 + n) % 2]
                    if n < E0 // 2:
                        for a in range(2):
                            last = nc.tensor.matmul(to[a * D:(a + 1) * D, :], ew2[:, n * 2 + a, :],
                                                    h1[a][n][:], start=True, stop=True)
                    else:
                        last = nc.tensor.matmul(to[:], sw2[:], s1[k % 2][:], start=True, stop=True)
                    last.then_inc(second, 1)

                def spread_gates(i, k, q):
                    wait(pe, gated, before(i, k) * 2 + q)
                    if q == 0:
                        wait(pe, gb_ready, through(i, k))
                    pe.sem_inc(passed, 1)
                    nc.tensor.matmul(ps_g[:], pick_b[:, q, :], gb[k % 2][:], start=True, stop=True).then_inc(spread, 1)

                def turn_gates(i, k, tiles):
                    if 0 in tiles:
                        wait(pe, cur_ready, through(i, k))
                        wait(pe, gT_ready, before(i, k))
                        pe.sem_inc(passed, 1)
                    for c in tiles:
                        last = nc.tensor.transpose(ps_t[:, c * P:(c + 1) * P], cur[k % 2][:, c, :], w["ident"][:])
                    if C - 1 in tiles:
                        last.then_inc(turned, 1)

                def output_halves(i, k):
                    p = k % 2
                    wait(pe, second_act, through(i, k) * N2)
                    wait(pe, gated, through(i, k) * 2)
                    wait(pe, halves_ready, before(i, k))
                    nc.tensor.matmul(ps_e[0:D, :], ew3[:, 0, :], h2[0][p][:], start=True, stop=False)
                    nc.tensor.matmul(ps_e[D:P, :], ew3[:, 1, :], h2[1][p][:], start=True, stop=True)
                    nc.tensor.matmul(ps_e[0:D, :], sw3[:], s2[p][:], start=False, stop=False)
                    nc.tensor.matmul(ps_e[0:D, :], eb3[:], gT[p][:], start=False, stop=True).then_inc(halved, 1)

                def output(i, k, c):
                    if c == 0:
                        wait(pe, halves_ready, through(i, k))
                        wait(pe, added, before(i, k))
                        pe.sem_inc(passed, 1)
                    last = nc.tensor.matmul(ps_o[:, c, :], halves[:, c * P:(c + 1) * P], twice[:], start=True, stop=True)
                    if c == C - 1:
                        last.then_inc(out_done, 1)

                def slot(i, k):
                    if live(i, k):
                        layer_1(i, k, 0)
                        spread_gates(i, k, 0)
                    if live(i, k - 1):
                        output_halves(i, k - 1)
                    if live(i, k + 1):
                        turn_gates(i, k + 1, (0, 1))
                    if live(i, k):
                        layer_1(i, k, 2)
                        layer_2(i, k, 0)
                    if live(i, k - 1):
                        output(i, k - 1, 0)
                    if live(i, k):
                        layer_1(i, k, E0)
                    if live(i, k + 1):
                        turn_gates(i, k + 1, (2, 3))
                    if live(i, k - 1):
                        output(i, k - 1, 1)
                    if live(i, k):
                        layer_2(i, k, 1)
                    if live(i, k - 1):
                        output(i, k - 1, 2)
                    if live(i, k):
                        spread_gates(i, k, 1)
                    if live(i, k - 1):
                        output(i, k - 1, 3)
                    if live(i, k):
                        layer_2(i, k, 2)

                pe.wait_ge(ready, past(1))
                pipe.run(pe, slot)

            @block.scalar
            def _(act):
                def act_1(i, k, n):
                    wait(act, first, before(i, k) * N1 + n + 1)
                    if n == E0:
                        to, bias = s1[k % 2][:], sb1[:]
                    else:
                        to, bias = h1[n % 2][n // 2][:], eb1[:, n:n + 1]
                    m = D if n == E0 else P
                    nc.scalar.activation(to, ps_1[(k * N1 + n) % 2][0:m, :], ACT.Relu, bias=bias).then_inc(first_act, 1)

                def act_2(i, k, n):
                    wait(act, second, before(i, k) * N2 + n + 1)
                    if n == 0:
                        wait(act, halved, before(i, k - 1))
                    to, bias = (h2[n][k % 2], eb2[:, n:n + 1]) if n < 2 else (s2[k % 2], sb2[:])
                    nc.scalar.activation(to[:], ps_2[(k * N2 + n) % 2][:], ACT.Relu, bias=bias).then_inc(second_act, 1)

                def slot(i, k):
                    if live(i, k):
                        act_1(i, k, 0)
                        act_1(i, k, 1)
                    if live(i, k - 1):
                        wait(act, halved, through(i, k - 1))
                        wait(act, out_done, before(i, k - 1))
                        nc.scalar.activation(halves[:], ps_e[:], ACT.Copy).then_inc(halves_ready, 1)
                    if live(i, k):
                        for step, n in ((act_1, 2), (act_1, 3), (act_2, 0), (act_1, E0), (act_2, 1), (act_2, 2)):
                            step(i, k, n)
                    if live(i, k + 1):
                        wait(act, gT_ready, through(i, k + 1))
                        wait(act, spread, before(i, k) * 2)
                        nc.scalar.activation(gb[(k + 1) % 2][:], gT[(k + 1) % 2][:], ACT.Copy).then_inc(gb_ready, 1)

                pipe.run(act, slot)

            @block.vector
            def _(vec):
                def gate(i, k, q):
                    wait(vec, spread, before(i, k) * 2 + q + 1)
                    wait(vec, second_act, before(i, k) * N2 + q + 1)
                    vec.tensor_tensor(h2[q][k % 2][:], h2[q][k % 2][:], ps_g[:], ALU.mult).then_inc(gated, 1)

                def slot(i, k):
                    if live(i, k):
                        gate(i, k, 0)
                    if live(i, k + 1):
                        wait(vec, turned, through(i, k + 1))
                        wait(vec, halved, before(i, k))
                        nc.vector.tensor_copy(gT[(k + 1) % 2][:], ps_t[:]).then_inc(gT_ready, 1)
                    if live(i, k):
                        gate(i, k, 1)
                    if live(i, k - 1):
                        wait(vec, out_done, through(i, k - 1))
                        g0 = before(i, k - 1) * C
                        vec.tensor_tensor(rows3(H, g0, C), rows3(H, g0, C), ps_o[:], ALU.add).then_inc(added, 1)

                nc.vector.tensor_copy(pick_b[:], pick[:]).then_inc(ready, 1)
                pipe.run(vec, slot)


def edge_bias(nc, w, bias_scr):
    W = 2048
    steps = EDGES // W
    with ExitStack() as ctx:
        s = Stage(nc, ctx, "edge")
        target, number = s.two("target", [P, W], I32), s.two("number", [P, W])
        wrapped = s.one("wrapped", [P, W])
        fixed = s.one("fixed", [P, W])
        match = s.two("match", [P, W])
        token = s.one("token", [P, C])
        last_of = s.one("last_of", [P, steps * C])
        last, found = s.one("last", [P, C]), s.one("found", [P, C])
        at = s.one("at", [P, C], I32)
        attr = s.one("attr", [P, C, 3])
        we, be = s.one("we", [P, 3, HEADS]), s.one("be", [P, HEADS])
        value, term = s.one("value", [P, HEADS, C]), s.one("term", [P, HEADS, C])
        parts, rest = s.one("parts", [HEADS * C, 3, P], BF16), s.one("rest", [HEADS * C, P])
        ps_v = s.bank("ps_v", [HEADS * C, P])
        load(nc, "edge_w", [(token[:], w["token_columns"]),
                            (we[:], row(w["L1_attn_We"].rearrange("k h -> (k h)")).to_broadcast([P, 3 * HEADS])
                             .rearrange("p (k h) -> p k h", h=HEADS)),
                            (be[:], spread_row(w["L1_attn_be"]))])
        landed, matched, shrunk = s.counters("landed"), s.counters("matched"), s.counters("shrunk")
        passed, made, used = s.counter("passed"), s.counter("made"), s.counters("used")
        fix_step = s.counter("fix_step")
        turned, high, rest_ready, mid = s.counter("turned"), s.counter("high"), s.counter("rest_ready"), s.counter("mid")
        gathered = w["gathered"][2]
        stored = s.counter("stored")
        block = s.block()
        half = C // 2

        @block.sync
        def _(sp):
            with sp.Fori(0, steps // 2) as i:
                for p in range(2):
                    sp.wait_ge(used[p], past(i))
                    sp.sem_inc(passed, 1)
                    at_edges = ds((i * 2 + p) * W, W)
                    sp.dma_start(target[p][:], w["L1_attn_edge_index"][1:2, at_edges].to_broadcast([P, W])).then_inc(landed[p], 16)
                    sp.dma_start(number[p][:], w["edge_numbers"][0:1, at_edges].to_broadcast([P, W])).then_inc(landed[p], 16)
            sp.wait_ge(made, past(12))
            sp.dma_start(bias_scr.rearrange("a (r p) -> r a p", p=P), parts[:]).then_inc(stored, 16)
            sp.wait_ge(stored, past(16))

        @block.vector
        def _(vec):
            with vec.Fori(0, steps // 2) as i:
                for p in range(2):
                    k = i * 2 + p
                    vec.wait_ge(landed[p], past((i + 1) * 32))
                    vec.wait_ge(matched[0], past(k * half))
                    vec.wait_ge(matched[1], past(k * half))
                    vec.wait_ge(fix_step, past(k * 2))
                    vec.tensor_scalar(wrapped[:], target[p][:], 0.0, float(L), ALU.is_lt, ALU.mult).then_inc(fix_step, 1)
                    vec.wait_ge(fix_step, past(k * 2 + 1))
                    vec.tensor_tensor(fixed[:], target[p][:], wrapped[:], ALU.add).then_inc(fix_step, 1)
                    vec.wait_ge(fix_step, past(k * 2 + 2))
                    for c in range(C):
                        n = k * half + c // 2
                        vec.wait_ge(shrunk[c % 2], past(n))
                        step = vec.scalar_tensor_tensor(match[c % 2][:], fixed[:], token[:, c:c + 1], number[p][:],
                                                        ALU.is_equal, ALU.mult)
                        step.then_inc(matched[c % 2], 1)
                        if c % 2:
                            for q in range(2):
                                vec.wait_ge(matched[q], past(n + 1))
                                done = vec.tensor_reduce(last_of[:, ds(k * C + c - 1 + q, 1)], match[q][:], AX.X, ALU.max)
                                done.then_inc(shrunk[q], 1)
                    for q in range(2):
                        vec.wait_ge(shrunk[q], past((k + 1) * half))
                    vec.sem_inc(used[p], 1)
            n = Count(1)

            def then(step):
                step.then_inc(made, n.up())
                vec.wait_ge(made, n.value)

            then(vec.tensor_reduce(last[:], last_of[:].rearrange("p (k c) -> p c k", c=C), AX.X, ALU.max))
            then(vec.tensor_scalar(found[:], last[:], 0.0, None, ALU.is_gt))
            then(vec.tensor_scalar(at[:], last[:], -1.0, 0.0, ALU.add, ALU.max))
            vec.wait_ge(gathered, 16 * C)

            def attribute(k):
                return attr[:, :, k].unsqueeze(1).to_broadcast([P, HEADS, C])

            def weight(x):
                return x.unsqueeze(2).to_broadcast([P, HEADS, C])

            then(vec.tensor_tensor(value[:], attribute(0), weight(we[:, 0, :]), ALU.mult))
            for k in range(1, 3):
                then(vec.tensor_tensor(term[:], attribute(k), weight(we[:, k, :]), ALU.mult))
                then(vec.tensor_tensor(value[:], value[:], term[:], ALU.add))
            then(vec.tensor_tensor(value[:], value[:], weight(be[:]), ALU.add))
            then(vec.tensor_tensor(value[:], value[:], found[:].unsqueeze(1).to_broadcast([P, HEADS, C]), ALU.mult))
            vec.wait_ge(high, past(1))
            vec.tensor_tensor(rest[:], ps_v[:], parts[:, 0, :], ALU.subtract).then_inc(rest_ready, 1)
            vec.wait_ge(mid, past(1))
            then(vec.tensor_tensor(parts[:, 2, :], rest[:], parts[:, 1, :], ALU.subtract))
            then(vec.memset(found[:], 0.0))

        @block.gpsimd
        def _(pool):
            pool.wait_ge(made, past(3))
            for c in range(C):
                nc.gpsimd.indirect_dma_start(
                    out=attr[:, c, :], out_offset=None, in_=w["L1_attn_edge_attr"],
                    in_offset=bass.IndirectOffsetOnAxis(ap=at[:, c:c + 1], axis=0)).then_inc(gathered, 16)

        @block.tensor
        def _(pe):
            pe.wait_ge(made, past(10))
            nc.tensor.transpose(ps_v[:], value[:].rearrange("p h c -> p (h c)"), w["ident"][:]).then_inc(turned, 1)

        @block.scalar
        def _(act):
            act.wait_ge(turned, past(1))
            nc.scalar.activation(parts[:, 0, :], ps_v[:], ACT.Copy).then_inc(high, 1)
            act.wait_ge(rest_ready, past(1))
            nc.scalar.activation(parts[:, 1, :], rest[:], ACT.Copy).then_inc(mid, 1)


PARTS = 3
CROSS = PARTS * PARTS * HD
BIAS, PEAK = CROSS, CROSS + PARTS
STACK = PEAK + PARTS
QUAD = 4
UNROLL = 3


def edge_attention(nc, w, H):
    bias_scr = nc.dram_tensor("scratch_bias", (PARTS, HEADS * L), BF16).ap()
    peak_scr = nc.dram_tensor("scratch_peak", (PARTS, HEADS * L), BF16).ap()
    rows_scr = nc.dram_tensor("scratch_rows", (P, G, D), F32).ap()
    q_scr = nc.dram_tensor("scratch_q", (PARTS, PARTS, HD, HEADS * L), BF16).ap()
    k_scr = nc.dram_tensor("scratch_k", (PARTS, HD, HEADS * L), BF16).ap()
    edge_bias(nc, w, bias_scr)
    with ExitStack() as ctx:
        T = ctx.enter_context(nc.sbuf_tensor("attn_T", [P, G, D], F32))
        layer_norm(nc, "ln_a", H, T, 1e-5)
        move(nc, "attn_rows", rows_scr, T[:])
    with ExitStack() as ctx:
        s = Stage(nc, ctx, "attn")
        wqk, wv, wo = s.one("wqk", [D + 1, 2 * D]), s.one("wv", [D + 1, D]), s.one("wo", [D + 1, D])
        ks = [s.one(f"ks{m}", [STACK, HEADS, L], BF16) for m in range(UNROLL)]
        qs = [s.one(f"qs{m}", [STACK, HEADS, L], BF16) for m in range(UNROLL)]
        values = [s.one(f"values{m}", [P, C, HEADS, 32]) for m in range(UNROLL)]
        xT, oT = s.one("xT", [D + 1, L]), s.one("oT", [D + 1, L])
        with ExitStack() as zero:
            made = zero.enter_context(nc.semaphore("attn_made"))
            block = zero.enter_context(nc.Block())

            @block.vector
            def _(vec):
                for m in range(UNROLL):
                    vec.memset(ks[m][:], 1.0).then_inc(made, 1)
                vec.memset(xT[D:D + 1, :], 1.0).then_inc(made, 1)
                vec.memset(oT[D:D + 1, :], 1.0).then_inc(made, 1)

            @block.gpsimd
            def _(pool):
                for m in range(UNROLL):
                    pool.memset(qs[m][:], 1.0).then_inc(made, 1)
                for m in range(UNROLL):
                    pool.memset(values[m][:, :, :, 0:HD], 0.0)
                    pool.memset(values[m][:, :, :, HD:HD + 1], 1.0)
                    pool.memset(values[m][:, :, :, HD + 1:], 0.0).then_inc(made, 1)

        load(nc, "attn_w", [
            (wqk[0:D, 0:D], w["wq_columns"]), (wqk[0:D, D:], w["wk_columns"]),
            (wqk[D:D + 1, 0:D], row(w["bq_columns"])), (wqk[D:D + 1, D:], row(w["bk_columns"])),
            (wv[0:D, :], w["L1_attn_Wv"]), (wv[D:D + 1, :], row(w["L1_attn_bv"])),
            (wo[0:D, :], w["L1_attn_Wo"]), (wo[D:D + 1, :], row(w["L1_attn_bo"]))]
            + [(ks[m][BIAS:PEAK, :, :].rearrange("a h t -> a (h t)"), bias_scr) for m in range(UNROLL)])

        cur = s.one("cur", [P, C, D])
        parts, rest = s.one("parts", [P, PARTS, L], BF16), s.one("rest", [P, L])
        peaks = [s.one(f"peaks{m}", [P, HEADS * C]) for m in range(UNROLL)]
        peak_parts = s.one("peak_parts", [HEADS * C, PARTS, P], BF16)
        peak_rest = s.one("peak_rest", [HEADS * C, P])
        probs = s.two("probs", [P, QUAD, C, L])
        o_rows = s.two("o_rows", [P, L])
        share = s.one("share", [P, C, QUAD])
        o_norm = s.one("o_norm", [P, C, 2, QUAD * HD])
        ps_row = s.banks("ps_row", [P, L])
        ps_col = s.banks("ps_col", [P, 2, L])
        ps_o = s.bank("ps_o", [P, L])
        ps_m = s.bank("ps_m", [P, L])
        passed, ready = s.counter("passed"), s.counter("ready")
        cur_in, qk_stored, peak_stored = s.counter("cur_in"), s.counter("qk_stored"), s.counter("peak_stored")
        stack_in = [s.counter(f"stack_in{m}") for m in range(UNROLL)]
        peak_in = [s.counter(f"peak_in{m}") for m in range(UNROLL)]
        turned, x_copied = s.counter("turned"), s.counter("x_copied")
        qk_done, qk_high, qk_rest, qk_mid, qk_low = (s.counter(f"qk_{n}") for n in ("done", "high", "rest", "mid", "low"))
        v_done, v_copied = s.counter("v_done"), s.counter("v_copied")
        row_scored, row_maxed = s.counter("row_scored"), s.counter("row_maxed")
        pk_done, pk_high, pk_rest, pk_mid, pk_low = (s.counter(f"pk_{n}") for n in ("done", "high", "rest", "mid", "low"))
        col_scored, powered = s.counter("col_scored"), s.counter("powered")
        o_done, o_copied, o_turned = s.counter("o_done"), s.counter("o_copied"), s.counter("o_turned")
        shared, normed, n_turned = s.counter("shared"), s.counter("normed"), s.counter("n_turned")
        n_copied, out_done, added = s.counter("n_copied"), s.counter("out_done"), s.counter("added")
        arm(nc, s.sems)
        block = ctx.enter_context(nc.Block())

        ROWS, COLS = HEADS * C, HEADS * C // 2
        STEPS = ROWS // 2
        COL_START = 4
        STACK_DMAS = 1 + PARTS
        FULL = (SEQS - 1 - 2) // UNROLL

        def slots(eng, slot):
            for k in range(-1, 2):
                slot(0, k)
            with eng.Fori(0, FULL) as i:
                for k in range(2, 2 + UNROLL):
                    slot(i, k)
            for k in range(2 + FULL * UNROLL, SEQS + 2):
                slot(0, k)

        def live(i, k):
            return not isinstance(i, int) or 0 <= k < SEQS

        def before(i, k):
            return max(0, min(k, SEQS)) if isinstance(i, int) else i * UNROLL + k

        def through(i, k):
            return before(i, k + 1)

        def round_of(i, k):
            return i + k // UNROLL

        def wait(eng, sem, n):
            if not isinstance(n, int) or n > 0:
                eng.wait_ge(sem, past(n))

        def col_items(step):
            first = max(0, step - COL_START) * 4 // 3
            return range(first, max(0, step + 1 - COL_START) * 4 // 3)

        @block.sync
        def _(sp):
            def fetch(i, k):
                wait(sp, turned, before(i, k))
                sp.sem_inc(passed, 1)
                sp.dma_start(cur[:], rows_scr[:, ds(before(i, k) * C, C), :]).then_inc(cur_in, 16)

            def slot(i, k):
                if live(i, k - 1):
                    m = (k - 1) % UNROLL
                    wait(sp, pk_low, through(i, k - 1))
                    sp.dma_start(peak_scr.rearrange("a (r p) -> r a p", p=P), peak_parts[:]).then_inc(peak_stored, 16)
                    wait(sp, peak_stored, through(i, k - 1) * 16)
                    sp.dma_start(qs[m][PEAK:STACK, :, :].rearrange("a h t -> a (h t)"), peak_scr).then_inc(peak_in[m], 16)
                    wait(sp, peak_in[m], (round_of(i, k - 1) + 1) * 16)
                    sp.sem_inc(passed, 1)
                if live(i, k + 1):
                    m = (k + 1) % UNROLL
                    wait(sp, qk_low, through(i, k + 1))
                    wait(sp, qk_mid, through(i, k + 1))
                    for copy in range(PARTS):
                        sp.dma_start(q_scr[:, copy].rearrange("a c (h t) -> (c h) a t", t=L),
                                     parts[0:D]).then_inc(qk_stored, 16)
                    sp.dma_start(k_scr.rearrange("b c (h t) -> (c h) b t", t=L), parts[D:]).then_inc(qk_stored, 16)
                    wait(sp, qk_stored, through(i, k + 1) * (16 * STACK_DMAS))
                    wait(sp, col_scored, before(i, k - 1) * COLS)
                    sp.sem_inc(passed, 1)
                    sp.dma_start(qs[m][0:CROSS].rearrange("r h t -> r (h t)"),
                                 q_scr.rearrange("a b c x -> (a b c) x")).then_inc(stack_in[m], 16)
                    for copy in range(PARTS):
                        rows = ks[m][copy * PARTS * HD:(copy + 1) * PARTS * HD]
                        sp.dma_start(rows.rearrange("r h t -> r (h t)"),
                                     k_scr.rearrange("b c x -> (b c) x")).then_inc(stack_in[m], 16)
                    if live(i, k + 2):
                        fetch(i, k + 2)
                    wait(sp, stack_in[m], (round_of(i, k + 1) + 1) * (16 * STACK_DMAS))
                    sp.sem_inc(passed, 1)

            fetch(0, 0)
            slots(sp, slot)

        @block.tensor
        def _(pe):
            def row_item(i, k, n):
                m = k % UNROLL
                if n == 0:
                    wait(pe, stack_in[m], (round_of(i, k) + 1) * (16 * STACK_DMAS))
                wait(pe, row_maxed, before(i, k) * ROWS + (n - 1))
                h, c = n // C, n % C
                nc.tensor.matmul(ps_row[n % 2][:], qs[m][0:PEAK, h, c * P:(c + 1) * P], ks[m][0:PEAK, h, :],
                                 start=True, stop=True).then_inc(row_scored, 1)

            def col_item(i, k, n):
                m = k % UNROLL
                if n == 0:
                    wait(pe, peak_in[m], (round_of(i, k) + 1) * 16)
                wait(pe, powered, before(i, k) * COLS + (n - 1))
                h, c = n // 2, n % 2 * 2
                for j in range(2):
                    last = nc.tensor.matmul(ps_col[n % 2][:, j, :], ks[m][:, h, (c + j) * P:(c + j + 1) * P],
                                            qs[m][:, h, :], start=True, stop=True)
                last.then_inc(col_scored, 1)

            def weigh(i, k, quad, c):
                if c == 0:
                    wait(pe, powered, before(i, k) * COLS + (quad + 1) * (COLS // 2))
                    wait(pe, o_copied, before(i, k) * 2 + quad)
                    if quad == 0:
                        wait(pe, v_copied, through(i, k))
                for hh in range(QUAD):
                    last = nc.tensor.matmul(ps_o[32 * hh:32 * hh + 32, :], values[k % UNROLL][:, c, quad * QUAD + hh, :],
                                            probs[quad][:, hh, c, :], start=(c == 0), stop=(c == C - 1))
                if c == C - 1:
                    last.then_inc(o_done, 1)

            def turn_out(i, k, quad):
                wait(pe, o_copied, before(i, k) * 2 + quad + 1)
                pe.sem_inc(passed, 1)
                for c in range(C):
                    last = nc.tensor.transpose(ps_m[:, c * P:(c + 1) * P], o_rows[quad][:, c * P:(c + 1) * P], w["ident"][:])
                last.then_inc(o_turned, 1)

            def slot(i, k):
                for step in range(STEPS):
                    if live(i, k):
                        row_item(i, k, step * 2)
                        row_item(i, k, step * 2 + 1)
                    if step == 0 and live(i, k - 1):
                        wait(pe, row_maxed, before(i, k - 1) * ROWS + ROWS)
                        wait(pe, normed, before(i, k - 2) * 2 + 1 if live(i, k - 2) else 0)
                        pe.sem_inc(passed, 1)
                        nc.tensor.transpose(ps_m[0:ROWS, 0:P], peaks[(k - 1) % UNROLL][:], w["ident"][:]).then_inc(pk_done, 1)
                    if step < C and live(i, k - 2):
                        weigh(i, k - 2, 1, step)
                    if step == 1 and live(i, k + 1):
                        wait(pe, cur_in, through(i, k + 1) * 16)
                        wait(pe, pk_rest, through(i, k - 1))
                        pe.sem_inc(passed, 1)
                        for c in range(C):
                            last = nc.tensor.transpose(ps_m[0:D, c * P:(c + 1) * P], cur[:, c, :], w["ident"][:])
                        last.then_inc(turned, 1)
                    if step == 2 and live(i, k + 1):
                        wait(pe, x_copied, through(i, k + 1))
                        pe.sem_inc(passed, 1)
                        nc.tensor.matmul(ps_m[:], wqk[:], xT[:], start=True, stop=True).then_inc(qk_done, 1)
                    if step == 3 and live(i, k + 1):
                        wait(pe, qk_rest, through(i, k + 1))
                        pe.sem_inc(passed, 1)
                        for c in range(C):
                            last = nc.tensor.matmul(ps_m[:, c * D:(c + 1) * D], xT[:, c * P:(c + 1) * P], wv[:],
                                                    start=True, stop=True)
                        last.then_inc(v_done, 1)
                    if step == 4 and live(i, k - 2):
                        wait(pe, v_copied, through(i, k + 1))
                        wait(pe, normed, before(i, k - 2) * 2 + 1)
                        turn_out(i, k - 2, 1)
                    if step == 6 and live(i, k - 2):
                        wait(pe, normed, through(i, k - 2) * 2)
                        pe.sem_inc(passed, 1)
                        for c in range(C):
                            last = nc.tensor.transpose(ps_m[0:D, c * P:(c + 1) * P],
                                                       o_norm[:, c, :, :].rearrange("p q x -> p (q x)"), w["ident"][:])
                        last.then_inc(n_turned, 1)
                    if step == 8 and live(i, k - 2):
                        wait(pe, n_copied, through(i, k - 2))
                        pe.sem_inc(passed, 1)
                        for c in range(C):
                            last = nc.tensor.matmul(ps_m[:, c * D:(c + 1) * D], oT[:, c * P:(c + 1) * P], wo[:],
                                                    start=True, stop=True)
                        last.then_inc(out_done, 1)
                    if live(i, k - 1):
                        for n in col_items(step):
                            col_item(i, k - 1, n)
                        if 10 <= step < 10 + C:
                            weigh(i, k - 1, 0, step - 10)
                        if step == 14:
                            wait(pe, added, through(i, k - 2))
                            turn_out(i, k - 1, 0)

            wait(pe, ready, 1)
            slots(pe, slot)

        @block.scalar
        def _(act):
            def copy_out(i, k, quad):
                wait(act, o_done, before(i, k) * 2 + quad + 1)
                wait(act, o_turned, before(i, k) * 2 + quad - 1)
                nc.scalar.activation(o_rows[quad][:], ps_o[:], ACT.Copy).then_inc(o_copied, 1)

            def slot(i, k):
                if live(i, k - 1):
                    wait(act, pk_done, through(i, k - 1))
                    wait(act, peak_stored, before(i, k - 1) * 16)
                    nc.scalar.activation(peak_parts[:, 0, :], ps_m[0:ROWS, 0:P], ACT.Copy, scale=-1.0).then_inc(pk_high, 1)
                    wait(act, pk_rest, through(i, k - 1))
                    nc.scalar.activation(peak_parts[:, 1, :], peak_rest[:], ACT.Copy).then_inc(pk_mid, 1)
                if live(i, k + 1):
                    wait(act, qk_done, through(i, k + 1))
                    wait(act, qk_stored, before(i, k + 1) * (16 * STACK_DMAS))
                    nc.scalar.activation(parts[:, 0, :], ps_m[:], ACT.Copy).then_inc(qk_high, 1)
                    wait(act, qk_rest, through(i, k + 1))
                    nc.scalar.activation(parts[:, 1, :], rest[:], ACT.Copy).then_inc(qk_mid, 1)
                if live(i, k - 2):
                    copy_out(i, k - 2, 1)
                if live(i, k - 1):
                    for step in range(STEPS):
                        for n in col_items(step):
                            wait(act, col_scored, before(i, k - 1) * COLS + n + 1)
                            quad, h, c = n // (COLS // 2), n // 2 % QUAD, n % 2 * 2
                            if n % (COLS // 2) == 0:
                                wait(act, o_done, before(i, k - 1) * 2 + quad - 1)
                            nc.scalar.activation(probs[quad][:, h, c:c + 2, :], ps_col[n % 2][:], ACT.Exp).then_inc(powered, 1)
                        if step == 14:
                            copy_out(i, k - 1, 0)

            slots(act, slot)

        @block.vector
        def _(vec):
            def normalise(i, k, quad):
                n = before(i, k) * 2 + quad
                wait(vec, o_turned, n + 1)
                wait(vec, normed, n)
                wait(vec, n_turned, before(i, k))
                o = ps_m[:].rearrange("p (c h x) -> p c h x", c=C, x=32)
                vec.reciprocal(share[:], o[:, :, :, HD]).then_inc(shared, 1)
                wait(vec, shared, n + 1)
                vec.tensor_tensor(o_norm[:, :, quad, :].rearrange("p c (h x) -> p c h x", x=HD), o[:, :, :, 0:HD],
                                  share[:].unsqueeze(3).to_broadcast([P, C, QUAD, HD]), ALU.mult).then_inc(normed, 1)

            def slot(i, k):
                for step in range(STEPS):
                    if live(i, k):
                        for n in (step * 2, step * 2 + 1):
                            wait(vec, row_scored, before(i, k) * ROWS + n + 1)
                            if n == 0:
                                wait(vec, pk_done, before(i, k - 2))
                            vec.tensor_reduce(peaks[k % UNROLL][:, n:n + 1], ps_row[n % 2][:], AX.X,
                                              ALU.max).then_inc(row_maxed, 1)
                    if step == 0 and live(i, k - 1):
                        wait(vec, pk_high, through(i, k - 1))
                        wait(vec, pk_low, before(i, k - 1))
                        vec.scalar_tensor_tensor(peak_rest[:], ps_m[0:ROWS, 0:P], -1.0, peak_parts[:, 0, :], ALU.mult,
                                                 ALU.subtract).then_inc(pk_rest, 1)
                    if step == 1 and live(i, k - 1):
                        wait(vec, pk_mid, through(i, k - 1))
                        vec.tensor_tensor(peak_parts[:, 2, :], peak_rest[:], peak_parts[:, 1, :],
                                          ALU.subtract).then_inc(pk_low, 1)
                    if step == 1 and live(i, k + 1):
                        wait(vec, turned, through(i, k + 1))
                        wait(vec, v_done, before(i, k + 1))
                        nc.vector.tensor_copy(xT[0:D, :], ps_m[0:D, :]).then_inc(x_copied, 1)
                    if step == 2 and live(i, k + 1):
                        wait(vec, qk_high, through(i, k + 1))
                        wait(vec, qk_low, before(i, k + 1))
                        vec.tensor_tensor(rest[:], ps_m[:], parts[:, 0, :], ALU.subtract).then_inc(qk_rest, 1)
                    if step == 3 and live(i, k + 1):
                        wait(vec, qk_mid, through(i, k + 1))
                        vec.tensor_tensor(parts[:, 2, :], rest[:], parts[:, 1, :], ALU.subtract).then_inc(qk_low, 1)
                        wait(vec, v_done, through(i, k + 1))
                        wait(vec, o_done, before(i, k - 2) * 2)
                        nc.vector.tensor_copy(values[(k + 1) % UNROLL][:, :, :, 0:HD],
                                              ps_m[:, 0:C * D].rearrange("p (c h x) -> p c h x", c=C, x=HD)
                                              ).then_inc(v_copied, 1)
                    if live(i, k - 2):
                        if step == 5:
                            normalise(i, k - 2, 1)
                        if step == 7:
                            wait(vec, n_turned, through(i, k - 2))
                            wait(vec, out_done, before(i, k - 2))
                            nc.vector.tensor_copy(oT[0:D, :], ps_m[0:D, :]).then_inc(n_copied, 1)
                        if step == 9:
                            wait(vec, out_done, through(i, k - 2))
                            g0 = before(i, k - 2) * C
                            vec.tensor_tensor(rows3(H, g0, C), rows3(H, g0, C),
                                              ps_m[:, 0:C * D].rearrange("p (c d) -> p c d", d=D), ALU.add).then_inc(added, 1)
                    if step == 15 and live(i, k - 1):
                        normalise(i, k - 1, 0)

            vec.tensor_scalar(wqk[:, 0:D], wqk[:, 0:D], HD ** -0.5, None, ALU.mult).then_inc(ready, 1)
            slots(vec, slot)


def gelu_experts(nc, w, H):
    pairs = E1 // 2
    with ExitStack() as outer:
        xT = outer.enter_context(nc.sbuf_tensor("moe_xT", [P, SEQS * L], F32))
        gates = outer.enter_context(nc.sbuf_tensor("moe_gates", [P, G, GATE_ROWS], BF16))
        with ExitStack() as ctx:
            T = ctx.enter_context(nc.sbuf_tensor("moe_T", [P, G, D], F32))
            logits = ctx.enter_context(nc.sbuf_tensor("moe_logits", [P, G, E1], F32))
            route = ctx.enter_context(nc.sbuf_tensor("moe_route", [D + 1, E1], F32))
            clear(nc, "moe_route", route[D:D + 1, :])
            load(nc, "moe_route_w", [(route[0:D, :], w["router_columns"])])
            layer_norm(nc, "ln_m", H, T, 1e-5)
            router(nc, w, "moe", T, xT, {"logits": logits, "weights": route}, E1)
            add_rows(nc, "moe_tokens", H, T)
            comb = ctx.enter_context(nc.sbuf_tensor("moe_comb", [P, G, E1], F32))
            top_two(nc, w, "moe_top", logits, comb, E1, False)
            gate_parts(nc, "moe_parts", comb, gates, E1, False)

        with ExitStack() as ctx:
            s = Stage(nc, ctx, "moe")
            w1 = s.one("w1", [P, pairs // 2, 2 * D])
            twice = s.one("twice", [P, D])
            w2 = s.one("w2", [P, pairs, D])
            b1 = s.one("b1", [P, pairs])
            b2 = s.one("b2", [GATE_ROWS, D])
            pick = s.one("pick", [GATE_ROWS, pairs, P])
            pick_b = s.one("pick_b", [GATE_ROWS, pairs, P], BF16)
            clear(nc, "moe_b2", b2[:])
            load(nc, "moe_w", [
                (twice[:], w["stacked_identity"]),
                *((w1[u * D:(u + 1) * D, n, a * D:(a + 1) * D], w["L1_ffn_w1"][(n * 2 + u) * 2 + a])
                  for u in range(2) for n in range(2) for a in range(2)),
                (w2[:], w["L1_ffn_w2"].rearrange("(q a) g o -> (a g) q o", a=2)),
                (b1[:], w["moe_b1_columns"]), *((b2[r * PART_ROW:r * PART_ROW + E1, :], w["L1_ffn_b2"]) for r in range(3)), (pick[:], w["pick_parts"])])
            cur = s.two("cur", [P, C, GATE_ROWS])
            gT = s.two("gT", [GATE_ROWS, L])
            gb = s.two("gb", [GATE_ROWS, L], BF16)
            gb_ready, ready = s.counter("gb_ready"), s.counter("ready")
            h = [s.two(f"h{q}", [P, L]) for q in range(pairs)]
            hg = [s.two(f"hg{q}", [P, L]) for q in range(pairs)]
            ps_t = s.bank("ps_t", [GATE_ROWS, L])
            ps_1, ps_g = s.banks("ps_1", [P, L]), s.banks("ps_g", [P, L])
            ps_e = s.bank("ps_e", [P, L])
            ps_o = s.bank("ps_o", [P, C, D])
            halves = s.one("halves", [P, L])
            x = s.two("x", [P, L])
            x_ready = s.counter("x_ready")
            halved, halves_ready = s.counter("halved"), s.counter("halves_ready")
            passed = s.counter("passed")
            cur_ready, turned, gT_ready = s.counter("cur_ready"), s.counter("turned"), s.counter("gT_ready")
            first, gelus = s.counter("first"), s.counter("gelus")
            spread, gated = s.counter("spread"), s.counter("gated")
            out_done, added = s.counter("out_done"), s.counter("added")
            block = s.block()
            pipe = Slots(2, -1, 2, SEQS - 1, SEQS + 1)
            live, before, through = pipe.live, pipe.before, pipe.through

            @block.gpsimd
            def _(pool):
                def slot(i, k):
                    if live(i, k + 1):
                        wait(pool, first, before(i, k) * pairs)
                        nc.gpsimd.tensor_copy(x[(k + 1) % 2][:], xT[:, ds(before(i, k + 1) * L, L)]).then_inc(x_ready, 1)
                        wait(pool, turned, before(i, k))
                        nc.gpsimd.tensor_copy(cur[(k + 1) % 2][:], gates[:, ds(before(i, k + 1) * C, C), :]).then_inc(cur_ready, 1)

                pipe.run(pool, slot)

            @block.tensor
            def _(pe):
                def first_layers(i, k, q):
                    wait(pe, gelus, before(i, k) * pairs + q)
                    if q == 0:
                        wait(pe, x_ready, through(i, k))
                    pe.sem_inc(passed, 1)
                    for u in range(2):
                        up = slice(u * D, (u + 1) * D)
                        nc.tensor.matmul(ps_1[u][:], w1[up, q // 2, :], x[k % 2][up, :],
                                         start=True, stop=True).then_inc(first, 1)

                def spread_gates(i, k, q):
                    wait(pe, gated, before(i, k) * pairs + q - 1)
                    if q == 0:
                        wait(pe, gb_ready, through(i, k))
                    pe.sem_inc(passed, 1)
                    nc.tensor.matmul(ps_g[q % 2][:], pick_b[:, q, :], gb[k % 2][:], start=True, stop=True).then_inc(spread, 1)

                def turn_gates(i, k, tiles):
                    if 0 in tiles:
                        wait(pe, cur_ready, through(i, k))
                        wait(pe, gT_ready, before(i, k))
                        pe.sem_inc(passed, 1)
                    for c in tiles:
                        last = nc.tensor.transpose(ps_t[:, c * P:(c + 1) * P], cur[k % 2][:, c, :], w["ident"][:])
                    if C - 1 in tiles:
                        last.then_inc(turned, 1)

                def output_halves(i, k):
                    wait(pe, gated, through(i, k) * pairs)
                    wait(pe, halves_ready, before(i, k))
                    for q in range(pairs):
                        nc.tensor.matmul(ps_e[q % 2 * D:(q % 2 + 1) * D, :], w2[:, q, :], hg[q][k % 2][:],
                                         start=(q < 2), stop=(q == pairs - 1))
                    nc.tensor.matmul(ps_e[0:D, :], b2[:], gT[k % 2][:], start=False, stop=True).then_inc(halved, 1)

                def output(i, k, c):
                    if c == 0:
                        wait(pe, halves_ready, through(i, k))
                        wait(pe, added, before(i, k))
                        pe.sem_inc(passed, 1)
                    last = nc.tensor.matmul(ps_o[:, c, :], halves[:, c * P:(c + 1) * P], twice[:], start=True, stop=True)
                    if c == C - 1:
                        last.then_inc(out_done, 1)

                def slot(i, k):
                    if live(i, k):
                        first_layers(i, k, 0)
                        spread_gates(i, k, 0)
                    if live(i, k + 1):
                        turn_gates(i, k + 1, (0, 1))
                    if live(i, k):
                        spread_gates(i, k, 1)
                    if live(i, k - 1):
                        output_halves(i, k - 1)
                    if live(i, k + 1):
                        turn_gates(i, k + 1, (2, 3))
                    if live(i, k):
                        first_layers(i, k, 2)
                    if live(i, k - 1):
                        output(i, k - 1, 0)
                    if live(i, k):
                        spread_gates(i, k, 2)
                    if live(i, k - 1):
                        output(i, k - 1, 1)
                        output(i, k - 1, 2)
                    if live(i, k):
                        spread_gates(i, k, 3)
                    if live(i, k - 1):
                        output(i, k - 1, 3)

                pe.wait_ge(ready, past(1))
                pipe.run(pe, slot)

            @block.scalar
            def _(act):
                def slot(i, k):
                    for q in range(pairs):
                        if live(i, k):
                            wait(act, first, before(i, k) * pairs + q + 1)
                            if q == 0:
                                wait(act, gated, before(i, k - 1) * pairs)
                            nc.scalar.activation(h[q][k % 2][:], ps_1[q % 2][:], ACT.Gelu, bias=b1[:, q:q + 1]).then_inc(gelus, 1)
                        if q == 1 and live(i, k - 1):
                            wait(act, halved, through(i, k - 1))
                            wait(act, out_done, before(i, k - 1))
                            nc.scalar.activation(halves[:], ps_e[:], ACT.Copy).then_inc(halves_ready, 1)
                    if live(i, k + 1):
                        wait(act, gT_ready, through(i, k + 1))
                        wait(act, spread, before(i, k) * pairs)
                        nc.scalar.activation(gb[(k + 1) % 2][:], gT[(k + 1) % 2][:], ACT.Copy).then_inc(gb_ready, 1)

                pipe.run(act, slot)

            @block.vector
            def _(vec):
                def slot(i, k):
                    if live(i, k):
                        for q in range(pairs):
                            wait(vec, spread, before(i, k) * pairs + q + 1)
                            wait(vec, gelus, before(i, k) * pairs + q + 1)
                            if q == 0:
                                wait(vec, halved, before(i, k - 1))
                            vec.tensor_tensor(hg[q][k % 2][:], h[q][k % 2][:], ps_g[q % 2][:], ALU.mult).then_inc(gated, 1)
                    if live(i, k + 1):
                        wait(vec, turned, through(i, k + 1))
                        wait(vec, halved, before(i, k))
                        nc.vector.tensor_copy(gT[(k + 1) % 2][:], ps_t[:]).then_inc(gT_ready, 1)
                    if live(i, k - 1):
                        wait(vec, out_done, through(i, k - 1))
                        g0 = before(i, k - 1) * C
                        vec.tensor_tensor(rows3(H, g0, C), rows3(H, g0, C), ps_o[:], ALU.add).then_inc(added, 1)

                nc.vector.tensor_copy(pick_b[:], pick[:]).then_inc(ready, 1)
                pipe.run(vec, slot)


def program(nc, w, out):
    with ExitStack() as ctx:
        w["gathered"] = [ctx.enter_context(nc.semaphore(f"gathered{n}")) for n in range(3)]
        ident = ctx.enter_context(nc.sbuf_tensor("ident", [P, P], F32))
        load(nc, "consts", [(ident[:], w["identity"])])
        w["ident"] = ident
        H = ctx.enter_context(nc.sbuf_tensor("H", [P, G, D], F32))
        embed(nc, w, H)
        scr = {n: nc.dram_tensor(f"scratch_{n}", shape, dt).ap() for n, shape, dt in (
            ("H", (P, G, D), F32), ("gate", (DIN, SEQS, L), F32), ("u", (DIN, SEQS, L), F32),
            ("delta", (DIN, SEQS, L), F32), ("bc", (2 * DST, 3, SEQS, L), BF16))}
        move(nc, "spill", scr["H"], H[:])
        mamba_inputs(nc, w, H, H, scr)
        selective_scan(nc, w, H, scr)
        w["scr_H"] = scr["H"]
        renew(nc)
        fourier_mixer(nc, w, H)
        renew(nc)
        expert_ffn(nc, w, H)
        renew(nc)
        edge_attention(nc, w, H)
        renew(nc)
        gelu_experts(nc, w, H)
        with ExitStack() as run:
            written = run.enter_context(nc.semaphore("written"))
            block = run.enter_context(nc.Block())

            @block.sync
            def _(sp):
                sp.dma_start(out.rearrange("b (c p) d -> p (b c) d", p=P), H[:]).then_inc(written, 16)
                sp.wait_ge(written, 16)


def layouts(inputs):
    import numpy as np
    a = {}
    for name, x in inputs.items():
        a[name] = np.ascontiguousarray(np.asarray(x))
    ids = a.pop("x")
    a["ids"] = np.ascontiguousarray(ids.reshape(G, P).T)
    a["table"] = np.concatenate([a.pop("L0_tok_emb_table"), a.pop("L0_tok_geo_table"), a.pop("L0_tok_visit_table")], axis=1)
    a["conv_taps"] = np.ascontiguousarray(a.pop("L0_attn_conv_w").T)
    a["scan_select"] = np.tile(np.repeat(np.eye(NR, dtype=np.float32)[:, :, None], P, axis=2), (3, 1, 1))
    a["eb1_columns"] = np.ascontiguousarray(a.pop("L0_ffn_eb1").T)
    a["eb2_columns"] = np.ascontiguousarray(a.pop("L0_ffn_eb2").reshape(E0 // 2, P).T)
    a["router_columns"] = np.ascontiguousarray(a.pop("L1_ffn_router_w").T)
    a["moe_b1_columns"] = np.ascontiguousarray(a.pop("L1_ffn_b1").reshape(E1 // 2, P).T)
    for n in ("q", "k"):
        a[f"w{n}_columns"] = np.ascontiguousarray(a.pop(f"L1_attn_W{n}").reshape(D, HEADS, HD).transpose(0, 2, 1)).reshape(D, D)
        a[f"b{n}_columns"] = np.ascontiguousarray(a.pop(f"L1_attn_b{n}").reshape(HEADS, HD).T).reshape(D)
    a["token_columns"] = np.ascontiguousarray(np.arange(L, dtype=np.float32).reshape(C, P).T)
    a["edge_numbers"] = np.arange(1, EDGES + 1, dtype=np.float32).reshape(1, EDGES)
    a["preference"] = np.arange(E1, 0, -1, dtype=np.float32)
    pick = np.repeat(np.eye(E1, dtype=np.float32).reshape(E1, E1 // 2, 2), D, axis=2)
    a["pick_parts"] = np.zeros((GATE_ROWS, E1 // 2, P), np.float32)
    for r in range(3):
        a["pick_parts"][r * PART_ROW:r * PART_ROW + E1] = pick
    t = np.arange(L)
    k = np.arange(L // 2 + 1)
    angle = 2 * np.pi / L * (t[:, None] * k[None, :] % L)
    cos, sin = np.cos(angle), np.sin(angle)
    root = L ** 0.5
    forward = np.concatenate([cos, -sin[:, 1:L // 2]], axis=1) / root
    weight = np.where((k == 0) | (k == L // 2), 1.0, 2.0)[:, None] * root / L
    inverse = np.concatenate([(weight * cos.T)[0:L // 2], (weight * cos.T)[L // 2:], -(weight * sin.T)[1:L // 2]])
    a["dft"] = np.ascontiguousarray(forward.reshape(C, P, L).transpose(1, 0, 2).astype(np.float32))
    a["idft"] = np.ascontiguousarray(inverse.reshape(C, P, L).transpose(1, 0, 2).astype(np.float32))
    a["stacked_identity"] = np.tile(np.eye(D, dtype=np.float32), (2, 1))
    a["identity"] = np.eye(P, dtype=np.float32)
    return a


def kernel(**inputs):
    import concourse.bacc as _bacc
    from concourse.bass_utils import run_bass_kernel_spmd as _run

    nc = _bacc.Bacc("TRN2", target_bir_lowering=False, num_devices=1)
    arrays = layouts(inputs)
    w = {n: nc.dram_tensor(f"in_{n}", a.shape, mybir.dt.from_np(a.dtype), kind="ExternalInput").ap() for n, a in arrays.items()}
    out = nc.dram_tensor("out", (SEQS, L, D), F32, kind="ExternalOutput").ap()
    program(nc, w, out)
    r = _run(nc, [{f"in_{n}": a for n, a in arrays.items()}], core_ids=[0])
    return r.results[0]["out"]
```

```python
from contextlib import ExitStack

import concourse.bass as bass
from concourse import mybir

F32 = mybir.dt.float32
BF16 = mybir.dt.bfloat16
I32 = mybir.dt.int32
ALU = mybir.AluOpType
ACT = mybir.ActivationFunctionType
AX = mybir.AxisListType

P = 128
SEQS, L, D = 32, 512, 64
C = L // P
G = SEQS * C
ITEMS = 25000
VISIT = 24
ROW = 2 * D + VISIT
DIN, DST, DTR = 128, 48, 4
CONV = 4
FD = 128
HEADS, HD = 8, 8
EDGES = 16384
EDGE_STEP = EDGES // SEQS
E0, E1 = 4, 8
ds = bass.ds


class Count:

    def __init__(self, base=0):
        self.base, self.n = base, 0

    def up(self):
        self.n += 1
        return 1

    @property
    def value(self):
        return self.base + self.n


def past(n):
    return n + 1


def arm(nc, sems):
    with nc.Block() as block:
        @block.sync
        def _(sp):
            for s in sems:
                sp.sem_inc(s, 1)


def renew(nc):
    with nc.Block() as block:
        @block.sync
        def _(sp):
            numbers = sorted(nc.released_uncleared_semaphores)
            sp.sem_clear(range(numbers[0], numbers[-1] + 1))


def rows3(tile, g0, n):
    return tile[:, ds(g0, n), :]


def layer_norm(nc, name, src, dst, eps, gamma=None, beta=None):
    W = 16
    steps = G // W
    with ExitStack() as ctx:
        sq = [ctx.enter_context(nc.sbuf_tensor(f"{name}_sq{i}", [P, W, D], F32)) for i in range(2)]
        total = ctx.enter_context(nc.sbuf_tensor(f"{name}_total", [P, G], F32))
        var = ctx.enter_context(nc.sbuf_tensor(f"{name}_var", [P, G], F32))
        rstd = ctx.enter_context(nc.sbuf_tensor(f"{name}_rstd", [P, G], F32))
        eps_col = ctx.enter_context(nc.sbuf_tensor(f"{name}_eps", [P, 1], F32))
        summed = ctx.enter_context(nc.semaphore(f"{name}_summed"))
        centred = ctx.enter_context(nc.semaphore(f"{name}_centred"))
        squared = ctx.enter_context(nc.semaphore(f"{name}_squared"))
        spread = ctx.enter_context(nc.semaphore(f"{name}_spread"))
        rooted = ctx.enter_context(nc.semaphore(f"{name}_rooted"))
        scaled = ctx.enter_context(nc.semaphore(f"{name}_scaled"))
        shifted = ctx.enter_context(nc.semaphore(f"{name}_shifted"))
        block = ctx.enter_context(nc.Block())

        def over(stat, g0, n):
            return stat[:, ds(g0, n)].unsqueeze(2).to_broadcast([P, n, D])

        @block.vector
        def _(vec):
            vec.memset(eps_col[:], eps).then_inc(spread, 1)
            with vec.Fori(0, steps // 2) as i:
                for p in range(2):
                    k = i * 2 + p
                    vec.tensor_reduce(total[:, ds(k * W, W)], rows3(src, k * W, W), AX.X, ALU.add).then_inc(summed, 1)
                for p in range(2):
                    k = i * 2 + p
                    vec.wait_ge(summed, k + 1)
                    vec.scalar_tensor_tensor(rows3(dst, k * W, W), over(total, k * W, W), -1.0 / D,
                                             rows3(src, k * W, W), ALU.mult, ALU.add).then_inc(centred, 1)
                for p in range(2):
                    k = i * 2 + p
                    vec.wait_ge(squared, k + 1)
                    vec.tensor_reduce(var[:, ds(k * W, W)], sq[p][:], AX.X, ALU.add).then_inc(spread, 1)
            vec.wait_ge(rooted, 2)
            with vec.Fori(0, steps) as k:
                vec.wait_ge(centred, steps)
                vec.tensor_tensor(rows3(dst, k * W, W), rows3(dst, k * W, W), over(rstd, k * W, W),
                                  ALU.mult).then_inc(scaled, 1)
                if gamma is not None:
                    vec.wait_ge(scaled, k * 2 + 1)
                    vec.tensor_tensor(rows3(dst, k * W, W), rows3(dst, k * W, W),
                                      gamma[:].unsqueeze(1).to_broadcast([P, W, D]), ALU.mult).then_inc(scaled, 1)

        if gamma is not None:
            @block.gpsimd
            def _(pool):
                with pool.Fori(0, steps) as k:
                    pool.wait_ge(scaled, k * 2 + 2)
                    nc.gpsimd.tensor_tensor(rows3(dst, k * W, W), rows3(dst, k * W, W),
                                            beta[:].unsqueeze(1).to_broadcast([P, W, D]), ALU.add).then_inc(shifted, 1)

        @block.scalar
        def _(act):
            with act.Fori(0, steps // 2) as i:
                for p in range(2):
                    k = i * 2 + p
                    act.wait_ge(centred, k + 1)
                    act.wait_ge(spread, i * 2 + 1)
                    nc.scalar.activation(sq[p][:], rows3(dst, k * W, W), ACT.Square).then_inc(squared, 1)
            act.wait_ge(spread, steps + 1)
            nc.scalar.activation(rstd[:], var[:], ACT.Ln, scale=1.0 / D, bias=eps_col[:]).then_inc(rooted, 1)
            act.wait_ge(rooted, 1)
            nc.scalar.activation(rstd[:], rstd[:], ACT.Exp, scale=-0.5).then_inc(rooted, 1)


def load(nc, name, pairs, gpsimd_pairs=()):
    with ExitStack() as ctx:
        landed = ctx.enter_context(nc.semaphore(f"{name}_landed"))
        block = ctx.enter_context(nc.Block())

        @block.sync
        def _(sp):
            for dst, src in pairs[::2]:
                sp.dma_start(dst, src).then_inc(landed, 16)
            sp.wait_ge(landed, 16 * len(pairs))

        @block.scalar
        def _(act):
            for dst, src in pairs[1::2]:
                act.dma_start(dst, src).then_inc(landed, 16)


def column(vector):
    return vector.rearrange("(n o) -> n o", o=1)


def row(vector):
    return vector.rearrange("(o n) -> o n", o=1)


def spread_row(vector):
    return row(vector).to_broadcast([P, vector.shape[0]])


class Slots:

    def __init__(self, unroll, first, start, stop, last, count=SEQS):
        self.unroll, self.first, self.start, self.last, self.count = unroll, first, start, last, count
        self.turns = (stop - start) // unroll

    def run(self, eng, slot):
        for k in range(self.first, self.start):
            slot(0, k)
        with eng.Fori(0, self.turns) as i:
            for k in range(self.start, self.start + self.unroll):
                slot(i, k)
        for k in range(self.start + self.turns * self.unroll, self.last):
            slot(0, k)

    def live(self, i, k):
        return not isinstance(i, int) or 0 <= k < self.count

    def before(self, i, k):
        return max(0, min(k, self.count)) if isinstance(i, int) else i * self.unroll + k

    def through(self, i, k):
        return self.before(i, k + 1)

    def round_of(self, i, k):
        return i + k // self.unroll


def wait(eng, sem, n):
    if not isinstance(n, int) or n > 0:
        eng.wait_ge(sem, past(n))


def embed(nc, w, H):
    with ExitStack() as ctx:
        def sb(name, shape, dt=F32):
            return ctx.enter_context(nc.sbuf_tensor(name, shape, dt))

        ids = sb("ids", [P, G], I32)
        rows_at = sb("rows_at", [P, G], I32)
        keep = sb("keep", [P, G])
        emb = sb("emb", [P, G, D])
        w_pair = sb("w_pair", [P, P])
        w_visit = sb("w_visit", [VISIT, D])
        b_pair = sb("b_pair", [P, 1])
        b_visit = sb("b_visit", [D, 1])
        fuse_a = sb("fuse_a", [P, D])
        fuse_b = sb("fuse_b", [D + 1, D])
        gamma = sb("tok_gamma", [P, D])
        beta = sb("tok_beta", [P, D])
        at = [sb(f"at{p}", [P, C], I32) for p in range(2)]
        rows = [sb(f"rows{p}", [P, C, ROW]) for p in range(2)]
        pairT = [sb(f"pairT{p}", [P, L]) for p in range(2)]
        visitT = [sb(f"visitT{p}", [VISIT, L]) for p in range(2)]
        pair_h = [sb(f"pair_h{p}", [P, L]) for p in range(2)]
        visit_h = [sb(f"visit_h{p}", [D + 1, L]) for p in range(2)]
        target = [sb(f"target{p}", [P, EDGE_STEP], I32) for p in range(2)]
        wrapped, fixed = sb("wrapped", [P, EDGE_STEP]), sb("fixed", [P, EDGE_STEP])
        number = sb("number", [P, EDGE_STEP])
        token = sb("token", [P, C])
        match = sb("match", [P, C, EDGE_STEP])

        with ExitStack() as zero:
            zeroed = zero.enter_context(nc.semaphore("tok_zeroed"))
            block = zero.enter_context(nc.Block())

            @block.vector
            def _(vec):
                vec.memset(w_pair[:], 0.0).then_inc(zeroed, 1)
                for p in range(2):
                    vec.memset(visit_h[p][D:D + 1, :], 1.0).then_inc(zeroed, 1)

        load(nc, "tok_w", [
            (token[:], w["token_columns"]), (number[:], w["edge_numbers"].to_broadcast([P, EDGE_STEP])),
            (ids[:], w["ids"]), (w_pair[0:D, 0:D], w["L0_tok_w_item"]), (w_pair[D:P, D:P], w["L0_tok_w_geo"]),
            (w_visit[:], w["L0_tok_w_visit"]), (b_pair[0:D, :], column(w["L0_tok_b_item"])),
            (b_pair[D:P, :], column(w["L0_tok_b_geo"])), (b_visit[:], column(w["L0_tok_b_visit"])),
            (fuse_a[:], w["L0_tok_w_fuse"][0:P, :]), (fuse_b[0:D, :], w["L0_tok_w_fuse"][P:P + D, :]),
            (fuse_b[D:D + 1, :], row(w["L0_tok_b_fuse"])),
            (gamma[:], spread_row(w["L0_tok_ln_gamma"])), (beta[:], spread_row(w["L0_tok_ln_beta"]))])

        with ExitStack() as run:
            sems = []

            def sem(name):
                sems.append(run.enter_context(nc.semaphore(name)))
                return sems[-1]

            ps_pair = run.enter_context(nc.psum_tensor("ps_pair", [P, L], F32))
            ps_visit = run.enter_context(nc.psum_tensor("ps_visit", [VISIT, L], F32))
            ps_ph = run.enter_context(nc.psum_tensor("ps_ph", [P, L], F32))
            ps_vh = run.enter_context(nc.psum_tensor("ps_vh", [D, L], F32))
            ps_fuse = run.enter_context(nc.psum_tensor("ps_fuse", [P, C, D], F32))
            passed, ids_ready, at_ready = sem("tok_passed"), sem("ids_ready"), sem("at_ready")
            gathered = w["gathered"][0:2]
            turned, emb_kept = sem("turned"), sem("emb_kept")
            pair_copied, visit_copied = sem("pair_copied"), sem("visit_copied")
            projected, gelus, fused, stored = sem("projected"), sem("gelus"), sem("fused"), sem("stored")
            landed = [sem(f"edge_landed{p}") for p in range(2)]
            fix_step, matched, shrunk = sem("edge_fix_step"), sem("edge_matched"), sem("edge_shrunk")
            arm(nc, sems)
            block = run.enter_context(nc.Block())
            pipe = Slots(2, -1, 2, SEQS - 1, SEQS + 1)
            live, before, through = pipe.live, pipe.before, pipe.through

            @block.gpsimd
            def _(pool):
                def slot(i, k):
                    if live(i, k + 1):
                        p = (k + 1) % 2
                        wait(pool, turned, before(i, k))
                        wait(pool, emb_kept, before(i, k))
                        nc.gpsimd.tensor_copy(at[p][:], rows_at[:, ds(before(i, k + 1) * C, C)]).then_inc(at_ready, 1)
                        wait(pool, at_ready, through(i, k + 1))
                        pool.sem_inc(passed, 1)
                        for c in range(C):
                            nc.gpsimd.indirect_dma_start(
                                out=rows[p][:, c, :], out_offset=None, in_=w["table"],
                                in_offset=bass.IndirectOffsetOnAxis(ap=at[p][:, c:c + 1], axis=0),
                            ).then_inc(gathered[p], 16)

                pool.wait_ge(ids_ready, past(1))
                pipe.run(pool, slot)

            @block.tensor
            def _(pe):
                def slot(i, k):
                    p, q = k % 2, (k + 1) % 2
                    if live(i, k):
                        wait(pe, pair_copied, through(i, k))
                        wait(pe, visit_copied, through(i, k))
                        wait(pe, gelus, before(i, k))
                        pe.sem_inc(passed, 1)
                        nc.tensor.matmul(ps_ph[:], w_pair[:], pairT[p][:], start=True, stop=True)
                        nc.tensor.matmul(ps_vh[:], w_visit[:], visitT[p][:], start=True, stop=True).then_inc(projected, 1)
                    if live(i, k + 1):
                        pe.wait_ge(gathered[q], pipe.round_of(i, k + 1) * (16 * C) + 16 * C)
                        pe.sem_inc(passed, 1)
                        for c in range(C):
                            nc.tensor.transpose(ps_pair[:, c * P:(c + 1) * P], rows[q][:, c, 0:P], w["ident"][:])
                        for c in range(C):
                            last = nc.tensor.transpose(ps_visit[:, c * P:(c + 1) * P], rows[q][:, c, P:ROW],
                                                       w["ident"][:])
                        last.then_inc(turned, 1)
                    if live(i, k - 1):
                        wait(pe, gelus, through(i, k - 1))
                        wait(pe, stored, before(i, k - 1))
                        pe.sem_inc(passed, 1)
                        for c in range(C):
                            nc.tensor.matmul(ps_fuse[:, c, :], pair_h[q][:, c * P:(c + 1) * P], fuse_a[:],
                                             start=True, stop=False)
                            last = nc.tensor.matmul(ps_fuse[:, c, :], visit_h[q][:, c * P:(c + 1) * P], fuse_b[:],
                                                    start=False, stop=True)
                        last.then_inc(fused, 1)

                pipe.run(pe, slot)

            @block.vector
            def _(vec):
                def search(i, k):
                    n, p = before(i, k), k % 2
                    wait(vec, landed[p], (pipe.round_of(i, k) + 1) * 16)
                    wait(vec, matched, n * C)
                    vec.tensor_scalar(wrapped[:], target[p][:], 0.0, float(L), ALU.is_lt, ALU.mult).then_inc(fix_step, 1)
                    wait(vec, fix_step, n * 2 + 1)
                    vec.tensor_tensor(fixed[:], target[p][:], wrapped[:], ALU.add).then_inc(fix_step, 1)
                    wait(vec, fix_step, n * 2 + 2)
                    wait(vec, shrunk, n)
                    for c in range(C):
                        vec.scalar_tensor_tensor(match[:, c, :], fixed[:], token[:, c:c + 1], number[:],
                                                 ALU.is_equal, ALU.mult).then_inc(matched, 1)
                    wait(vec, matched, n * C + C)
                    vec.tensor_reduce(w["last_of"][:, ds(n * C, C)], match[:], AX.X, ALU.max).then_inc(shrunk, 1)

                def slot(i, k):
                    if live(i, k + 1):
                        q = (k + 1) % 2
                        wait(vec, turned, through(i, k + 1))
                        wait(vec, projected, before(i, k))
                        nc.vector.tensor_copy(pairT[q][:], ps_pair[:]).then_inc(pair_copied, 1)
                        nc.vector.tensor_copy(rows3(emb, before(i, k + 1) * C, C), rows[q][:, :, 0:D]).then_inc(emb_kept, 1)
                    if live(i, k):
                        search(i, k)

                vec.tensor_scalar(rows_at[:], ids[:], 0.0, float(ITEMS), ALU.max, ALU.min).then_inc(ids_ready, 1)
                vec.tensor_scalar(keep[:], ids[:], 0.0, 0.1, ALU.not_equal, ALU.mult).then_inc(ids_ready, 1)
                pipe.run(vec, slot)

            @block.scalar
            def _(act):
                def slot(i, k):
                    p, q = k % 2, (k + 1) % 2
                    if live(i, k):
                        wait(act, projected, through(i, k))
                        wait(act, fused, before(i, k - 1))
                        nc.scalar.activation(pair_h[p][:], ps_ph[:], ACT.Gelu, bias=b_pair[:])
                        nc.scalar.activation(visit_h[p][0:D, :], ps_vh[:], ACT.Gelu, bias=b_visit[:]).then_inc(gelus, 1)
                    if live(i, k + 1):
                        wait(act, turned, through(i, k + 1))
                        nc.scalar.activation(visitT[q][:], ps_visit[:], ACT.Copy).then_inc(visit_copied, 1)
                    if live(i, k - 1):
                        wait(act, fused, through(i, k - 1))
                        act.sem_inc(passed, 1)
                        nc.scalar.activation(rows3(H, before(i, k - 1) * C, C), ps_fuse[:], ACT.Gelu).then_inc(stored, 1)

                pipe.run(act, slot)

            @block.sync
            def _(sp):
                def slot(i, k):
                    if live(i, k + 1):
                        p = (k + 1) % 2
                        wait(sp, matched, before(i, k) * C)
                        sp.sem_inc(passed, 1)
                        edges = ds(before(i, k + 1) * EDGE_STEP, EDGE_STEP)
                        sp.dma_start(target[p][:], w["L1_attn_edge_index"][1:2, edges].to_broadcast([P, EDGE_STEP])
                                     ).then_inc(landed[p], 16)

                pipe.run(sp, slot)

        layer_norm(nc, "tok_ln", H, H, 1e-5, gamma, beta)

        with ExitStack() as run:
            masked = run.enter_context(nc.semaphore("tok_masked"))
            block = run.enter_context(nc.Block())

            @block.vector
            def _(vec):
                W = 16
                with vec.Fori(0, G // W) as k:
                    vec.tensor_tensor(rows3(H, k * W, W), rows3(H, k * W, W),
                                      keep[:, ds(k * W, W)].unsqueeze(2).to_broadcast([P, W, D]),
                                      ALU.mult).then_inc(masked, 1)
                    vec.wait_ge(masked, k * 2 + 1)
                    vec.tensor_tensor(rows3(H, k * W, W), rows3(H, k * W, W), rows3(emb, k * W, W),
                                      ALU.add).then_inc(masked, 1)


def move(nc, name, dst, src):
    with ExitStack() as ctx:
        moved = ctx.enter_context(nc.semaphore(f"{name}_moved"))
        block = ctx.enter_context(nc.Block())

        @block.sync
        def _(sp):
            sp.dma_start(dst, src).then_inc(moved, 16)
            sp.wait_ge(moved, 16)


def clear(nc, name, tile):
    with ExitStack() as ctx:
        cleared = ctx.enter_context(nc.semaphore(f"{name}_cleared"))
        block = ctx.enter_context(nc.Block())

        @block.vector
        def _(vec):
            vec.memset(tile, 0.0).then_inc(cleared, 1)


def mamba_inputs(nc, w, H, X, scr):
    with ExitStack() as ctx:
        def sb(name, shape, dt=F32):
            return ctx.enter_context(nc.sbuf_tensor(name, shape, dt))

        T = sb("pre_T", [P, G, D])
        norms = [sb(f"pre_{n}", [P, D]) for n in ("g1", "b1", "g2", "b2")]
        w_in = sb("pre_w_in", [D, 2 * DIN])
        w_bc = sb("pre_w_bc", [DIN, 2 * DST])
        w_dtin = sb("pre_w_dtin", [DIN, DTR])
        w_dt = sb("pre_w_dt", [DTR, DIN])
        taps = sb("pre_taps", [DIN, CONV])
        conv_b = sb("pre_conv_b", [DIN, 1])
        dt_b = sb("pre_dt_b", [DIN, 1])
        load(nc, "pre_w", [
            (norms[0][:], spread_row(w["L0_attn_ln1_g"])), (norms[1][:], spread_row(w["L0_attn_ln1_b"])),
            (norms[2][:], spread_row(w["L0_attn_mln_g"])), (norms[3][:], spread_row(w["L0_attn_mln_b"])),
            (w_in[:], w["L0_attn_w_in"]), (w_bc[:], w["L0_attn_w_xproj"][:, DTR:]),
            (w_dtin[:], w["L0_attn_w_xproj"][:, 0:DTR]), (w_dt[:], w["L0_attn_w_dt"]),
            (taps[:], w["conv_taps"]), (conv_b[:], column(w["L0_attn_conv_b"])),
            (dt_b[:], column(w["L0_attn_b_dt"]))])
        layer_norm(nc, "ln_x", H, X, 1e-5)
        layer_norm(nc, "ln_1", X, T, 1e-3, norms[0], norms[1])
        layer_norm(nc, "ln_2", T, T, 1e-3, norms[2], norms[3])

        s = Stage(nc, ctx, "pre")
        cur = s.two("cur", [P, C, D])
        mT = s.one("mT", [D, L])
        conv = s.one("conv", [DIN, L])
        u, gate, delta = s.two("u", [DIN, L]), s.two("gate", [DIN, L]), s.two("delta", [DIN, L])
        parts = s.two("parts", [2 * DST, 3, L], BF16)
        rest, dts = s.one("rest", [2 * DST, L]), s.one("dts", [DTR, L])
        size, soft = s.one("size", [DIN, L]), s.one("soft", [DIN, L])
        ps_m = s.bank("ps_m", [D, L])
        ps_xm, ps_res = s.banks("ps_xm", [DIN, L]), s.banks("ps_res", [DIN, L])
        ps_bc, ps_dt, ps_delta = s.bank("ps_bc", [2 * DST, L]), s.bank("ps_dt", [DTR, L]), s.bank("ps_delta", [DIN, L])
        passed, cur_ready, turned, m_copied = (s.counter(n) for n in ("passed", "cur_ready", "turned", "m_copied"))
        projected, tap_done, convolved = s.counter("projected"), s.counter("tap_done"), s.counter("convolved")
        gated, u_ready, xdbl, dt_copied = (s.counter(n) for n in ("gated", "u_ready", "xdbl", "dt_copied"))
        dt_spread, soft_step, softened = s.counter("dt_spread"), s.counter("soft_step"), s.counter("softened")
        soft_max, delta_ready = s.counter("soft_max"), s.counter("delta_ready")
        high, rest_ready, mid, split = (s.counter(n) for n in ("high", "rest_ready", "mid", "split"))
        in_dram = {"gate_u": s.counters("gate_u_saved"), "bc": s.counters("bc_saved"), "delta": s.counters("delta_saved")}
        block = s.block()
        TRANSFERS = {"gate_u": 2, "bc": 1, "delta": 1}
        pipe = Slots(2, -1, 3, SEQS - 1, SEQS + 2)
        live, before, through = pipe.live, pipe.before, pipe.through

        def is_saved(eng, what, i, k):
            wait(eng, in_dram[what][k % 2], pipe.round_of(i, k) * (16 * TRANSFERS[what]))

        @block.gpsimd
        def _(pool):
            def slot(i, k):
                if live(i, k + 1):
                    wait(pool, turned, before(i, k))
                    nc.gpsimd.tensor_copy(cur[(k + 1) % 2][:], rows3(T, before(i, k + 1) * C, C)).then_inc(cur_ready, 1)

            pipe.run(pool, slot)

        @block.tensor
        def _(pe):
            def slot(i, k):
                if live(i, k + 1):
                    q = (k + 1) % 2
                    wait(pe, cur_ready, through(i, k + 1))
                    wait(pe, m_copied, before(i, k + 1))
                    pe.sem_inc(passed, 1)
                    for c in range(C):
                        last = nc.tensor.transpose(ps_m[:, c * P:(c + 1) * P], cur[q][:, c, :], w["ident"][:])
                    last.then_inc(turned, 1)
                if live(i, k - 1):
                    wait(pe, u_ready, through(i, k - 1))
                    wait(pe, dt_copied, before(i, k - 1))
                    wait(pe, rest_ready, before(i, k - 1))
                    pe.sem_inc(passed, 1)
                    nc.tensor.matmul(ps_dt[:], w_dtin[:], u[(k - 1) % 2][:], start=True, stop=True)
                    nc.tensor.matmul(ps_bc[:], w_bc[:], u[(k - 1) % 2][:], start=True, stop=True).then_inc(xdbl, 1)
                if live(i, k + 1):
                    wait(pe, m_copied, through(i, k + 1))
                    wait(pe, convolved, before(i, k))
                    wait(pe, gated, before(i, k))
                    pe.sem_inc(passed, 1)
                    nc.tensor.matmul(ps_xm[q][:], w_in[:, 0:DIN], mT[:], start=True, stop=True)
                    nc.tensor.matmul(ps_res[q][:], w_in[:, DIN:], mT[:], start=True, stop=True).then_inc(projected, 1)
                if live(i, k - 1):
                    wait(pe, dt_copied, through(i, k - 1))
                    wait(pe, soft_step, before(i, k - 1) * 2)
                    wait(pe, soft_max, before(i, k - 1))
                    pe.sem_inc(passed, 1)
                    nc.tensor.matmul(ps_delta[:], w_dt[:], dts[:], start=True, stop=True).then_inc(dt_spread, 1)

            pipe.run(pe, slot)

        @block.vector
        def _(vec):
            def convolve(i, k):
                wait(vec, projected, through(i, k))
                wait(vec, u_ready, before(i, k))
                step = Count(before(i, k) * (CONV - 1))
                xm = ps_xm[k % 2]
                vec.tensor_scalar(conv[:], xm[:], taps[:, CONV - 1:CONV], None, ALU.mult).then_inc(tap_done, step.up())
                for tap in range(CONV - 2, -1, -1):
                    lag = CONV - 1 - tap
                    wait(vec, tap_done, step.value)
                    done = vec.scalar_tensor_tensor(conv[:, lag:], xm[:, 0:L - lag], taps[:, tap:tap + 1],
                                                    conv[:, lag:], ALU.mult, ALU.add)
                    if tap:
                        done.then_inc(tap_done, step.up())
                    else:
                        done.then_inc(convolved, 1)

            def slot(i, k):
                if live(i, k - 2):
                    wait(vec, dt_spread, through(i, k - 2))
                    wait(vec, delta_ready, before(i, k - 2))
                    wait(vec, soft_step, before(i, k - 2) * 2 + 1)
                    vec.tensor_scalar(size[:], ps_delta[:], dt_b[:], 0.0, ALU.add, ALU.max).then_inc(soft_max, 1)
                if live(i, k + 1):
                    wait(vec, turned, through(i, k + 1))
                    wait(vec, projected, before(i, k + 1))
                    nc.vector.tensor_copy(mT[:], ps_m[:]).then_inc(m_copied, 1)
                if live(i, k):
                    convolve(i, k)
                if live(i, k - 1):
                    p = (k - 1) % 2
                    wait(vec, xdbl, through(i, k - 1))
                    wait(vec, dt_spread, before(i, k - 1))
                    nc.vector.tensor_copy(dts[:], ps_dt[:]).then_inc(dt_copied, 1)
                if live(i, k - 2):
                    wait(vec, softened, through(i, k - 2))
                    wait(vec, soft_max, through(i, k - 2))
                    is_saved(vec, "delta", i, k - 2)
                    vec.tensor_tensor(delta[k % 2][:], size[:], soft[:], ALU.add).then_inc(delta_ready, 1)
                if live(i, k - 1):
                    wait(vec, high, through(i, k - 1))
                    wait(vec, split, before(i, k - 1))
                    vec.tensor_tensor(rest[:], ps_bc[:], parts[p][:, 0, :], ALU.subtract).then_inc(rest_ready, 1)
                    wait(vec, mid, through(i, k - 1))
                    vec.tensor_tensor(parts[p][:, 2, :], rest[:], parts[p][:, 1, :], ALU.subtract).then_inc(split, 1)

            pipe.run(vec, slot)

        @block.scalar
        def _(act):
            def slot(i, k):
                if live(i, k - 2):
                    wait(act, dt_spread, through(i, k - 2))
                    wait(act, delta_ready, before(i, k - 2))
                    step = Count(before(i, k - 2) * 2)
                    nc.scalar.activation(soft[:], ps_delta[:], ACT.Abs, bias=dt_b[:]).then_inc(soft_step, step.up())
                    wait(act, soft_step, step.value)
                    nc.scalar.activation(soft[:], soft[:], ACT.Exp, scale=-1.0).then_inc(soft_step, step.up())
                    wait(act, soft_step, step.value)
                    nc.scalar.activation(soft[:], soft[:], ACT.Ln, bias=1.0).then_inc(softened, 1)
                if live(i, k):
                    wait(act, projected, through(i, k))
                    is_saved(act, "gate_u", i, k)
                    nc.scalar.activation(gate[k % 2][:], ps_res[k % 2][:], ACT.Silu).then_inc(gated, 1)
                    wait(act, convolved, through(i, k))
                    wait(act, xdbl, before(i, k - 1))
                    nc.scalar.activation(u[k % 2][:], conv[:], ACT.Silu, bias=conv_b[:]).then_inc(u_ready, 1)
                if live(i, k - 1):
                    q = (k - 1) % 2
                    wait(act, xdbl, through(i, k - 1))
                    is_saved(act, "bc", i, k - 1)
                    nc.scalar.activation(parts[q][:, 0, :], ps_bc[:], ACT.Copy).then_inc(high, 1)
                    wait(act, rest_ready, through(i, k - 1))
                    nc.scalar.activation(parts[q][:, 1, :], rest[:], ACT.Copy).then_inc(mid, 1)

            pipe.run(act, slot)

        @block.sync
        def _(sp):
            def save(what, name, i, k, ready, tile):
                wait(sp, ready, through(i, k))
                sp.sem_inc(passed, 1)
                at = ds(before(i, k), 1)
                dst = scr[name][:, :, at, :] if name == "bc" else scr[name][:, at, :]
                sp.dma_start(dst, tile.unsqueeze(2 if name == "bc" else 1)).then_inc(in_dram[what][k % 2], 16)

            def slot(i, k):
                if live(i, k - 2):
                    save("delta", "delta", i, k - 2, delta_ready, delta[k % 2][:])
                if live(i, k):
                    save("gate_u", "gate", i, k, gated, gate[k % 2][:])
                    save("gate_u", "u", i, k, u_ready, u[k % 2][:])
                if live(i, k - 1):
                    save("bc", "bc", i, k - 1, split, parts[(k - 1) % 2][:])

            pipe.run(sp, slot)
            for what, sems in in_dram.items():
                for p in range(2):
                    sp.wait_ge(sems[p], past(16 * TRANSFERS[what] * (SEQS // 2)))


NR = 12
ROUNDS = DST // NR
PAIRS = SEQS // 2
AHEAD = 8
LOG_EPS = -27.631021115928547


def selective_scan(nc, w, X, scr):
    with ExitStack() as ctx:
        s = Stage(nc, ctx, "scan")
        GROUP = 3
        RING = 2 * GROUP
        A = s.one("A", [DIN, DST])
        skip, w_out = s.one("skip", [DIN, 1]), s.one("w_out", [DIN, D])
        sel_f = s.one("sel_f", [3 * NR, NR, P])
        sel = s.one("sel", [3 * NR, NR, P], BF16)
        ones, bias = s.one("ones", [P, L]), s.one("bias", [P, 1])
        load(nc, "scan_w", [(A[:], w["L0_attn_A_log"]), (skip[:], column(w["L0_attn_D"])),
                            (w_out[:], w["L0_attn_w_out"]), (sel_f[:], w["scan_select"])])
        pair_shape = [DIN, 2, L]
        delta, u, gate = s.two("delta", pair_shape), s.two("u", pair_shape), s.one("gate", pair_shape)
        bc = s.two("bc", [3 * NR, 2 * ROUNDS, 2, L], BF16)
        du, after = s.two("du", pair_shape), s.two("after", pair_shape)
        decay = [s.one(f"decay{k}", pair_shape) for k in range(RING)]
        guard = [s.one(f"guard{k}", pair_shape) for k in range(RING)]
        h = s.two("h", pair_shape)
        hg = [s.one(f"hg{k}", pair_shape) for k in range(3)]
        ch, y = s.two("ch", pair_shape), s.one("y", pair_shape)
        ps_b = s.banks("ps_b", pair_shape)
        ps_c, ps_y = s.bank("ps_c", pair_shape), s.bank("ps_y", pair_shape)
        ps_o = ps_c[:, 0, :].rearrange("p (g d) -> p g d", d=D)

        passed, a_step, loaded, gate_in = (s.counter(n) for n in ("passed", "a_step", "loaded", "gate_in"))
        prepared, b_ready, c_ready = s.counter("prepared"), s.counter("b_ready"), s.counter("c_ready")
        decayed, guarded, fed = s.counter("decayed"), s.counter("guarded"), s.counter("fed")
        scanned, multiplied, weighted, summed = (s.counter(n) for n in ("scanned", "multiplied", "weighted", "summed"))
        y_taken, y_gated, projected, added = (s.counter(n) for n in ("y_taken", "y_gated", "projected", "added"))
        block = s.block()
        pipe = Slots(2, -1, 1, PAIRS - 1, PAIRS + 1, PAIRS)
        live, before, through = pipe.live, pipe.before, pipe.through
        LOADS = 2 + 6
        A_STEPS = 6
        OUTPUT_AT = 5

        def done(n):
            return past(n + (AHEAD + 1))

        def item(i, k, j, r):
            return before(i, k) * DST + j * NR + r

        @block.sync
        def _(sp):
            def slot(i, k):
                if live(i, k + 1):
                    p, pair = (k + 1) % 2, before(i, k + 1)
                    wait(sp, y_taken, before(i, k))
                    wait(sp, loaded, pair * (16 * LOADS))
                    sp.sem_inc(passed, 1)
                    sp.dma_start(delta[p][:], scr["delta"][:, ds(pair * 2, 2), :]).then_inc(loaded, 16)
                    sp.dma_start(u[p][:], scr["u"][:, ds(pair * 2, 2), :]).then_inc(loaded, 16)
                    for part in range(3):
                        for half in range(2):
                            src = scr["bc"][half * DST:(half + 1) * DST, part, ds(pair * 2, 2), :]
                            sp.dma_start(bc[p][part * NR:(part + 1) * NR, half * ROUNDS:(half + 1) * ROUNDS],
                                         src.rearrange("(j r) s t -> r j (s t)", r=NR)
                                         .rearrange("r j (s t) -> r j s t", s=2)).then_inc(loaded, 16)
                if live(i, k):
                    wait(sp, y_gated, before(i, k))
                    sp.sem_inc(passed, 1)
                    sp.dma_start(gate[:], scr["gate"][:, ds(before(i, k) * 2, 2), :]).then_inc(gate_in, 16)

            pipe.run(sp, slot)

        @block.tensor
        def _(pe):
            def spread(dst, p, r, j, half):
                for s in range(2):
                    last = nc.tensor.matmul(dst[:, s, :], sel[:, r, :], bc[p][:, ds(half * ROUNDS + j, 1), s, :],
                                            start=True, stop=True)
                return last

            def output(i, k):
                wait(pe, y_gated, through(i, k))
                for g in range(2 * C):
                    last = nc.tensor.matmul(ps_o[:, g, :], y[:, g // C, (g % C) * P:(g % C + 1) * P], w_out[:],
                                            start=True, stop=True)
                last.then_inc(projected, 1)

            def slot(i, k):
                p = k % 2

                def b_item(r, j):
                    pe.wait_ge(scanned, done(item(i, k, j, r) - 2))
                    pe.sem_inc(passed, 1)
                    spread(ps_b[r % 2], p, r, j, 0).then_inc(b_ready, 1)

                def c_item(r, j):
                    pe.wait_ge(weighted, done(item(i, k, j, r) - 1))
                    pe.sem_inc(passed, 1)
                    spread(ps_c, p, r, j, 1).then_inc(c_ready, 1)

                def y_item(r, j, first=False, final=False):
                    pe.wait_ge(weighted, done(item(i, k, j, r)))
                    for s in range(2):
                        last = nc.tensor.matmul(ps_y[:, s, :], w["ident"][:], ch[r % 2][:, s, :],
                                                start=first, stop=final)
                    last.then_inc(summed, 1)

                def step(r, j, first_round=False, last_round=False):
                    if r < NR - 1:
                        b_item(r + 1, j)
                    elif not last_round:
                        b_item(0, j + 1)
                    if first_round and r == OUTPUT_AT and live(i, k - 1):
                        pe.wait_ge(weighted, done(item(i, k, j, r) - 2))
                        output(i, k - 1)
                        wait(pe, added, through(i, k - 1))
                    if not (first_round and r < 1):
                        c_item((r - 1) % NR, j if r >= 1 else j - 1)
                    if not (first_round and r < 2):
                        y_item((r - 2) % NR, j if r >= 2 else j - 1, first=first_round and r == 2)

                if live(i, k):
                    for r in range(NR):
                        if r == 2:
                            wait(pe, y_taken, before(i, k))
                        step(r, 0, first_round=True)
                    with pe.Fori(1, ROUNDS - 1) as j:
                        for r in range(NR):
                            step(r, j)
                    for r in range(NR):
                        step(r, ROUNDS - 1, last_round=True)
                    c_item(NR - 1, ROUNDS - 1)
                    y_item(NR - 2, ROUNDS - 1)
                if live(i, k + 1):
                    pe.wait_ge(loaded, past(through(i, k + 1) * (16 * LOADS)))
                    pe.wait_ge(scanned, done(item(i, k + 1, 0, 0) - 2))
                    pe.sem_inc(passed, 1)
                    spread(ps_b[0], (k + 1) % 2, 0, 0, 0).then_inc(b_ready, 1)
                if live(i, k):
                    y_item(NR - 1, ROUNDS - 1, final=True)
                elif live(i, k - 1):
                    pe.wait_ge(weighted, done(before(i, k) * DST - 1))
                    output(i, k - 1)

            pe.sem_inc(b_ready, AHEAD)
            pe.sem_inc(c_ready, AHEAD)
            pe.sem_inc(summed, AHEAD)
            pe.wait_ge(a_step, past(A_STEPS))
            pipe.run(pe, slot)

        @block.scalar
        def _(act):
            def slot(i, k):
                if live(i, k):
                    act.wait_ge(loaded, past(through(i, k) * (16 * LOADS)))
                    act.wait_ge(prepared, past(through(i, k) * 3))
                    with act.Fori(0, ROUNDS) as j:
                        for r0 in range(0, NR, GROUP):
                            for r in range(r0, r0 + GROUP):
                                n = item(i, k, j, r)
                                act.wait_ge(scanned, done(n - RING))
                                act.sem_inc(passed, 1)
                                nc.scalar.activation(decay[r % RING][:, :, 1:], delta[k % 2][:, :, 1:], ACT.Exp,
                                                     scale=A[:, ds(j * NR + r, 1)]).then_inc(decayed, 1)
                            for r in range(r0, r0 + GROUP):
                                n = item(i, k, j, r)
                                act.wait_ge(multiplied, done(n - RING))
                                act.sem_inc(passed, 1)
                                nc.scalar.activation(guard[r % RING][:], after[k % 2][:], ACT.Sigmoid,
                                                     scale=A[:, ds(j * NR + r, 1)], bias=bias[:]).then_inc(guarded, 1)

            act.sem_inc(decayed, AHEAD)
            act.sem_inc(guarded, AHEAD)
            nc.scalar.activation(A[:], A[:], ACT.Exp).then_inc(a_step, 1)
            act.wait_ge(a_step, past(A_STEPS))
            pipe.run(act, slot)

        @block.gpsimd
        def _(pool):
            def multiply(i, k, j, r):
                n = item(i, k, j, r)
                pool.wait_ge(guarded, done(n))
                pool.wait_ge(weighted, done(n - 3))
                pool.wait_ge(scanned, done(n))
                nc.gpsimd.tensor_tensor(hg[r % 3][:], h[r % 2][:], guard[r % RING][:], ALU.mult).then_inc(multiplied, 1)

            def gate_output(i, k):
                wait(pool, y_taken, through(i, k))
                wait(pool, gate_in, through(i, k) * 16)
                nc.gpsimd.tensor_tensor(y[:], y[:], gate[:], ALU.mult).then_inc(y_gated, 1)

            def slot(i, k):
                if live(i, k):
                    for r in range(NR):
                        multiply(i, k, 0, r)
                        if r == 1 and live(i, k - 1):
                            gate_output(i, k - 1)
                    with pool.Fori(1, ROUNDS) as j:
                        for r in range(NR):
                            multiply(i, k, j, r)
                elif live(i, k - 1):
                    gate_output(i, k - 1)

            pool.sem_inc(multiplied, AHEAD)
            pipe.run(pool, slot)

        @block.vector
        def _(vec):
            def prepare(i, k):
                p = k % 2
                vec.wait_ge(loaded, past(through(i, k) * (16 * LOADS)))
                vec.wait_ge(guarded, done(before(i, k - 1) * DST - 1))
                vec.wait_ge(fed, done(before(i, k - 1) * DST - 1))
                for s in range(2):
                    vec.tensor_tensor_scan(after[p][:, s, L - 2::-1], ones[:, 0:L - 1], delta[p][:, s, L - 1:0:-1],
                                           0.0, ALU.mult, ALU.add).then_inc(prepared, 1)
                vec.tensor_tensor(du[p][:], delta[p][:], u[p][:], ALU.mult).then_inc(prepared, 1)

            def take_y(i, k):
                vec.wait_ge(summed, done(through(i, k) * DST - 1))
                wait(vec, projected, before(i, k))
                vec.scalar_tensor_tensor(y[:], u[k % 2][:], skip[:], ps_y[:], ALU.mult, ALU.add).then_inc(y_taken, 1)

            def add_output(i, k):
                wait(vec, projected, through(i, k))
                pair = before(i, k)
                vec.tensor_tensor(rows3(X, pair * (2 * C), 2 * C), rows3(X, pair * (2 * C), 2 * C), ps_o,
                                  ALU.add).then_inc(added, 1)

            def slot(i, k):
                def feed(r, j):
                    vec.wait_ge(b_ready, done(item(i, k, j, r)))
                    vec.tensor_tensor(ps_b[r % 2][:], du[k % 2][:], ps_b[r % 2][:], ALU.mult).then_inc(fed, 1)

                def scan(r, j):
                    n = item(i, k, j, r)
                    vec.wait_ge(decayed, done(n))
                    vec.wait_ge(multiplied, done(n - 2))
                    vec.wait_ge(fed, done(n))
                    vec.tensor_tensor_scan(h[r % 2][:].rearrange("p s t -> p (s t)"),
                                           decay[r % RING][:].rearrange("p s t -> p (s t)"),
                                           ps_b[r % 2][:].rearrange("p s t -> p (s t)"),
                                           0.0, ALU.mult, ALU.add).then_inc(scanned, 1)

                def weight(r, j):
                    n = item(i, k, j, r)
                    vec.wait_ge(multiplied, done(n))
                    vec.wait_ge(c_ready, done(n))
                    vec.wait_ge(summed, done(n - 2))
                    vec.tensor_tensor(ch[r % 2][:], hg[r % 3][:], ps_c[:], ALU.mult).then_inc(weighted, 1)

                if live(i, k):
                    vec.wait_ge(prepared, past(through(i, k) * 3))
                    for r in range(NR):
                        feed(r, 0)
                        if r >= 2:
                            weight(r - 2, 0)
                        scan(r, 0)
                        if live(i, k - 1):
                            if r == 1:
                                take_y(i, k - 1)
                            if r == OUTPUT_AT:
                                add_output(i, k - 1)
                    with vec.Fori(1, ROUNDS - 1) as j:
                        for r in range(NR):
                            feed(r, j)
                            weight((r - 2) % NR, j if r >= 2 else j - 1)
                            scan(r, j)
                if live(i, k + 1):
                    prepare(i, k + 1)
                if live(i, k):
                    j = ROUNDS - 1
                    for r in range(NR):
                        feed(r, j)
                        weight((r - 2) % NR, j if r >= 2 else j - 1)
                        scan(r, j)
                    weight(NR - 2, ROUNDS - 1)
                    weight(NR - 1, ROUNDS - 1)
                elif live(i, k - 1):
                    take_y(i, k - 1)
                    add_output(i, k - 1)

            vec.sem_inc(scanned, AHEAD)
            vec.sem_inc(weighted, AHEAD)
            vec.sem_inc(fed, AHEAD)
            nc.vector.tensor_copy(sel[:], sel_f[:]).then_inc(a_step, 1)
            vec.memset(ones[:], 1.0).then_inc(a_step, 1)
            vec.memset(bias[:], -LOG_EPS).then_inc(a_step, 1)
            for q in range(2):
                vec.memset(after[q][:, :, L - 1:L], 0.0)
            for q in range(RING):
                last = vec.memset(decay[q][:, :, 0:1], 0.0)
            last.then_inc(a_step, 1)
            vec.wait_ge(a_step, past(A_STEPS - 1))
            vec.tensor_scalar(A[:], A[:], -1.0, None, ALU.mult).then_inc(a_step, 1)
            vec.wait_ge(a_step, past(A_STEPS))
            pipe.run(vec, slot)


def add_rows(nc, name, dst, src):
    with ExitStack() as ctx:
        summed = ctx.enter_context(nc.semaphore(f"{name}_summed"))
        block = ctx.enter_context(nc.Block())
        W = 32

        @block.vector
        def _(vec):
            with vec.Fori(0, G // W) as k:
                vec.tensor_tensor(rows3(dst, k * W, W), rows3(dst, k * W, W), rows3(src, k * W, W),
                                  ALU.add).then_inc(summed, 1)


class Stage:

    def __init__(self, nc, ctx, name):
        self.nc, self.ctx, self.name, self.sems = nc, ctx, name, []

    def one(self, name, shape, dt=F32):
        return self.ctx.enter_context(self.nc.sbuf_tensor(f"{self.name}_{name}", shape, dt))

    def two(self, name, shape, dt=F32):
        return [self.one(f"{name}{p}", shape, dt) for p in range(2)]

    def bank(self, name, shape, dt=F32):
        return self.ctx.enter_context(self.nc.psum_tensor(f"{self.name}_{name}", shape, dt))

    def banks(self, name, shape, dt=F32):
        return [self.bank(f"{name}{p}", shape, dt) for p in range(2)]

    def counter(self, name):
        self.sems.append(self.ctx.enter_context(self.nc.semaphore(f"{self.name}_{name}")))
        return self.sems[-1]

    def counters(self, name):
        return [self.counter(f"{name}{p}") for p in range(2)]

    def block(self):
        arm(self.nc, self.sems)
        return self.ctx.enter_context(self.nc.Block())


def fourier_mixer(nc, w, H):
    with ExitStack() as ctx:
        s = Stage(nc, ctx, "fft")
        T = s.one("T", [P, G, D])
        held = s.one("held", [P, G, D])
        gamma, beta = s.one("gamma", [P, D]), s.one("beta", [P, D])
        fc1 = s.one("fc1", [D + 1, FD])
        bn1 = s.one("bn1", [D, FD])
        fc2 = s.one("fc2", [FD, D])
        bn2 = s.one("bn2", [FD, D])
        bias2 = s.one("bias2", [1, D])
        ones = s.one("ones", [1, P])
        wr, wi = s.one("wr", [FD, FD]), s.one("wi", [FD, FD])
        bins_bias = s.one("bins_bias", [P, C, FD])
        dft, idft = s.one("dft", [P, C, L]), s.one("idft", [P, C, L])
        rb = row(w["L0_attn_rb"]).to_broadcast([P, FD])
        ib = row(w["L0_attn_ib"]).to_broadcast([P, FD])
        load(nc, "fft_w", [
            (held[:], w["scr_H"]),
            (gamma[:], spread_row(w["L0_attn_ln2_g"])), (beta[:], spread_row(w["L0_attn_ln2_b"])),
            (fc1[0:D, :], w["L0_attn_fc1_w"]), (fc1[D:D + 1, :], row(w["L0_attn_bn1_b"])),
            (bn1[:], row(w["L0_attn_bn1_s"]).to_broadcast([D, FD])), (fc2[:], w["L0_attn_fc2_w"]),
            (bn2[:], row(w["L0_attn_bn2_s"]).to_broadcast([FD, D])), (bias2[:], row(w["L0_attn_bn2_b"])),
            (wr[:], w["L0_attn_Wr"]), (wi[:], w["L0_attn_Wi"]),
            (bins_bias[:, 0, :], rb), (bins_bias[:, 1, :], rb), (bins_bias[1:P, 2, :], ib[1:P, :]),
            (bins_bias[0:1, 2, :], row(w["L0_attn_rb"])), (bins_bias[:, 3, :], ib),
            (dft[:], w["dft"]), (idft[:], w["idft"])])
        layer_norm(nc, "ln_f", H, T, 1e-3, gamma, beta)
        add_rows(nc, "fft_residual", H, held)

        rowsT = s.two("rowsT", [D + 1, L])
        f = s.two("f", [P, C, FD])
        spec = s.two("spec", [FD, L])
        minus_im = s.two("minus_im", [FD, L // 2])
        real = s.two("real", [FD, L // 2])
        z = s.two("z", [P, C, FD])
        back = s.two("back", [FD, L])
        cur = s.two("cur", [P, C, D])
        ps_a, ps_b = s.banks("ps_a", [P, L]), s.banks("ps_b", [P, L])
        ps_c, ps_d = s.banks("ps_c", [P, C, FD]), s.banks("ps_d", [P, L])
        passed, ready = s.counter("passed"), s.counter("ready")
        cur_ready, turned, rowsT_ready = s.counters("cur_ready"), s.counters("turned"), s.counters("rowsT_ready")
        fc1_done, f_ready, rfft_done = s.counters("fc1_done"), s.counters("f_ready"), s.counters("rfft_done")
        spec_ready, halves_ready, mixed = s.counters("spec_ready"), s.counters("halves_ready"), s.counters("mixed")
        biased, z_ready, irfft_done = s.counters("biased"), s.counters("z_ready"), s.counters("irfft_done")
        back_ready, fc2_done, added = s.counters("back_ready"), s.counters("fc2_done"), s.counters("added")
        block = s.block()

        @block.gpsimd
        def _(pool):
            with pool.Fori(0, SEQS // 2) as i:
                for p in range(2):
                    pool.wait_ge(turned[p], past(i))
                    nc.gpsimd.tensor_copy(cur[p][:], rows3(T, (i * 2 + p) * C, C)).then_inc(cur_ready[p], 1)

        @block.tensor
        def _(pe):
            pe.wait_ge(ready, past(7))
            with pe.Fori(0, SEQS // 2) as i:
                for p in range(2):
                    pe.wait_ge(cur_ready[p], past(i + 1))
                    pe.wait_ge(added[p], past(i))
                    pe.sem_inc(passed, 1)
                    for c in range(C):
                        last = nc.tensor.transpose(ps_a[p][0:D, c * P:(c + 1) * P], cur[p][:, c, :], w["ident"][:])
                    last.then_inc(turned[p], 1)
                for p in range(2):
                    pe.wait_ge(rowsT_ready[p], past(i + 1))
                    for c in range(C):
                        last = nc.tensor.matmul(ps_a[p][:, c * P:(c + 1) * P], rowsT[p][:, c * P:(c + 1) * P], fc1[:],
                                                start=True, stop=True)
                    last.then_inc(fc1_done[p], 1)
                for p in range(2):
                    pe.wait_ge(f_ready[p], past(i + 1))
                    for c in range(C):
                        last = nc.tensor.matmul(ps_b[p][:], f[p][:, c, :], dft[:, c, :], start=(c == 0),
                                                stop=(c == C - 1))
                    last.then_inc(rfft_done[p], 1)
                for p in range(2):
                    pe.wait_ge(spec_ready[p], past(i + 1))
                    pe.wait_ge(halves_ready[p], past(i * 2 + 2))
                    for k in range(C):
                        other = (minus_im, real)[k // 2][p]
                        nc.tensor.matmul(ps_c[p][:, k, :], spec[p][:, k * P:(k + 1) * P], wr[:], start=True, stop=False)
                        last = nc.tensor.matmul(ps_c[p][:, k, :], other[:, k % 2 * P:(k % 2 + 1) * P], wi[:],
                                                start=False, stop=True)
                    last.then_inc(mixed[p], 1)
                for p in range(2):
                    pe.wait_ge(z_ready[p], past(i + 1))
                    for k in range(C):
                        last = nc.tensor.matmul(ps_d[p][:], z[p][:, k, :], idft[:, k, :], start=(k == 0),
                                                stop=(k == C - 1))
                    last.then_inc(irfft_done[p], 1)
                for p in range(2):
                    pe.wait_ge(back_ready[p], past(i + 1))
                    for c in range(C):
                        to = ps_a[p][:, c * D:(c + 1) * D]
                        nc.tensor.matmul(to, back[p][:, c * P:(c + 1) * P], fc2[:], start=True, stop=False)
                        last = nc.tensor.matmul(to, ones[:], bias2[:], start=False, stop=True)
                    last.then_inc(fc2_done[p], 1)

        @block.scalar
        def _(act):
            with act.Fori(0, SEQS // 2) as i:
                for p in range(2):
                    act.wait_ge(fc1_done[p], past(i + 1))
                    nc.scalar.activation(f[p][:].rearrange("p c f -> p (c f)"), ps_a[p][:],
                                         ACT.Relu).then_inc(f_ready[p], 1)
                for p in range(2):
                    act.wait_ge(rfft_done[p], past(i + 1))
                    nc.scalar.activation(spec[p][:], ps_b[p][:], ACT.Copy).then_inc(spec_ready[p], 1)
                for p in range(2):
                    act.wait_ge(biased[p], past(i + 1))
                    nc.scalar.activation(z[p][:], z[p][:], ACT.Relu).then_inc(z_ready[p], 1)
                for p in range(2):
                    act.wait_ge(irfft_done[p], past(i + 1))
                    nc.scalar.activation(back[p][:], ps_d[p][:], ACT.Copy).then_inc(back_ready[p], 1)

        @block.vector
        def _(vec):
            vec.tensor_tensor(fc1[0:D, :], fc1[0:D, :], bn1[:], ALU.mult).then_inc(ready, 1)
            vec.tensor_tensor(fc2[:], fc2[:], bn2[:], ALU.mult).then_inc(ready, 1)
            vec.memset(ones[:], 1.0).then_inc(ready, 1)
            for p in range(2):
                vec.memset(rowsT[p][D:D + 1, :], 1.0).then_inc(ready, 1)
                vec.memset(minus_im[p][:, 0:1], 0.0)
                vec.memset(real[p][:, 0:1], 0.0).then_inc(ready, 1)
            with vec.Fori(0, SEQS // 2) as i:
                for p in range(2):
                    vec.wait_ge(turned[p], past(i + 1))
                    nc.vector.tensor_copy(rowsT[p][0:D, :], ps_a[p][0:D, :]).then_inc(rowsT_ready[p], 1)
                for p in range(2):
                    vec.wait_ge(spec_ready[p], past(i + 1))
                    vec.tensor_scalar(minus_im[p][:, 1:], spec[p][:, L // 2 + 1:], -1.0, None,
                                      ALU.mult).then_inc(halves_ready[p], 1)
                    nc.vector.tensor_copy(real[p][:, 1:], spec[p][:, 1:L // 2]).then_inc(halves_ready[p], 1)
                for p in range(2):
                    vec.wait_ge(mixed[p], past(i + 1))
                    vec.tensor_tensor(z[p][:], ps_c[p][:], bins_bias[:], ALU.add).then_inc(biased[p], 1)
                for p in range(2):
                    vec.wait_ge(fc2_done[p], past(i + 1))
                    g0 = (i * 2 + p) * C
                    vec.tensor_tensor(rows3(H, g0, C), rows3(H, g0, C),
                                      ps_a[p][:, 0:C * D].rearrange("p (c d) -> p c d", d=D),
                                      ALU.add).then_inc(added[p], 1)


def router(nc, w, name, T, xT, route_w, experts):
    with ExitStack() as ctx:
        s = Stage(nc, ctx, f"{name}_route")
        logits = route_w["logits"]
        cur = s.two("cur", [P, C, D])
        xc = s.two("xc", [D + 1, L])
        ps_t = s.banks("ps_t", [D, L])
        ps_l = s.banks("ps_l", [P, C, experts])
        passed, ready = s.counter("passed"), s.counter("ready")
        cur_ready, turned = s.counters("cur_ready"), s.counters("turned")
        kept, copied = s.counters("kept"), s.counters("copied")
        scored, saved = s.counters("scored"), s.counters("saved")
        block = s.block()

        @block.gpsimd
        def _(pool):
            with pool.Fori(0, SEQS // 2) as i:
                for p in range(2):
                    pool.wait_ge(turned[p], past(i))
                    nc.gpsimd.tensor_copy(cur[p][:], rows3(T, (i * 2 + p) * C, C)).then_inc(cur_ready[p], 1)

        @block.tensor
        def _(pe):
            pe.wait_ge(ready, past(2))
            with pe.Fori(0, SEQS // 2) as i:
                for p in range(2):
                    pe.wait_ge(cur_ready[p], past(i + 1))
                    pe.wait_ge(copied[p], past(i))
                    pe.sem_inc(passed, 1)
                    for c in range(C):
                        last = nc.tensor.transpose(ps_t[p][:, c * P:(c + 1) * P], cur[p][:, c, :], w["ident"][:])
                    last.then_inc(turned[p], 1)
                for p in range(2):
                    pe.wait_ge(copied[p], past(i + 1))
                    pe.wait_ge(saved[p], past(i))
                    pe.sem_inc(passed, 1)
                    for c in range(C):
                        last = nc.tensor.matmul(ps_l[p][:, c, :], xc[p][:, c * P:(c + 1) * P], route_w["weights"][:],
                                                start=True, stop=True)
                    last.then_inc(scored[p], 1)

        @block.scalar
        def _(act):
            with act.Fori(0, SEQS // 2) as i:
                for p in range(2):
                    act.wait_ge(copied[p], past(i + 1))
                    act.sem_inc(passed, 1)
                    nc.scalar.activation(xT[0:D, ds((i * 2 + p) * L, L)], xc[p][0:D, :], ACT.Copy)
                    nc.scalar.activation(xT[D:P, ds((i * 2 + p) * L, L)], xc[p][0:D, :], ACT.Copy).then_inc(kept[p], 1)

        @block.vector
        def _(vec):
            for p in range(2):
                vec.memset(xc[p][D:D + 1, :], 1.0).then_inc(ready, 1)
            with vec.Fori(0, SEQS // 2) as i:
                for p in range(2):
                    vec.wait_ge(turned[p], past(i + 1))
                    vec.wait_ge(scored[p], past(i))
                    vec.wait_ge(kept[p], past(i))
                    nc.vector.tensor_copy(xc[p][0:D, :], ps_t[p][:]).then_inc(copied[p], 1)
                for p in range(2):
                    vec.wait_ge(scored[p], past(i + 1))
                    nc.vector.tensor_copy(logits[:, ds((i * 2 + p) * C, C), :], ps_l[p][:]).then_inc(saved[p], 1)


def top_two(nc, w, name, probs, comb, experts, soften):
    with ExitStack() as ctx:
        def sb(n, shape):
            return ctx.enter_context(nc.sbuf_tensor(f"{name}_{n}", shape, F32))

        pref = sb("pref", [P, experts])
        best, total = sb("best", [P, G]), sb("total", [P, G])
        top = [sb("top0", [P, G]), sb("top1", [P, G])]
        hot = [sb("hot0", [P, G, experts]), sb("hot1", [P, G, experts])]
        rank = sb("rank", [P, G])
        even = sb("even", [P, G])
        load(nc, f"{name}_pref", [(pref[:], row(w["preference"][0:experts]).to_broadcast([P, experts]))])
        made = ctx.enter_context(nc.semaphore(f"{name}_made"))
        powered = ctx.enter_context(nc.semaphore(f"{name}_powered"))
        block = ctx.enter_context(nc.Block())

        def over(stat):
            return stat[:].unsqueeze(2).to_broadcast([P, G, experts])

        first_pass, second_pass = 2, 4

        @block.vector
        def _(vec):
            made_n = Count()

            def tt(out, a, b, op):
                vec.tensor_tensor(out, a, b, op).then_inc(made, made_n.up())
                vec.wait_ge(made, made_n.value)

            def reduced(out, a, op):
                vec.tensor_reduce(out, a, AX.X, op).then_inc(made, made_n.up())
                vec.wait_ge(made, made_n.value)

            def reciprocal(x):
                vec.reciprocal(x, x).then_inc(made, made_n.up())
                vec.wait_ge(made, made_n.value)

            reduced(best[:], probs[:], ALU.max)
            tt(probs[:], probs[:], over(best), ALU.subtract)
            vec.wait_ge(powered, 1)
            reduced(total[:], probs[:], ALU.add)
            reciprocal(total[:])
            tt(probs[:], probs[:], over(total), ALU.mult)
            for k in range(2):
                reduced(top[k][:], probs[:], ALU.max)
                tt(hot[k][:], probs[:], over(top[k]), ALU.is_equal)
                tt(hot[k][:], hot[k][:], pref[:].unsqueeze(1).to_broadcast([P, G, experts]), ALU.mult)
                reduced(rank[:], hot[k][:], ALU.max)
                tt(hot[k][:], hot[k][:], over(rank), ALU.is_equal)
                if k == 0:
                    vec.scalar_tensor_tensor(probs[:], hot[0][:], -2.0, probs[:], ALU.mult,
                                             ALU.add).then_inc(made, made_n.up())
                    vec.wait_ge(made, made_n.value)
            if soften:
                tt(even[:], top[1][:], top[0][:], ALU.subtract)
                vec.sem_inc(powered, 1)
                vec.wait_ge(powered, 3)
                vec.tensor_scalar(total[:], even[:], 1.0, None, ALU.add).then_inc(made, made_n.up())
                vec.wait_ge(made, made_n.value)
                reciprocal(total[:])
                nc.vector.tensor_copy(top[0][:], total[:]).then_inc(made, made_n.up())
                tt(top[1][:], even[:], total[:], ALU.mult)
            else:
                tt(total[:], top[0][:], top[1][:], ALU.add)
                vec.tensor_scalar(total[:], total[:], 1e-12, None, ALU.max).then_inc(made, made_n.up())
                vec.wait_ge(made, made_n.value)
                reciprocal(total[:])
                for k in range(2):
                    tt(top[k][:], top[k][:], total[:], ALU.mult)
            for k in range(2):
                tt(hot[k][:], hot[k][:], over(top[k]), ALU.mult)
            tt(comb[:], hot[0][:], hot[1][:], ALU.add)

        @block.scalar
        def _(act):
            act.wait_ge(made, 2)
            nc.scalar.activation(probs[:], probs[:], ACT.Exp).then_inc(powered, 1)
            if soften:
                act.wait_ge(powered, 2)
                nc.scalar.activation(even[:], even[:], ACT.Exp).then_inc(powered, 1)


PART_ROW = 32
GATE_ROWS = 2 * PART_ROW + E1


def gate_parts(nc, name, comb, parts, experts, ones):
    with ExitStack() as ctx:
        rest = ctx.enter_context(nc.sbuf_tensor(f"{name}_rest", [P, G, experts], F32))
        step = ctx.enter_context(nc.semaphore(f"{name}_step"))
        block = ctx.enter_context(nc.Block())

        @block.vector
        def _(vec):
            n = Count()

            def then(done):
                done.then_inc(step, n.up())
                vec.wait_ge(step, n.value)

            def part(k):
                return parts[:, :, k * PART_ROW:k * PART_ROW + experts]

            then(vec.memset(parts[:], 0.0))
            if ones:
                then(vec.memset(parts[:, :, experts:experts + 1], 1.0))
            then(nc.vector.tensor_copy(part(0), comb[:]))
            then(vec.tensor_tensor(rest[:], comb[:], part(0), ALU.subtract))
            then(nc.vector.tensor_copy(part(1), rest[:]))
            then(vec.tensor_tensor(part(2), rest[:], part(1), ALU.subtract))


def expert_ffn(nc, w, H):
    with ExitStack() as outer:
        xT = outer.enter_context(nc.sbuf_tensor("ffn_xT", [P, SEQS * L], F32))
        gates = outer.enter_context(nc.sbuf_tensor("ffn_gates", [P, G, GATE_ROWS], BF16))
        with ExitStack() as ctx:
            T = ctx.enter_context(nc.sbuf_tensor("ffn_T", [P, G, D], F32))
            logits = ctx.enter_context(nc.sbuf_tensor("ffn_logits", [P, G, E0], F32))
            gw = ctx.enter_context(nc.sbuf_tensor("ffn_gw", [D + 1, E0], F32))
            load(nc, "ffn_gate_w", [(gw[0:D, :], w["L0_ffn_gW"]), (gw[D:D + 1, :], row(w["L0_ffn_gb"]))])
            layer_norm(nc, "ln_e", H, T, 1e-5)
            router(nc, w, "ffn", T, xT, {"logits": logits, "weights": gw}, E0)
            comb = ctx.enter_context(nc.sbuf_tensor("ffn_comb", [P, G, E0], F32))
            top_two(nc, w, "ffn_top", logits, comb, E0, True)
            gate_parts(nc, "ffn_parts", comb, gates, E0, True)

        with ExitStack() as ctx:
            s = Stage(nc, ctx, "ffn")
            ew1 = s.one("ew1", [P, E0 // 2, P])
            ew2 = s.one("ew2", [P, E0, D])
            ew3 = s.one("ew3", [P, E0 // 2, D])
            eb1 = s.one("eb1", [P, E0])
            eb2 = s.one("eb2", [P, E0 // 2])
            eb3 = s.one("eb3", [GATE_ROWS, D])
            sw1, sw2, sw3 = s.one("sw1", [D, P]), s.one("sw2", [D, P]), s.one("sw3", [P, D])
            sb1, sb2 = s.one("sb1", [D, 1]), s.one("sb2", [P, 1])
            pick = s.one("pick", [GATE_ROWS, E0 // 2, P])
            pick_b = s.one("pick_b", [GATE_ROWS, E0 // 2, P], BF16)
            twice = s.one("twice", [P, D])
            clear(nc, "ffn_sw1", sw1[:, D:])
            clear(nc, "ffn_eb3", eb3[:])
            load(nc, "ffn_w", [
                (ew1[0:D], w["L0_ffn_eW1"].rearrange("(n a) f h -> a f n h", a=2)[0]),
                (ew1[D:P], w["L0_ffn_eW1"].rearrange("(n a) f h -> a f n h", a=2)[1]),
                (twice[:], w["stacked_identity"]), (ew2[:], w["L0_ffn_eW2"].rearrange("e h g -> h e g")),
                (ew3[:], w["L0_ffn_eW3"].rearrange("(q a) g o -> (a g) q o", a=2)),
                (eb1[:], w["eb1_columns"]), (eb2[:], w["eb2_columns"]),
                *((eb3[r * PART_ROW:r * PART_ROW + E0, :], w["L0_ffn_eb3"]) for r in range(3)),
                (eb3[E0:E0 + 1, :], row(w["L0_ffn_sb3"])),
                (sw1[:, 0:D], w["L0_ffn_sW1"]), (sw2[:], w["L0_ffn_sW2"]), (sw3[:], w["L0_ffn_sW3"]),
                (sb1[:], column(w["L0_ffn_sb1"])), (sb2[:], column(w["L0_ffn_sb2"])),
                (pick[:], w["pick_parts"][:, 0:E0 // 2, :])])
            cur = s.two("cur", [P, C, GATE_ROWS])
            gT = s.two("gT", [GATE_ROWS, L])
            gb = s.two("gb", [GATE_ROWS, L], BF16)
            gb_ready = s.counter("gb_ready")
            h1 = [s.two(f"h1_{e}", [P, L]) for e in range(2)]
            h2 = [s.two(f"h2_{q}", [P, L]) for q in range(2)]
            s1, s2 = s.two("s1", [D, L]), s.two("s2", [P, L])
            ps_g = s.bank("ps_g", [P, L])
            ps_t = s.bank("ps_t", [GATE_ROWS, L])
            ps_1 = s.banks("ps_1", [P, L])
            ps_2 = s.banks("ps_2", [P, L])
            ps_e = s.bank("ps_e", [P, L])
            ps_o = s.bank("ps_o", [P, C, D])
            halves = s.one("halves", [P, L])
            x = s.two("x", [P, L])
            x_ready = s.counter("x_ready")
            halved, halves_ready = s.counter("halved"), s.counter("halves_ready")
            passed, ready = s.counter("passed"), s.counter("ready")
            cur_ready, turned, gT_ready = s.counter("cur_ready"), s.counter("turned"), s.counter("gT_ready")
            first, first_act = s.counter("first"), s.counter("first_act")
            second, second_act = s.counter("second"), s.counter("second_act")
            spread, gated = s.counter("spread"), s.counter("gated")
            out_done, added = s.counter("out_done"), s.counter("added")
            block = s.block()
            N1, N2 = E0 + 1, E0 // 2 + 1
            pipe = Slots(2, -1, 2, SEQS - 1, SEQS + 1)
            live, before, through = pipe.live, pipe.before, pipe.through

            @block.gpsimd
            def _(pool):
                def slot(i, k):
                    if live(i, k + 1):
                        wait(pool, first, before(i, k) * N1)
                        nc.gpsimd.tensor_copy(x[(k + 1) % 2][:], xT[:, ds(before(i, k + 1) * L, L)]).then_inc(x_ready, 1)
                        wait(pool, turned, before(i, k))
                        nc.gpsimd.tensor_copy(cur[(k + 1) % 2][:], gates[:, ds(before(i, k + 1) * C, C), :]).then_inc(cur_ready, 1)

                pipe.run(pool, slot)

            @block.tensor
            def _(pe):
                def layer_1(i, k, n):
                    items = (n,) if n == E0 else (n, n + 1)
                    wait(pe, first_act, before(i, k) * N1 + items[-1] - 1)
                    if n == 0:
                        wait(pe, x_ready, through(i, k))
                    pe.sem_inc(passed, 1)
                    for n in items:
                        up = slice(D, P) if n % 2 else slice(0, D)
                        nc.tensor.matmul(ps_1[(k * N1 + n) % 2][:], sw1[:] if n == E0 else ew1[up, n // 2, :],
                                         x[k % 2][up, :], start=True, stop=True).then_inc(first, 1)

                def layer_2(i, k, n):
                    wait(pe, second_act, before(i, k) * N2 + n - 1)
                    wait(pe, first_act, before(i, k) * N1 + min(n * 2 + 2, N1))
                    pe.sem_inc(passed, 1)
                    to = ps_2[(k * N2 + n) % 2]
                    if n < E0 // 2:
                        for a in range(2):
                            last = nc.tensor.matmul(to[a * D:(a + 1) * D, :], ew2[:, n * 2 + a, :],
                                                    h1[a][n][:], start=True, stop=True)
                    else:
                        last = nc.tensor.matmul(to[:], sw2[:], s1[k % 2][:], start=True, stop=True)
                    last.then_inc(second, 1)

                def spread_gates(i, k, q):
                    wait(pe, gated, before(i, k) * 2 + q)
                    if q == 0:
                        wait(pe, gb_ready, through(i, k))
                    pe.sem_inc(passed, 1)
                    nc.tensor.matmul(ps_g[:], pick_b[:, q, :], gb[k % 2][:], start=True, stop=True).then_inc(spread, 1)

                def turn_gates(i, k, tiles):
                    if 0 in tiles:
                        wait(pe, cur_ready, through(i, k))
                        wait(pe, gT_ready, before(i, k))
                        pe.sem_inc(passed, 1)
                    for c in tiles:
                        last = nc.tensor.transpose(ps_t[:, c * P:(c + 1) * P], cur[k % 2][:, c, :], w["ident"][:])
                    if C - 1 in tiles:
                        last.then_inc(turned, 1)

                def output_halves(i, k):
                    p = k % 2
                    wait(pe, second_act, through(i, k) * N2)
                    wait(pe, gated, through(i, k) * 2)
                    wait(pe, halves_ready, before(i, k))
                    nc.tensor.matmul(ps_e[0:D, :], ew3[:, 0, :], h2[0][p][:], start=True, stop=False)
                    nc.tensor.matmul(ps_e[D:P, :], ew3[:, 1, :], h2[1][p][:], start=True, stop=True)
                    nc.tensor.matmul(ps_e[0:D, :], sw3[:], s2[p][:], start=False, stop=False)
                    nc.tensor.matmul(ps_e[0:D, :], eb3[:], gT[p][:], start=False, stop=True).then_inc(halved, 1)

                def output(i, k, c):
                    if c == 0:
                        wait(pe, halves_ready, through(i, k))
                        wait(pe, added, before(i, k))
                        pe.sem_inc(passed, 1)
                    last = nc.tensor.matmul(ps_o[:, c, :], halves[:, c * P:(c + 1) * P], twice[:], start=True, stop=True)
                    if c == C - 1:
                        last.then_inc(out_done, 1)

                def slot(i, k):
                    if live(i, k):
                        layer_1(i, k, 0)
                        spread_gates(i, k, 0)
                    if live(i, k - 1):
                        output_halves(i, k - 1)
                    if live(i, k + 1):
                        turn_gates(i, k + 1, (0, 1))
                    if live(i, k):
                        layer_1(i, k, 2)
                        layer_2(i, k, 0)
                    if live(i, k - 1):
                        output(i, k - 1, 0)
                    if live(i, k):
                        layer_1(i, k, E0)
                    if live(i, k + 1):
                        turn_gates(i, k + 1, (2, 3))
                    if live(i, k - 1):
                        output(i, k - 1, 1)
                    if live(i, k):
                        layer_2(i, k, 1)
                    if live(i, k - 1):
                        output(i, k - 1, 2)
                    if live(i, k):
                        spread_gates(i, k, 1)
                    if live(i, k - 1):
                        output(i, k - 1, 3)
                    if live(i, k):
                        layer_2(i, k, 2)

                pe.wait_ge(ready, past(1))
                pipe.run(pe, slot)

            @block.scalar
            def _(act):
                def act_1(i, k, n):
                    wait(act, first, before(i, k) * N1 + n + 1)
                    if n == E0:
                        to, bias = s1[k % 2][:], sb1[:]
                    else:
                        to, bias = h1[n % 2][n // 2][:], eb1[:, n:n + 1]
                    m = D if n == E0 else P
                    nc.scalar.activation(to, ps_1[(k * N1 + n) % 2][0:m, :], ACT.Relu, bias=bias).then_inc(first_act, 1)

                def act_2(i, k, n):
                    wait(act, second, before(i, k) * N2 + n + 1)
                    if n == 0:
                        wait(act, halved, before(i, k - 1))
                    to, bias = (h2[n][k % 2], eb2[:, n:n + 1]) if n < 2 else (s2[k % 2], sb2[:])
                    nc.scalar.activation(to[:], ps_2[(k * N2 + n) % 2][:], ACT.Relu, bias=bias).then_inc(second_act, 1)

                def slot(i, k):
                    if live(i, k):
                        act_1(i, k, 0)
                        act_1(i, k, 1)
                    if live(i, k - 1):
                        wait(act, halved, through(i, k - 1))
                        wait(act, out_done, before(i, k - 1))
                        nc.scalar.activation(halves[:], ps_e[:], ACT.Copy).then_inc(halves_ready, 1)
                    if live(i, k):
                        for step, n in ((act_1, 2), (act_1, 3), (act_2, 0), (act_1, E0), (act_2, 1), (act_2, 2)):
                            step(i, k, n)
                    if live(i, k + 1):
                        wait(act, gT_ready, through(i, k + 1))
                        wait(act, spread, before(i, k) * 2)
                        nc.scalar.activation(gb[(k + 1) % 2][:], gT[(k + 1) % 2][:], ACT.Copy).then_inc(gb_ready, 1)

                pipe.run(act, slot)

            @block.vector
            def _(vec):
                def gate(i, k, q):
                    wait(vec, spread, before(i, k) * 2 + q + 1)
                    wait(vec, second_act, before(i, k) * N2 + q + 1)
                    vec.tensor_tensor(h2[q][k % 2][:], h2[q][k % 2][:], ps_g[:], ALU.mult).then_inc(gated, 1)

                def slot(i, k):
                    if live(i, k):
                        gate(i, k, 0)
                    if live(i, k + 1):
                        wait(vec, turned, through(i, k + 1))
                        wait(vec, halved, before(i, k))
                        nc.vector.tensor_copy(gT[(k + 1) % 2][:], ps_t[:]).then_inc(gT_ready, 1)
                    if live(i, k):
                        gate(i, k, 1)
                    if live(i, k - 1):
                        wait(vec, out_done, through(i, k - 1))
                        g0 = before(i, k - 1) * C
                        vec.tensor_tensor(rows3(H, g0, C), rows3(H, g0, C), ps_o[:], ALU.add).then_inc(added, 1)

                nc.vector.tensor_copy(pick_b[:], pick[:]).then_inc(ready, 1)
                pipe.run(vec, slot)


def edge_bias(nc, w, bias_scr):
    with ExitStack() as ctx:
        s = Stage(nc, ctx, "edge")
        step_base = s.one("step_base", [P, SEQS])
        there, last_of = s.one("there", [P, SEQS, C]), s.one("last_of", [P, SEQS, C])
        last, found = s.one("last", [P, C]), s.one("found", [P, C])
        at = s.one("at", [P, C], I32)
        attr = s.one("attr", [P, C, 3])
        we, be = s.one("we", [P, 3, HEADS]), s.one("be", [P, HEADS])
        value, term = s.one("value", [P, HEADS, C]), s.one("term", [P, HEADS, C])
        parts, rest = s.one("parts", [HEADS * C, 3, P], BF16), s.one("rest", [HEADS * C, P])
        ps_v = s.bank("ps_v", [HEADS * C, P])
        load(nc, "edge_w", [(step_base[:], w["edge_bases"].to_broadcast([P, SEQS])),
                            (we[:], row(w["L1_attn_We"].rearrange("k h -> (k h)")).to_broadcast([P, 3 * HEADS])
                             .rearrange("p (k h) -> p k h", h=HEADS)),
                            (be[:], spread_row(w["L1_attn_be"]))])
        made = s.counter("made")
        turned, high, rest_ready, mid = s.counter("turned"), s.counter("high"), s.counter("rest_ready"), s.counter("mid")
        gathered = w["gathered"][2]
        stored = s.counter("stored")
        block = s.block()

        @block.sync
        def _(sp):
            sp.wait_ge(made, past(14))
            sp.dma_start(bias_scr.rearrange("a (r p) -> r a p", p=P), parts[:]).then_inc(stored, 16)
            sp.wait_ge(stored, past(16))

        @block.vector
        def _(vec):
            n = Count(1)

            def then(step):
                step.then_inc(made, n.up())
                vec.wait_ge(made, n.value)

            in_step = w["last_of"][:].rearrange("p (k c) -> p k c", c=C)
            then(vec.tensor_scalar(there[:], in_step, 0.0, None, ALU.is_gt))
            then(vec.tensor_tensor(there[:], there[:], step_base[:].unsqueeze(2).to_broadcast([P, SEQS, C]), ALU.mult))
            then(vec.tensor_tensor(last_of[:], in_step, there[:], ALU.add))
            then(vec.tensor_reduce(last[:], last_of[:].rearrange("p k c -> p c k"), AX.X, ALU.max))
            then(vec.tensor_scalar(found[:], last[:], 0.0, None, ALU.is_gt))
            then(vec.tensor_scalar(at[:], last[:], -1.0, 0.0, ALU.add, ALU.max))
            vec.wait_ge(gathered, 16 * C)

            def attribute(k):
                return attr[:, :, k].unsqueeze(1).to_broadcast([P, HEADS, C])

            def weight(x):
                return x.unsqueeze(2).to_broadcast([P, HEADS, C])

            then(vec.tensor_tensor(value[:], attribute(0), weight(we[:, 0, :]), ALU.mult))
            for k in range(1, 3):
                then(vec.tensor_tensor(term[:], attribute(k), weight(we[:, k, :]), ALU.mult))
                then(vec.tensor_tensor(value[:], value[:], term[:], ALU.add))
            then(vec.tensor_tensor(value[:], value[:], weight(be[:]), ALU.add))
            then(vec.tensor_tensor(value[:], value[:], found[:].unsqueeze(1).to_broadcast([P, HEADS, C]), ALU.mult))
            vec.wait_ge(high, past(1))
            vec.tensor_tensor(rest[:], ps_v[:], parts[:, 0, :], ALU.subtract).then_inc(rest_ready, 1)
            vec.wait_ge(mid, past(1))
            then(vec.tensor_tensor(parts[:, 2, :], rest[:], parts[:, 1, :], ALU.subtract))

        @block.gpsimd
        def _(pool):
            pool.wait_ge(made, past(6))
            for c in range(C):
                nc.gpsimd.indirect_dma_start(
                    out=attr[:, c, :], out_offset=None, in_=w["L1_attn_edge_attr"],
                    in_offset=bass.IndirectOffsetOnAxis(ap=at[:, c:c + 1], axis=0)).then_inc(gathered, 16)

        @block.tensor
        def _(pe):
            pe.wait_ge(made, past(13))
            nc.tensor.transpose(ps_v[:], value[:].rearrange("p h c -> p (h c)"), w["ident"][:]).then_inc(turned, 1)

        @block.scalar
        def _(act):
            act.wait_ge(turned, past(1))
            nc.scalar.activation(parts[:, 0, :], ps_v[:], ACT.Copy).then_inc(high, 1)
            act.wait_ge(rest_ready, past(1))
            nc.scalar.activation(parts[:, 1, :], rest[:], ACT.Copy).then_inc(mid, 1)


PARTS = 3
CROSS = PARTS * PARTS * HD
BIAS, PEAK = CROSS, CROSS + PARTS
STACK = PEAK + PARTS
QUAD = 4
UNROLL = 4


def edge_attention(nc, w, H):
    bias_scr = nc.dram_tensor("scratch_bias", (PARTS, HEADS * L), BF16).ap()
    peak_scr = nc.dram_tensor("scratch_peak", (PARTS, HEADS * L), BF16).ap()
    rows_scr = nc.dram_tensor("scratch_rows", (P, G, D), F32).ap()
    q_scr = nc.dram_tensor("scratch_q", (PARTS, PARTS, HD, HEADS * L), BF16).ap()
    k_scr = nc.dram_tensor("scratch_k", (PARTS, HD, HEADS * L), BF16).ap()
    edge_bias(nc, w, bias_scr)
    with ExitStack() as ctx:
        T = ctx.enter_context(nc.sbuf_tensor("attn_T", [P, G, D], F32))
        layer_norm(nc, "ln_a", H, T, 1e-5)
        move(nc, "attn_rows", rows_scr, T[:])
    with ExitStack() as ctx:
        s = Stage(nc, ctx, "attn")
        wqk, wv, wo = s.one("wqk", [D + 1, 2 * D]), s.one("wv", [D + 1, D]), s.one("wo", [D + 1, D])
        ks = [s.one(f"ks{m}", [STACK, HEADS, L], BF16) for m in range(UNROLL)]
        qs = [s.one(f"qs{m}", [STACK, HEADS, L], BF16) for m in range(UNROLL)]
        values = [s.one(f"values{m}", [P, C, HEADS, 32]) for m in range(UNROLL)]
        xT, oT = s.one("xT", [D + 1, L]), s.one("oT", [D + 1, L])
        with ExitStack() as zero:
            made = zero.enter_context(nc.semaphore("attn_made"))
            block = zero.enter_context(nc.Block())

            @block.vector
            def _(vec):
                for m in range(UNROLL):
                    vec.memset(ks[m][:], 1.0).then_inc(made, 1)
                vec.memset(xT[D:D + 1, :], 1.0).then_inc(made, 1)
                vec.memset(oT[D:D + 1, :], 1.0).then_inc(made, 1)

            @block.gpsimd
            def _(pool):
                for m in range(UNROLL):
                    pool.memset(qs[m][:], 1.0).then_inc(made, 1)
                for m in range(UNROLL):
                    pool.memset(values[m][:, :, :, 0:HD], 0.0)
                    pool.memset(values[m][:, :, :, HD:HD + 1], 1.0)
                    pool.memset(values[m][:, :, :, HD + 1:], 0.0).then_inc(made, 1)

        load(nc, "attn_w", [
            (wqk[0:D, 0:D], w["wq_columns"]), (wqk[0:D, D:], w["wk_columns"]),
            (wqk[D:D + 1, 0:D], row(w["bq_columns"])), (wqk[D:D + 1, D:], row(w["bk_columns"])),
            (wv[0:D, :], w["L1_attn_Wv"]), (wv[D:D + 1, :], row(w["L1_attn_bv"])),
            (wo[0:D, :], w["L1_attn_Wo"]), (wo[D:D + 1, :], row(w["L1_attn_bo"]))]
            + [(ks[m][BIAS:PEAK, :, :].rearrange("a h t -> a (h t)"), bias_scr) for m in range(UNROLL)])

        cur = s.one("cur", [P, C, D])
        parts, rest = s.one("parts", [P, PARTS, L], BF16), s.one("rest", [P, L])
        peaks = [s.one(f"peaks{m}", [P, HEADS * C]) for m in range(UNROLL)]
        peak_parts = s.one("peak_parts", [HEADS * C, PARTS, P], BF16)
        peak_rest = s.one("peak_rest", [HEADS * C, P])
        probs = s.two("probs", [P, QUAD, C, L])
        o_rows = s.two("o_rows", [P, L])
        share = s.one("share", [P, C, QUAD])
        o_norm = s.one("o_norm", [P, C, 2, QUAD * HD])
        ps_row = s.banks("ps_row", [P, L])
        ps_col = s.banks("ps_col", [P, 2, L])
        ps_o = s.bank("ps_o", [P, L])
        ps_m = s.bank("ps_m", [P, L])
        passed, ready = s.counter("passed"), s.counter("ready")
        cur_in, qk_stored, peak_stored = s.counter("cur_in"), s.counter("qk_stored"), s.counter("peak_stored")
        stack_in = [s.counter(f"stack_in{m}") for m in range(UNROLL)]
        peak_in = [s.counter(f"peak_in{m}") for m in range(UNROLL)]
        turned, x_copied = s.counter("turned"), s.counter("x_copied")
        qk_done, qk_high, qk_rest, qk_mid, qk_low = (s.counter(f"qk_{n}") for n in ("done", "high", "rest", "mid", "low"))
        v_done, v_copied = s.counter("v_done"), s.counter("v_copied")
        row_scored, row_maxed = s.counter("row_scored"), s.counter("row_maxed")
        pk_done, pk_high, pk_rest, pk_mid, pk_low = (s.counter(f"pk_{n}") for n in ("done", "high", "rest", "mid", "low"))
        col_scored, powered = s.counter("col_scored"), s.counter("powered")
        o_done, o_copied, o_turned = s.counter("o_done"), s.counter("o_copied"), s.counter("o_turned")
        shared, normed, n_turned = s.counter("shared"), s.counter("normed"), s.counter("n_turned")
        n_copied, out_done, added = s.counter("n_copied"), s.counter("out_done"), s.counter("added")
        arm(nc, s.sems)
        block = ctx.enter_context(nc.Block())

        ROWS, COLS = HEADS * C, HEADS * C // 2
        STEPS = ROWS // 2
        STACK_DMAS = 1 + PARTS
        pipe = Slots(UNROLL, -1, 4, SEQS - 2, SEQS + 4)
        live, before, through, round_of = pipe.live, pipe.before, pipe.through, pipe.round_of

        @block.sync
        def _(sp):
            def fetch(i, k):
                wait(sp, turned, before(i, k))
                sp.sem_inc(passed, 1)
                sp.dma_start(cur[:], rows_scr[:, ds(before(i, k) * C, C), :]).then_inc(cur_in, 16)

            def slot(i, k):
                if live(i, k + 2):
                    fetch(i, k + 2)
                if live(i, k + 1):
                    m = (k + 1) % UNROLL
                    wait(sp, qk_low, through(i, k + 1))
                    wait(sp, qk_mid, through(i, k + 1))
                    for copy in range(PARTS):
                        sp.dma_start(q_scr[:, copy].rearrange("a c (h t) -> (c h) a t", t=L),
                                     parts[0:D]).then_inc(qk_stored, 16)
                    sp.dma_start(k_scr.rearrange("b c (h t) -> (c h) b t", t=L), parts[D:]).then_inc(qk_stored, 16)
                    wait(sp, qk_stored, through(i, k + 1) * (16 * STACK_DMAS))
                    wait(sp, col_scored, before(i, k - 2) * COLS)
                    sp.sem_inc(passed, 1)
                    sp.dma_start(qs[m][0:CROSS].rearrange("r h t -> r (h t)"),
                                 q_scr.rearrange("a b c x -> (a b c) x")).then_inc(stack_in[m], 16)
                    for copy in range(PARTS):
                        rows = ks[m][copy * PARTS * HD:(copy + 1) * PARTS * HD]
                        sp.dma_start(rows.rearrange("r h t -> r (h t)"),
                                     k_scr.rearrange("b c x -> (b c) x")).then_inc(stack_in[m], 16)
                    wait(sp, stack_in[m], (round_of(i, k + 1) + 1) * (16 * STACK_DMAS))
                    sp.sem_inc(passed, 1)
                if live(i, k - 1):
                    m = (k - 1) % UNROLL
                    wait(sp, pk_low, through(i, k - 1))
                    sp.dma_start(peak_scr.rearrange("a (r p) -> r a p", p=P), peak_parts[:]).then_inc(peak_stored, 16)
                    wait(sp, peak_stored, through(i, k - 1) * 16)
                    sp.dma_start(qs[m][PEAK:STACK, :, :].rearrange("a h t -> a (h t)"), peak_scr).then_inc(peak_in[m], 16)
                    wait(sp, peak_in[m], (round_of(i, k - 1) + 1) * 16)
                    sp.sem_inc(passed, 1)

            fetch(0, 0)
            pipe.run(sp, slot)

        @block.tensor
        def _(pe):
            def row_item(i, k, n):
                m = k % UNROLL
                if n == 0:
                    wait(pe, stack_in[m], (round_of(i, k) + 1) * (16 * STACK_DMAS))
                wait(pe, row_maxed, before(i, k) * ROWS + (n - 1))
                h, c = n // C, n % C
                nc.tensor.matmul(ps_row[n % 2][:], qs[m][0:PEAK, h, c * P:(c + 1) * P], ks[m][0:PEAK, h, :],
                                 start=True, stop=True).then_inc(row_scored, 1)

            def col_item(i, k, n):
                m = k % UNROLL
                if n == 0:
                    wait(pe, peak_in[m], (round_of(i, k) + 1) * 16)
                wait(pe, powered, before(i, k) * COLS + (n - 1))
                h, c = n // 2, n % 2 * 2
                for j in range(2):
                    last = nc.tensor.matmul(ps_col[n % 2][:, j, :], ks[m][:, h, (c + j) * P:(c + j + 1) * P],
                                            qs[m][:, h, :], start=True, stop=True)
                last.then_inc(col_scored, 1)

            def weigh(i, k, quad, c):
                if c == 0:
                    wait(pe, powered, before(i, k) * COLS + (quad + 1) * (COLS // 2))
                    wait(pe, o_copied, before(i, k) * 2 + quad)
                    if quad == 0:
                        wait(pe, v_copied, through(i, k))
                for hh in range(QUAD):
                    last = nc.tensor.matmul(ps_o[32 * hh:32 * hh + 32, :], values[k % UNROLL][:, c, quad * QUAD + hh, :],
                                            probs[quad][:, hh, c, :], start=(c == 0), stop=(c == C - 1))
                if c == C - 1:
                    last.then_inc(o_done, 1)

            def turn_out(i, k, quad):
                wait(pe, o_copied, before(i, k) * 2 + quad + 1)
                pe.sem_inc(passed, 1)
                for c in range(C):
                    last = nc.tensor.transpose(ps_m[:, c * P:(c + 1) * P], o_rows[quad][:, c * P:(c + 1) * P], w["ident"][:])
                last.then_inc(o_turned, 1)

            def slot(i, k):
                for step in range(STEPS):
                    if live(i, k):
                        row_item(i, k, step * 2)
                        row_item(i, k, step * 2 + 1)
                    if live(i, k - 2):
                        col_item(i, k - 2, step)
                    if step % 2 == 0:
                        quad, c = 1 - step // (STEPS // 2), step // 2 % C
                        of = k - 2 - quad
                        if live(i, of):
                            weigh(i, of, quad, c)
                    if step == 1 and live(i, k + 1):
                        wait(pe, cur_in, through(i, k + 1) * 16)
                        wait(pe, added, before(i, k - 3))
                        pe.sem_inc(passed, 1)
                        for c in range(C):
                            last = nc.tensor.transpose(ps_m[0:D, c * P:(c + 1) * P], cur[:, c, :], w["ident"][:])
                        last.then_inc(turned, 1)
                    if step == 3 and live(i, k + 1):
                        wait(pe, x_copied, through(i, k + 1))
                        pe.sem_inc(passed, 1)
                        nc.tensor.matmul(ps_m[:], wqk[:], xT[:], start=True, stop=True).then_inc(qk_done, 1)
                    if step == 5 and live(i, k - 1):
                        wait(pe, row_maxed, through(i, k - 1) * ROWS)
                        wait(pe, added, before(i, k - 3))
                        wait(pe, qk_rest, through(i, k + 1))
                        pe.sem_inc(passed, 1)
                        nc.tensor.transpose(ps_m[0:ROWS, 0:P], peaks[(k - 1) % UNROLL][:], w["ident"][:]).then_inc(pk_done, 1)
                    if step == 7 and live(i, k - 3):
                        wait(pe, pk_rest, through(i, k - 1))
                        wait(pe, added, before(i, k - 3))
                        turn_out(i, k - 3, 0)
                    if step == 9 and live(i, k + 1):
                        wait(pe, qk_rest, through(i, k + 1))
                        wait(pe, pk_rest, through(i, k - 1))
                        wait(pe, normed, through(i, k - 3) * 2 - 1 if live(i, k - 3) else 0)
                        pe.sem_inc(passed, 1)
                        for c in range(C):
                            last = nc.tensor.matmul(ps_m[:, c * D:(c + 1) * D], xT[:, c * P:(c + 1) * P], wv[:],
                                                    start=True, stop=True)
                        last.then_inc(v_done, 1)
                    if step == 11 and live(i, k - 3):
                        wait(pe, v_copied, through(i, k + 1))
                        wait(pe, normed, through(i, k - 3) * 2 - 1)
                        turn_out(i, k - 3, 1)
                    if step == 13 and live(i, k - 3):
                        wait(pe, normed, through(i, k - 3) * 2)
                        pe.sem_inc(passed, 1)
                        for c in range(C):
                            last = nc.tensor.transpose(ps_m[0:D, c * P:(c + 1) * P],
                                                       o_norm[:, c, :, :].rearrange("p q x -> p (q x)"), w["ident"][:])
                        last.then_inc(n_turned, 1)
                    if step == 15 and live(i, k - 3):
                        wait(pe, n_copied, through(i, k - 3))
                        pe.sem_inc(passed, 1)
                        for c in range(C):
                            last = nc.tensor.matmul(ps_m[:, c * D:(c + 1) * D], oT[:, c * P:(c + 1) * P], wo[:],
                                                    start=True, stop=True)
                        last.then_inc(out_done, 1)

            wait(pe, ready, 1)
            pipe.run(pe, slot)

        @block.scalar
        def _(act):
            def copy_out(i, k, quad):
                wait(act, o_done, before(i, k) * 2 + quad + 1)
                wait(act, o_turned, before(i, k) * 2 + quad - 1)
                nc.scalar.activation(o_rows[quad][:], ps_o[:], ACT.Copy).then_inc(o_copied, 1)

            def slot(i, k):
                for step in range(STEPS):
                    if step == 4 and live(i, k + 1):
                        wait(act, qk_done, through(i, k + 1))
                        wait(act, qk_stored, before(i, k + 1) * (16 * STACK_DMAS))
                        nc.scalar.activation(parts[:, 0, :], ps_m[:], ACT.Copy).then_inc(qk_high, 1)
                    if step == 6 and live(i, k - 1):
                        wait(act, pk_done, through(i, k - 1))
                        wait(act, peak_stored, before(i, k - 1) * 16)
                        nc.scalar.activation(peak_parts[:, 0, :], ps_m[0:ROWS, 0:P], ACT.Copy, scale=-1.0).then_inc(pk_high, 1)
                    if step == 7 and live(i, k - 3):
                        copy_out(i, k - 3, 1)
                    if step == 15 and live(i, k - 2):
                        copy_out(i, k - 2, 0)
                    if live(i, k - 2):
                        n, h, c = step, step // 2 % QUAD, step % 2 * 2
                        quad = n // (COLS // 2)
                        wait(act, col_scored, before(i, k - 2) * COLS + n + 1)
                        if n % (COLS // 2) == 0:
                            wait(act, o_done, before(i, k - 2) * 2 + quad - 1)
                        nc.scalar.activation(probs[quad][:, h, c:c + 2, :], ps_col[n % 2][:], ACT.Exp).then_inc(powered, 1)
                    if step == 5 and live(i, k + 1):
                        wait(act, qk_rest, through(i, k + 1))
                        nc.scalar.activation(parts[:, 1, :], rest[:], ACT.Copy).then_inc(qk_mid, 1)
                    if step == 7 and live(i, k - 1):
                        wait(act, pk_rest, through(i, k - 1))
                        nc.scalar.activation(peak_parts[:, 1, :], peak_rest[:], ACT.Copy).then_inc(pk_mid, 1)

            pipe.run(act, slot)

        @block.vector
        def _(vec):
            def normalise(i, k, quad):
                n = before(i, k) * 2 + quad
                wait(vec, o_turned, n + 1)
                wait(vec, normed, n)
                wait(vec, n_turned, before(i, k))
                o = ps_m[:].rearrange("p (c h x) -> p c h x", c=C, x=32)
                vec.reciprocal(share[:], o[:, :, :, HD]).then_inc(shared, 1)
                wait(vec, shared, n + 1)
                vec.tensor_tensor(o_norm[:, :, quad, :].rearrange("p c (h x) -> p c h x", x=HD), o[:, :, :, 0:HD],
                                  share[:].unsqueeze(3).to_broadcast([P, C, QUAD, HD]), ALU.mult).then_inc(normed, 1)

            def slot(i, k):
                for step in range(STEPS):
                    if live(i, k):
                        for n in (step * 2, step * 2 + 1):
                            wait(vec, row_scored, before(i, k) * ROWS + n + 1)
                            if n == 0:
                                wait(vec, pk_done, before(i, k - 3))
                            vec.tensor_reduce(peaks[k % UNROLL][:, n:n + 1], ps_row[n % 2][:], AX.X,
                                              ALU.max).then_inc(row_maxed, 1)
                    if step == 0 and live(i, k - 4):
                        wait(vec, out_done, through(i, k - 4))
                        g0 = before(i, k - 4) * C
                        vec.tensor_tensor(rows3(H, g0, C), rows3(H, g0, C),
                                          ps_m[:, 0:C * D].rearrange("p (c d) -> p c d", d=D), ALU.add).then_inc(added, 1)
                    if step == 2 and live(i, k + 1):
                        wait(vec, turned, through(i, k + 1))
                        wait(vec, v_done, before(i, k + 1))
                        nc.vector.tensor_copy(xT[0:D, :], ps_m[0:D, :]).then_inc(x_copied, 1)
                    if step == 4 and live(i, k + 1):
                        wait(vec, qk_high, through(i, k + 1))
                        wait(vec, qk_low, before(i, k + 1))
                        vec.tensor_tensor(rest[:], ps_m[:], parts[:, 0, :], ALU.subtract).then_inc(qk_rest, 1)
                    if step == 6 and live(i, k + 1):
                        wait(vec, qk_mid, through(i, k + 1))
                        vec.tensor_tensor(parts[:, 2, :], rest[:], parts[:, 1, :], ALU.subtract).then_inc(qk_low, 1)
                    if step == 6 and live(i, k - 1):
                        wait(vec, pk_high, through(i, k - 1))
                        wait(vec, pk_low, before(i, k - 1))
                        vec.scalar_tensor_tensor(peak_rest[:], ps_m[0:ROWS, 0:P], -1.0, peak_parts[:, 0, :], ALU.mult,
                                                 ALU.subtract).then_inc(pk_rest, 1)
                    if step == 8 and live(i, k - 1):
                        wait(vec, pk_mid, through(i, k - 1))
                        vec.tensor_tensor(peak_parts[:, 2, :], peak_rest[:], peak_parts[:, 1, :],
                                          ALU.subtract).then_inc(pk_low, 1)
                    if step == 8 and live(i, k - 3):
                        normalise(i, k - 3, 0)
                    if step == 10 and live(i, k + 1):
                        wait(vec, v_done, through(i, k + 1))
                        wait(vec, o_done, before(i, k - 2) * 2)
                        nc.vector.tensor_copy(values[(k + 1) % UNROLL][:, :, :, 0:HD],
                                              ps_m[:, 0:C * D].rearrange("p (c h x) -> p c h x", c=C, x=HD)
                                              ).then_inc(v_copied, 1)
                    if step == 12 and live(i, k - 3):
                        normalise(i, k - 3, 1)
                    if step == 14 and live(i, k - 3):
                        wait(vec, n_turned, through(i, k - 3))
                        wait(vec, out_done, before(i, k - 3))
                        nc.vector.tensor_copy(oT[0:D, :], ps_m[0:D, :]).then_inc(n_copied, 1)

            vec.tensor_scalar(wqk[:, 0:D], wqk[:, 0:D], HD ** -0.5, None, ALU.mult).then_inc(ready, 1)
            pipe.run(vec, slot)


def gelu_experts(nc, w, H, out):
    pairs = E1 // 2
    with ExitStack() as outer:
        xT = outer.enter_context(nc.sbuf_tensor("moe_xT", [P, SEQS * L], F32))
        gates = outer.enter_context(nc.sbuf_tensor("moe_gates", [P, G, GATE_ROWS], BF16))
        with ExitStack() as ctx:
            T = ctx.enter_context(nc.sbuf_tensor("moe_T", [P, G, D], F32))
            logits = ctx.enter_context(nc.sbuf_tensor("moe_logits", [P, G, E1], F32))
            route = ctx.enter_context(nc.sbuf_tensor("moe_route", [D + 1, E1], F32))
            clear(nc, "moe_route", route[D:D + 1, :])
            load(nc, "moe_route_w", [(route[0:D, :], w["router_columns"])])
            layer_norm(nc, "ln_m", H, T, 1e-5)
            router(nc, w, "moe", T, xT, {"logits": logits, "weights": route}, E1)
            add_rows(nc, "moe_tokens", H, T)
            comb = ctx.enter_context(nc.sbuf_tensor("moe_comb", [P, G, E1], F32))
            top_two(nc, w, "moe_top", logits, comb, E1, False)
            gate_parts(nc, "moe_parts", comb, gates, E1, False)

        with ExitStack() as ctx:
            s = Stage(nc, ctx, "moe")
            w1 = s.one("w1", [P, pairs // 2, 2 * D])
            twice = s.one("twice", [P, D])
            w2 = s.one("w2", [P, pairs, D])
            b1 = s.one("b1", [P, pairs])
            b2 = s.one("b2", [GATE_ROWS, D])
            pick = s.one("pick", [GATE_ROWS, pairs, P])
            pick_b = s.one("pick_b", [GATE_ROWS, pairs, P], BF16)
            clear(nc, "moe_b2", b2[:])
            load(nc, "moe_w", [
                (twice[:], w["stacked_identity"]),
                *((w1[u * D:(u + 1) * D, n, a * D:(a + 1) * D], w["L1_ffn_w1"][(n * 2 + u) * 2 + a])
                  for u in range(2) for n in range(2) for a in range(2)),
                (w2[:], w["L1_ffn_w2"].rearrange("(q a) g o -> (a g) q o", a=2)),
                (b1[:], w["moe_b1_columns"]), *((b2[r * PART_ROW:r * PART_ROW + E1, :], w["L1_ffn_b2"]) for r in range(3)),
                (pick[:], w["pick_parts"])])
            cur = s.two("cur", [P, C, GATE_ROWS])
            gT = s.two("gT", [GATE_ROWS, L])
            gb = s.two("gb", [GATE_ROWS, L], BF16)
            gb_ready, ready = s.counter("gb_ready"), s.counter("ready")
            h = [s.two(f"h{q}", [P, L]) for q in range(pairs)]
            hg = [s.two(f"hg{q}", [P, L]) for q in range(pairs)]
            ps_t = s.bank("ps_t", [GATE_ROWS, L])
            ps_1, ps_g = s.banks("ps_1", [P, L]), s.banks("ps_g", [P, L])
            ps_e = s.bank("ps_e", [P, L])
            ps_o = s.bank("ps_o", [P, C, D])
            halves = s.one("halves", [P, L])
            x = s.two("x", [P, L])
            x_ready = s.counter("x_ready")
            halved, halves_ready = s.counter("halved"), s.counter("halves_ready")
            passed = s.counter("passed")
            cur_ready, turned, gT_ready = s.counter("cur_ready"), s.counter("turned"), s.counter("gT_ready")
            first, gelus = s.counter("first"), s.counter("gelus")
            spread, gated = s.counter("spread"), s.counter("gated")
            out_done, added, written = s.counter("out_done"), s.counter("added"), s.counter("written")
            block = s.block()
            pipe = Slots(2, -1, 2, SEQS - 1, SEQS + 1)
            live, before, through = pipe.live, pipe.before, pipe.through

            @block.gpsimd
            def _(pool):
                def slot(i, k):
                    if live(i, k + 1):
                        wait(pool, first, before(i, k) * pairs)
                        nc.gpsimd.tensor_copy(x[(k + 1) % 2][:], xT[:, ds(before(i, k + 1) * L, L)]).then_inc(x_ready, 1)
                        wait(pool, turned, before(i, k))
                        nc.gpsimd.tensor_copy(cur[(k + 1) % 2][:], gates[:, ds(before(i, k + 1) * C, C), :]).then_inc(cur_ready, 1)

                pipe.run(pool, slot)

            @block.tensor
            def _(pe):
                def first_layers(i, k, q):
                    wait(pe, gelus, before(i, k) * pairs + q)
                    if q == 0:
                        wait(pe, x_ready, through(i, k))
                    pe.sem_inc(passed, 1)
                    for u in range(2):
                        up = slice(u * D, (u + 1) * D)
                        nc.tensor.matmul(ps_1[u][:], w1[up, q // 2, :], x[k % 2][up, :],
                                         start=True, stop=True).then_inc(first, 1)

                def spread_gates(i, k, q):
                    wait(pe, gated, before(i, k) * pairs + q - 1)
                    if q == 0:
                        wait(pe, gb_ready, through(i, k))
                    pe.sem_inc(passed, 1)
                    nc.tensor.matmul(ps_g[q % 2][:], pick_b[:, q, :], gb[k % 2][:], start=True, stop=True).then_inc(spread, 1)

                def turn_gates(i, k, tiles):
                    if 0 in tiles:
                        wait(pe, cur_ready, through(i, k))
                        wait(pe, gT_ready, before(i, k))
                        pe.sem_inc(passed, 1)
                    for c in tiles:
                        last = nc.tensor.transpose(ps_t[:, c * P:(c + 1) * P], cur[k % 2][:, c, :], w["ident"][:])
                    if C - 1 in tiles:
                        last.then_inc(turned, 1)

                def output_halves(i, k):
                    wait(pe, gated, through(i, k) * pairs)
                    wait(pe, halves_ready, before(i, k))
                    for q in range(pairs):
                        nc.tensor.matmul(ps_e[q % 2 * D:(q % 2 + 1) * D, :], w2[:, q, :], hg[q][k % 2][:],
                                         start=(q < 2), stop=(q == pairs - 1))
                    nc.tensor.matmul(ps_e[0:D, :], b2[:], gT[k % 2][:], start=False, stop=True).then_inc(halved, 1)

                def output(i, k, c):
                    if c == 0:
                        wait(pe, halves_ready, through(i, k))
                        wait(pe, added, before(i, k))
                        pe.sem_inc(passed, 1)
                    last = nc.tensor.matmul(ps_o[:, c, :], halves[:, c * P:(c + 1) * P], twice[:], start=True, stop=True)
                    if c == C - 1:
                        last.then_inc(out_done, 1)

                def slot(i, k):
                    if live(i, k):
                        first_layers(i, k, 0)
                        spread_gates(i, k, 0)
                    if live(i, k + 1):
                        turn_gates(i, k + 1, (0, 1))
                    if live(i, k):
                        spread_gates(i, k, 1)
                    if live(i, k - 1):
                        output_halves(i, k - 1)
                    if live(i, k + 1):
                        turn_gates(i, k + 1, (2, 3))
                    if live(i, k):
                        first_layers(i, k, 2)
                    if live(i, k - 1):
                        output(i, k - 1, 0)
                    if live(i, k):
                        spread_gates(i, k, 2)
                    if live(i, k - 1):
                        output(i, k - 1, 1)
                        output(i, k - 1, 2)
                    if live(i, k):
                        spread_gates(i, k, 3)
                    if live(i, k - 1):
                        output(i, k - 1, 3)

                pe.wait_ge(ready, past(1))
                pipe.run(pe, slot)

            @block.scalar
            def _(act):
                def slot(i, k):
                    for q in range(pairs):
                        if live(i, k):
                            wait(act, first, before(i, k) * pairs + q + 1)
                            if q == 0:
                                wait(act, gated, before(i, k - 1) * pairs)
                            nc.scalar.activation(h[q][k % 2][:], ps_1[q % 2][:], ACT.Gelu,
                                                 bias=b1[:, q:q + 1]).then_inc(gelus, 1)
                        if q == 1 and live(i, k - 1):
                            wait(act, halved, through(i, k - 1))
                            wait(act, out_done, before(i, k - 1))
                            nc.scalar.activation(halves[:], ps_e[:], ACT.Copy).then_inc(halves_ready, 1)
                    if live(i, k + 1):
                        wait(act, gT_ready, through(i, k + 1))
                        wait(act, spread, before(i, k) * pairs)
                        nc.scalar.activation(gb[(k + 1) % 2][:], gT[(k + 1) % 2][:], ACT.Copy).then_inc(gb_ready, 1)

                pipe.run(act, slot)

            @block.vector
            def _(vec):
                def slot(i, k):
                    if live(i, k):
                        for q in range(pairs):
                            wait(vec, spread, before(i, k) * pairs + q + 1)
                            wait(vec, gelus, before(i, k) * pairs + q + 1)
                            if q == 0:
                                wait(vec, halved, before(i, k - 1))
                            vec.tensor_tensor(hg[q][k % 2][:], h[q][k % 2][:], ps_g[q % 2][:],
                                              ALU.mult).then_inc(gated, 1)
                    if live(i, k + 1):
                        wait(vec, turned, through(i, k + 1))
                        wait(vec, halved, before(i, k))
                        nc.vector.tensor_copy(gT[(k + 1) % 2][:], ps_t[:]).then_inc(gT_ready, 1)
                    if live(i, k - 1):
                        wait(vec, out_done, through(i, k - 1))
                        g0 = before(i, k - 1) * C
                        vec.tensor_tensor(rows3(H, g0, C), rows3(H, g0, C), ps_o[:], ALU.add).then_inc(added, 1)

                nc.vector.tensor_copy(pick_b[:], pick[:]).then_inc(ready, 1)
                pipe.run(vec, slot)

            @block.sync
            def _(sp):
                def slot(i, k):
                    if live(i, k - 1):
                        wait(sp, added, through(i, k - 1))
                        sp.sem_inc(passed, 1)
                        b = before(i, k - 1)
                        sp.dma_start(out[ds(b, 1)].rearrange("b (c p) d -> p (b c) d", p=P),
                                     rows3(H, b * C, C)).then_inc(written, 16)

                pipe.run(sp, slot)
                sp.wait_ge(written, past(16 * SEQS))




def program(nc, w, out):
    with ExitStack() as ctx:
        w["gathered"] = [ctx.enter_context(nc.semaphore(f"gathered{n}")) for n in range(3)]
        w["last_of"] = ctx.enter_context(nc.sbuf_tensor("last_of", [P, SEQS * C], F32))
        ident = ctx.enter_context(nc.sbuf_tensor("ident", [P, P], F32))
        load(nc, "consts", [(ident[:], w["identity"])])
        w["ident"] = ident
        H = ctx.enter_context(nc.sbuf_tensor("H", [P, G, D], F32))
        embed(nc, w, H)
        scr = {n: nc.dram_tensor(f"scratch_{n}", shape, dt).ap() for n, shape, dt in (
            ("H", (P, G, D), F32), ("gate", (DIN, SEQS, L), F32), ("u", (DIN, SEQS, L), F32),
            ("delta", (DIN, SEQS, L), F32), ("bc", (2 * DST, 3, SEQS, L), BF16))}
        move(nc, "spill", scr["H"], H[:])
        mamba_inputs(nc, w, H, H, scr)
        selective_scan(nc, w, H, scr)
        w["scr_H"] = scr["H"]
        renew(nc)
        fourier_mixer(nc, w, H)
        renew(nc)
        expert_ffn(nc, w, H)
        renew(nc)
        edge_attention(nc, w, H)
        renew(nc)
        gelu_experts(nc, w, H, out)


def layouts(inputs):
    import numpy as np
    a = {}
    for name, x in inputs.items():
        a[name] = np.ascontiguousarray(np.asarray(x))
    ids = a.pop("x")
    a["ids"] = np.ascontiguousarray(ids.reshape(G, P).T)
    a["table"] = np.concatenate([a.pop("L0_tok_emb_table"), a.pop("L0_tok_geo_table"), a.pop("L0_tok_visit_table")], axis=1)
    a["conv_taps"] = np.ascontiguousarray(a.pop("L0_attn_conv_w").T)
    a["scan_select"] = np.tile(np.repeat(np.eye(NR, dtype=np.float32)[:, :, None], P, axis=2), (3, 1, 1))
    a["eb1_columns"] = np.ascontiguousarray(a.pop("L0_ffn_eb1").T)
    a["eb2_columns"] = np.ascontiguousarray(a.pop("L0_ffn_eb2").reshape(E0 // 2, P).T)
    a["router_columns"] = np.ascontiguousarray(a.pop("L1_ffn_router_w").T)
    a["moe_b1_columns"] = np.ascontiguousarray(a.pop("L1_ffn_b1").reshape(E1 // 2, P).T)
    for n in ("q", "k"):
        a[f"w{n}_columns"] = np.ascontiguousarray(a.pop(f"L1_attn_W{n}").reshape(D, HEADS, HD).transpose(0, 2, 1)).reshape(D, D)
        a[f"b{n}_columns"] = np.ascontiguousarray(a.pop(f"L1_attn_b{n}").reshape(HEADS, HD).T).reshape(D)
    a["token_columns"] = np.ascontiguousarray(np.arange(L, dtype=np.float32).reshape(C, P).T)
    a["edge_numbers"] = np.arange(1, EDGE_STEP + 1, dtype=np.float32).reshape(1, EDGE_STEP)
    a["edge_bases"] = (EDGE_STEP * np.arange(SEQS, dtype=np.float32)).reshape(1, SEQS)
    a["preference"] = np.arange(E1, 0, -1, dtype=np.float32)
    pick = np.repeat(np.eye(E1, dtype=np.float32).reshape(E1, E1 // 2, 2), D, axis=2)
    a["pick_parts"] = np.zeros((GATE_ROWS, E1 // 2, P), np.float32)
    for r in range(3):
        a["pick_parts"][r * PART_ROW:r * PART_ROW + E1] = pick
    t = np.arange(L)
    k = np.arange(L // 2 + 1)
    angle = 2 * np.pi / L * (t[:, None] * k[None, :] % L)
    cos, sin = np.cos(angle), np.sin(angle)
    root = L ** 0.5
    forward = np.concatenate([cos, -sin[:, 1:L // 2]], axis=1) / root
    weight = np.where((k == 0) | (k == L // 2), 1.0, 2.0)[:, None] * root / L
    inverse = np.concatenate([(weight * cos.T)[0:L // 2], (weight * cos.T)[L // 2:], -(weight * sin.T)[1:L // 2]])
    a["dft"] = np.ascontiguousarray(forward.reshape(C, P, L).transpose(1, 0, 2).astype(np.float32))
    a["idft"] = np.ascontiguousarray(inverse.reshape(C, P, L).transpose(1, 0, 2).astype(np.float32))
    a["stacked_identity"] = np.tile(np.eye(D, dtype=np.float32), (2, 1))
    a["identity"] = np.eye(P, dtype=np.float32)
    return a


def kernel(**inputs):
    import concourse.bacc as _bacc
    from concourse.bass_utils import run_bass_kernel_spmd as _run

    nc = _bacc.Bacc("TRN2", target_bir_lowering=False, num_devices=1)
    arrays = layouts(inputs)
    w = {n: nc.dram_tensor(f"in_{n}", a.shape, mybir.dt.from_np(a.dtype), kind="ExternalInput").ap()
         for n, a in arrays.items()}
    out = nc.dram_tensor("out", (SEQS, L, D), F32, kind="ExternalOutput").ap()
    program(nc, w, out)
    r = _run(nc, [{f"in_{n}": a for n, a in arrays.items()}], core_ids=[0])
    return r.results[0]["out"]
```
